# Optimizing a Trainium2 kernel written in Bass

```python
import numpy as np
import jax
import jax.numpy as jnp

def _softmax(x, axis=-1):
    return jax.nn.softmax(x, axis=axis)

def _gelu(x):
    return jax.nn.gelu(x, approximate=True)

def _silu(x):
    return jax.nn.silu(x)

def _sigmoid(x):
    return jax.nn.sigmoid(x)

def _layernorm(x, axis=-1, eps=1e-05):
    m = jnp.mean(x, axis=axis, keepdims=True)
    v = jnp.var(x, axis=axis, keepdims=True)
    return (x - m) / jnp.sqrt(v + eps)

def _scatter_add(tgt, idx, src, axis=0):
    return tgt.at[idx].add(src)

def _segment_sum(src, seg, n):
    return jax.ops.segment_sum(src, seg, n)
kernel_name = 'mk_early_fusion_d2_tok_img256_r4_f450c7'

def setup_inputs(seed: int=0):
    np.random.seed(seed)
    _w = jnp.asarray

    def _rec_inputs():
        import jax
        import jax.numpy as jnp
        _rk = jax.random.key(seed)
        x = -7.10856e-05 + 0.999911 * jax.random.normal(jax.random.fold_in(_rk, 1), (8, 64, 128, 64), jnp.float32)
        txt = -0.000161634 + 0.479995 * jax.random.normal(jax.random.fold_in(_rk, 2), (8, 32, 64), jnp.float32)
        return (x, txt)
    x, txt = _rec_inputs()

    def _L0_tok_setup():
        import jax, jax.numpy as jnp
        import numpy as np
        PATCH_LEN = 16
        STRIDE = 8
        PAD = 8
        key = jax.random.key(seed)
        k1, k2 = jax.random.split(key)
        x = jax.random.normal(k1, (32, 64, 128, 64), dtype=jnp.float32)
        in_feat = 64 * (PATCH_LEN // 2 + 1) * 2
        W = jax.random.normal(k2, (64, in_feat), dtype=jnp.float32) * 0.02
        return {'x': x, 'W': W}
    _L0_tok_all = _L0_tok_setup()
    _L0_tok_in = {k: v for k, v in _L0_tok_all.items() if k in ('W',)}
    del _L0_tok_all

    def _L0_attn_setup():
        import jax, jax.numpy as jnp
        import numpy as np
        HEADS = 8
        key = jax.random.key(seed)
        k1, k2, k3 = jax.random.split(key, 3)
        b, n, d = (4, 512, 64)
        x = jax.random.normal(k1, (b, n, d), dtype=jnp.float32)
        w_qkv = jax.random.normal(k2, (d, 3 * d), dtype=jnp.float32) * d ** (-0.5)
        b_qkv = jnp.zeros((3 * d,), dtype=jnp.float32)
        w_out = jax.random.normal(k3, (d, d), dtype=jnp.float32) * d ** (-0.5)
        b_out = jnp.zeros((d,), dtype=jnp.float32)
        return {'x': x, 'w_qkv': w_qkv, 'b_qkv': b_qkv, 'w_out': w_out, 'b_out': b_out}
    _L0_attn_all = _L0_attn_setup()
    _L0_attn_in = {k: v for k, v in _L0_attn_all.items() if k in ('w_qkv', 'b_qkv', 'w_out', 'b_out')}
    del _L0_attn_all

    def _L0_ffn_setup():
        import jax, jax.numpy as jnp
        import numpy as np
        B, S, H, F, E, K = (8, 1024, 64, 128, 16, 2)
        EPS = 1e-05
        key = jax.random.key(seed)
        ks = jax.random.split(key, 9)
        sc = 0.02
        return {'x': jax.random.normal(ks[0], (B, S, H), dtype=jnp.float32), 'gate_w': jax.random.normal(ks[1], (H, E), dtype=jnp.float32) * sc, 'gate_b': jnp.zeros((E,), dtype=jnp.float32), 'w1': jax.random.normal(ks[2], (E, H, F), dtype=jnp.float32) * sc, 'b1': jnp.zeros((E, F), dtype=jnp.float32), 'w2': jax.random.normal(ks[3], (E, F, H), dtype=jnp.float32) * sc, 'b2': jnp.zeros((E, H), dtype=jnp.float32), 'gamma': jnp.ones((H,), dtype=jnp.float32), 'beta': jnp.zeros((H,), dtype=jnp.float32)}
    _L0_ffn_all = _L0_ffn_setup()
    _L0_ffn_in = {k: v for k, v in _L0_ffn_all.items() if k in ('gate_w', 'gate_b', 'w1', 'b1', 'w2', 'b2', 'gamma', 'beta')}
    del _L0_ffn_all

    def _L1_attn_setup():
        import jax, jax.numpy as jnp
        import numpy as np
        U_DECAY = 0.97
        X_DECAY = 0.97
        LN_EPS = 1e-05
        L1_EPS = 1e-12

        def _ln(x):
            m = jnp.mean(x, axis=-1, keepdims=True)
            v = jnp.mean((x - m) ** 2, axis=-1, keepdims=True)
            return (x - m) * jax.lax.rsqrt(v + LN_EPS)
        key = jax.random.key(seed)
        k0, k1, k2, k3 = jax.random.split(key, 4)
        B, T, d, n = (8, 64, 64, 256)
        embeddings = jax.random.normal(k0, (B, T, d), dtype=jnp.float32)
        E = jax.random.normal(k1, (d, n), dtype=jnp.float32) / n ** 0.5
        Dx = jax.random.normal(k2, (n, d), dtype=jnp.float32) / d ** 0.5
        Dy = jax.random.normal(k3, (n, d), dtype=jnp.float32) / d ** 0.5
        return {'embeddings': embeddings, 'E': E, 'Dx': Dx, 'Dy': Dy}
    _L1_attn_all = _L1_attn_setup()
    _L1_attn_in = {k: v for k, v in _L1_attn_all.items() if k in ('E', 'Dx', 'Dy')}
    del _L1_attn_all

    def _L1_ffn_setup():
        import jax, jax.numpy as jnp
        import numpy as np
        B, S, D, H, E, K = (8, 2048, 64, 256, 8, 2)
        key = jax.random.key(seed)
        ks = jax.random.split(key, 7)
        s_in = 1.0 / np.sqrt(D)
        s_hid = 1.0 / np.sqrt(H)
        return {'x': jax.random.normal(ks[0], (B, S, D), dtype=jnp.float32), 'Wg': jax.random.uniform(ks[1], (E, D), jnp.float32, -s_in, s_in), 'bg': jax.random.uniform(ks[2], (E,), jnp.float32, -s_in, s_in), 'W1': jax.random.uniform(ks[3], (E, H, D), jnp.float32, -s_in, s_in), 'b1': jax.random.uniform(ks[4], (E, H), jnp.float32, -s_in, s_in), 'W2': jax.random.uniform(ks[5], (E, D, H), jnp.float32, -s_hid, s_hid), 'b2': jax.random.uniform(ks[6], (E, D), jnp.float32, -s_hid, s_hid)}
    _L1_ffn_all = _L1_ffn_setup()
    _L1_ffn_in = {k: v for k, v in _L1_ffn_all.items() if k in ('Wg', 'bg', 'W1', 'b1', 'W2', 'b2')}
    del _L1_ffn_all
    return {'x': x, 'txt': txt, 'L0_tok_W': _L0_tok_in['W'], 'L0_attn_w_qkv': _L0_attn_in['w_qkv'], 'L0_attn_b_qkv': _L0_attn_in['b_qkv'], 'L0_attn_w_out': _L0_attn_in['w_out'], 'L0_attn_b_out': _L0_attn_in['b_out'], 'L0_ffn_gate_w': _L0_ffn_in['gate_w'], 'L0_ffn_gate_b': _L0_ffn_in['gate_b'], 'L0_ffn_w1': _L0_ffn_in['w1'], 'L0_ffn_b1': _L0_ffn_in['b1'], 'L0_ffn_w2': _L0_ffn_in['w2'], 'L0_ffn_b2': _L0_ffn_in['b2'], 'L0_ffn_gamma': _L0_ffn_in['gamma'], 'L0_ffn_beta': _L0_ffn_in['beta'], 'L1_attn_E': _L1_attn_in['E'], 'L1_attn_Dx': _L1_attn_in['Dx'], 'L1_attn_Dy': _L1_attn_in['Dy'], 'L1_ffn_Wg': _L1_ffn_in['Wg'], 'L1_ffn_bg': _L1_ffn_in['bg'], 'L1_ffn_W1': _L1_ffn_in['W1'], 'L1_ffn_b1': _L1_ffn_in['b1'], 'L1_ffn_W2': _L1_ffn_in['W2'], 'L1_ffn_b2': _L1_ffn_in['b2']}

def reference(x, txt, L0_tok_W, L0_attn_w_qkv, L0_attn_b_qkv, L0_attn_w_out, L0_attn_b_out, L0_ffn_gate_w, L0_ffn_gate_b, L0_ffn_w1, L0_ffn_b1, L0_ffn_w2, L0_ffn_b2, L0_ffn_gamma, L0_ffn_beta, L1_attn_E, L1_attn_Dx, L1_attn_Dy, L1_ffn_Wg, L1_ffn_bg, L1_ffn_W1, L1_ffn_b1, L1_ffn_W2, L1_ffn_b2):
    import jax
    import jax.numpy as jnp

    def _L0_tok_ref(x, W):
        import jax, jax.numpy as jnp
        import numpy as np
        PATCH_LEN = 16
        STRIDE = 8
        PAD = 8
        B, C, T, V = x.shape
        xp = jnp.pad(x, ((0, 0), (0, 0), (0, PAD), (0, 0)), mode='edge')
        Tp = T + PAD
        N = (Tp - PATCH_LEN) // STRIDE + 1
        idx = jnp.arange(N)[:, None] * STRIDE + jnp.arange(PATCH_LEN)[None, :]
        patches = xp[:, :, idx, :]
        patches = jnp.transpose(patches, (0, 4, 2, 3, 1))
        xf = jnp.fft.rfft(patches, axis=-2, norm='ortho')
        F = xf.shape[-2]
        x_real = xf.real.reshape(B, V, N, F * C)
        x_imag = xf.imag.reshape(B, V, N, F * C)
        x_emb = jnp.concatenate([x_real, x_imag], axis=-1)
        x_emb = x_emb @ W.T
        return x_emb.reshape(B, V * N, -1)

    def _L0_attn_ref(x, w_qkv, b_qkv, w_out, b_out):
        import jax, jax.numpy as jnp
        import numpy as np
        HEADS = 8
        b, n, d = x.shape
        h = HEADS
        dh = d // h
        scale = d ** (-0.5)
        qkv = x @ w_qkv + b_qkv
        q, k, v = jnp.split(qkv, 3, axis=-1)
        to_heads = lambda t: t.reshape(b, n, h, dh).transpose(0, 2, 1, 3)
        q, k, v = (to_heads(q), to_heads(k), to_heads(v))
        dots = jnp.einsum('bhid,bhjd->bhij', q, k) * scale
        attn = jax.nn.softmax(dots, axis=-1)
        out = jnp.einsum('bhij,bhjd->bhid', attn, v)
        out = out.transpose(0, 2, 1, 3).reshape(b, n, d)
        return out @ w_out + b_out

    def _L0_ffn_ref(x, gate_w, gate_b, w1, b1, w2, b2, gamma, beta):
        import jax, jax.numpy as jnp
        import numpy as np
        B, S, H, F, E, K = (8, 1024, 64, 128, 16, 2)
        EPS = 1e-05
        gate_logits = x @ gate_w + gate_b
        topk_vals, topk_idx = jax.lax.top_k(gate_logits, K)
        topk_w = jax.nn.softmax(topk_vals, axis=-1)
        h = jax.nn.relu(jnp.einsum('bsh,ehf->bsef', x, w1) + b1)
        expert_out = jnp.einsum('bsef,efh->bseh', h, w2) + b2
        sel = jnp.take_along_axis(expert_out, topk_idx[:, :, :, None], axis=2)
        moe = jnp.sum(topk_w[..., None] * sel, axis=2)
        y = x + moe
        mu = jnp.mean(y, axis=-1, keepdims=True)
        var = jnp.var(y, axis=-1, keepdims=True)
        return (y - mu) / jnp.sqrt(var + EPS) * gamma + beta

    def _L1_attn_ref(embeddings, E, Dx, Dy):
        import jax, jax.numpy as jnp
        import numpy as np
        U_DECAY = 0.97
        X_DECAY = 0.97
        LN_EPS = 1e-05
        L1_EPS = 1e-12

        def _ln(x):
            m = jnp.mean(x, axis=-1, keepdims=True)
            v = jnp.mean((x - m) ** 2, axis=-1, keepdims=True)
            return (x - m) * jax.lax.rsqrt(v + LN_EPS)
        B, T, d = embeddings.shape
        n = E.shape[1]

        def step(carry, v_prev):
            x_state, rho = carry
            x_update = jax.nn.relu(v_prev @ Dx.T)
            x_t = X_DECAY * x_state + x_update
            x_t = x_t / jnp.maximum(jnp.sum(jnp.abs(x_t), axis=-1, keepdims=True), L1_EPS)
            a_star = jnp.einsum('bdn,bn->bd', rho, x_t)
            y_core = _ln(a_star) @ Dy.T
            y_t = jax.nn.relu(y_core) * jax.nn.relu(x_t)
            v_star = _ln(y_t @ E.T)
            rho_t = U_DECAY * rho + _ln(v_prev)[:, :, None] * x_t[:, None, :]
            return ((x_t, rho_t), v_star)
        x0 = jnp.zeros((B, n), dtype=embeddings.dtype)
        rho0 = jnp.zeros((B, d, n), dtype=embeddings.dtype)
        _, vs = jax.lax.scan(step, (x0, rho0), jnp.swapaxes(embeddings, 0, 1))
        return jnp.swapaxes(vs, 0, 1)

    def _L1_ffn_ref(x, Wg, bg, W1, b1, W2, b2):
        import jax, jax.numpy as jnp
        import numpy as np
        B, S, D, H, E, K = (8, 2048, 64, 256, 8, 2)
        gate_scores = jnp.einsum('bsd,ed->bse', x, Wg) + bg
        topk_scores, topk_idx = jax.lax.top_k(gate_scores, K)
        topk_probs = jax.nn.softmax(topk_scores, axis=-1)
        combine = jnp.sum(topk_probs[..., None] * jax.nn.one_hot(topk_idx, E, dtype=x.dtype), axis=-2)
        out = jnp.zeros_like(x)
        for e in range(E):
            h = jax.nn.relu(jnp.einsum('bsd,hd->bsh', x, W1[e]) + b1[e])
            y = jnp.einsum('bsh,dh->bsd', h, W2[e]) + b2[e]
            out = out + combine[..., e:e + 1] * y
        return out
    h = _L0_tok_ref(x, L0_tok_W)
    h = jnp.concatenate([h, txt], axis=1)
    h = h + _L0_attn_ref(_layernorm(h, axis=-1), L0_attn_w_qkv, L0_attn_b_qkv, L0_attn_w_out, L0_attn_b_out)
    h = h + _L0_ffn_ref(_layernorm(h, axis=-1), L0_ffn_gate_w, L0_ffn_gate_b, L0_ffn_w1, L0_ffn_b1, L0_ffn_w2, L0_ffn_b2, L0_ffn_gamma, L0_ffn_beta)
    h = h + _L1_attn_ref(_layernorm(h, axis=-1), L1_attn_E, L1_attn_Dx, L1_attn_Dy)
    h = h + _L1_ffn_ref(_layernorm(h, axis=-1), L1_ffn_Wg, L1_ffn_bg, L1_ffn_W1, L1_ffn_b1, L1_ffn_W2, L1_ffn_b2)
    return h

_drawn_inputs = setup_inputs


def setup_inputs(seed=0):
    import zlib

    import numpy as np

    out = dict(_drawn_inputs(seed))
    spreads = {'L0_attn_b_qkv': (0.0, 0.1),
     'L0_attn_b_out': (0.0, 0.1),
     'L0_ffn_gate_b': (0.0, 0.1),
     'L0_ffn_b1': (0.0, 0.703),
     'L0_ffn_b2': (0.0, 0.1),
     'L0_ffn_gamma': (1.0, 0.2),
     'L0_ffn_beta': (0.0, 0.1)}
    factors = {'L0_ffn_w1': 4.185, 'L0_ffn_w2': 2.896, 'L1_ffn_b1': 4.857, 'L1_ffn_b2': 3.869}
    for name, (base, spread) in spreads.items():
        noise = np.random.default_rng([zlib.crc32(name.encode()), seed]).standard_normal(out[name].shape)
        drawn = base * np.exp(spread * noise) if base else spread * noise
        out[name] = jnp.asarray(drawn.astype(out[name].dtype))
    for name, factor in factors.items():
        out[name] = (out[name] * factor).astype(out[name].dtype)
    return out
```

```python
from contextlib import ExitStack

import numpy as np

import concourse.bass as bass
from concourse import mybir
from concourse.alu_op_type import AluOpType as ALU

F32 = mybir.dt.float32
BF16 = mybir.dt.bfloat16
U32 = mybir.dt.uint32
ACT = mybir.ActivationFunctionType
AX = mybir.AxisListType

P = 128
B, C, T, V, D = 8, 64, 128, 64, 64
STRIDE, PATCH = 8, 16
WIN = T // STRIDE
TXT = 32
TOK = V * WIN
SEQ = TOK + TXT
NT = -(-SEQ // P)
FULL = SEQ // P
CH = SEQ // 3
NC = SEQ // CH
HEADS, DH = 8, 8
QUAD = 4
HG = HEADS // QUAD
PARTS = 3
KS = PARTS * PARTS * DH
KPAD = 96
KMAX = KPAD + PARTS
LN_EPS = 1e-5
DECAY = 0.97
NN = 256
L1_EPS = 1e-12
EINS = 16
PAIRS = [(0, 0), (0, 1), (1, 0), (0, 2), (2, 0), (1, 1)]
GK = len(PAIRS) * EINS


def shape_constants():
    f = np.arange(PATCH // 2 + 1)[:, None]
    t = np.arange(PATCH)[None, :]
    turn = (f * t) % PATCH
    cos, sin = np.cos(2 * np.pi * turn / PATCH) / 4, -np.sin(2 * np.pi * turn / PATCH) / 4
    sin[(2 * turn) % PATCH == 0] = 0
    dft = np.concatenate([cos, sin])
    dft = dft.reshape(-1, 2, 2, 4).transpose(0, 2, 1, 3)
    p, x = np.arange(P)[:, None], np.arange(SEQ)[None, :]
    lag = x - 1 - p
    decay = np.where(lag >= 0, DECAY ** np.maximum(lag, 0).astype(np.float64), 0.0)
    first = [PAIRS.index((0, 0)), PAIRS.index((1, 0)), PAIRS.index((2, 0))]
    pick = np.zeros((GK, EINS // 2, P))
    for n in range(EINS // 2):
        for k in first:
            pick[k * EINS + 2 * n, n, 0:64] = 1
            pick[k * EINS + 2 * n + 1, n, 64:128] = 1
    part_of = np.repeat(np.eye(PARTS)[[bi for _, bi in PAIRS]], EINS, axis=0)
    own = np.tile(np.eye(EINS), (len(PAIRS), 1))
    return {
        "dft": dft.reshape(18, 16).astype(np.float32),
        "eye": np.eye(P, dtype=np.float32),
        "decay": decay.astype(np.float32),
        "part_of": part_of.astype(np.float32),
        "own": own.astype(np.float32),
        "column": np.eye(B, dtype=np.float32)[None],
        "rows": np.repeat(np.eye(B, dtype=np.float32)[:, :, None], P, axis=2),
        "number": np.arange(EINS, dtype=np.float32)[None, :],
        "pick": pick.astype(np.float32),
    }


class Program:

    def __init__(self, nc, ctx, arg, const, out):
        self.nc, self.ctx, self.arg, self.const, self.out = nc, ctx, arg, const, out
        self.hid = ctx.enter_context(nc.sbuf_tensor("hid", [P, B, NT, D], F32))
        self.eye = ctx.enter_context(nc.sbuf_tensor("eye", [P, P], F32))
        self.eye_bf = ctx.enter_context(nc.sbuf_tensor("eye_bf", [P, P], BF16))
        self.eps = ctx.enter_context(nc.sbuf_tensor("eps", [P, NT], F32))
        self.minus_half = ctx.enter_context(nc.sbuf_tensor("minus_half", [P, NT], F32))

        self.qk_scr = nc.dram_tensor("qk_scr", (B, 2, HEADS, PARTS, DH, SEQ), BF16, kind="Internal").ap()
        self.v_scr = nc.dram_tensor("v_scr", (B, P, NT * HEADS * 32), F32, kind="Internal").ap()
        self.sum_scr = nc.dram_tensor("sum_scr", (B, P, HG * SEQ), F32, kind="Internal").ap()
        self.max_scr = nc.dram_tensor("max_scr", (B, PARTS, HEADS * FULL + HG, P), BF16, kind="Internal").ap()

        self.sems, self.sem_ctx = [], ExitStack()

    def sem(self, name):
        self.sems.append(self.sem_ctx.enter_context(self.nc.semaphore(name)))
        return self.sems[-1]

    def software_dma_sem(self, name):
        return self.ctx.enter_context(self.nc.semaphore(name))

    def free_sems(self):
        with self.nc.Block() as block:
            @block.gpsimd
            def _(pool):
                for sem in self.sems:
                    pool.sem_clear(sem)
        self.sem_ctx.close()
        self.sems = []


def tokens_stage(g):
    nc, arg, hid = g.nc, g.arg, g.hid
    x, W = arg["x"], arg["L0_tok_W"]
    consts_in, w_in, txt_in = g.sem("consts_in"), g.sem("w_in"), g.software_dma_sem("txt_in")
    fold_done, fold_copied = g.sem("fold_done"), g.sem("fold_copied")
    x_in = [g.sem(f"x_in{s}") for s in range(2)]
    x_used = [g.sem(f"x_used{s}") for s in range(2)]
    projected, evacuated = g.sem("projected"), g.sem("evacuated")
    turned, stored, zeroed, eye_ready = g.sem("turned"), g.sem("stored"), g.sem("zeroed"), g.sem("eye_ready")
    NR = 2 * (PATCH // 2 + 1)
    with ExitStack() as c:
        sb = lambda n, s, d=F32: c.enter_context(nc.sbuf_tensor(n, s, d))
        dft = sb("dft", [NR, 16])
        w_raw = sb("w_raw", [NR, D, C])
        w_fold = sb("w_fold", [P, 4, 2, D])
        xt = [sb(f"xt{s}", [P, WIN + 1, 4, V]) for s in range(2)]
        tokT = sb("tokT", [P, 512])
        p_fold = c.enter_context(nc.psum_tensor("p_fold", [P, 512], F32))
        p_tok = c.enter_context(nc.psum_tensor("p_tok", [P, 512], F32))
        p_turn = c.enter_context(nc.psum_tensor("p_turn", [P, 4, 2, D], F32))
        block = c.enter_context(nc.Block())

        @block.sync
        def _(sp):
            sp.dma_start(dft[:], g.const["dft"]).then_inc(consts_in, 16)
            sp.dma_start(w_raw[:], W.rearrange("o (r c) -> r o c", c=C)).then_inc(w_in, 16)
            sp.dma_start(g.eye[:], g.const["eye"]).then_inc(consts_in, 16)
            with sp.Fori(0, B // 2) as i:
                for s in range(2):
                    sp.wait_ge(x_used[s], i)
                    for par in range(2):
                        rows = slice(par * C, par * C + C)
                        src = x[2 * i + s, :, :, :].rearrange("c (n q j) v -> q c n (j v)", q=2, j=4)
                        sp.dma_start(xt[s][rows, 0:WIN, :, :].rearrange("p n j v -> p n (j v)"),
                                     src[par, :, :, :]).then_inc(x_in[s], 16)
                        sp.dma_start(xt[s][rows, WIN, :, :],
                                     x[2 * i + s, :, T - 1:T, :].to_broadcast([C, 4, V])).then_inc(x_in[s], 16)

        @block.gpsimd
        def _(pool):
            pool.wait_ge(zeroed, 1)
            pool.dma_start(hid[0:TXT, :, FULL, :], arg["txt"].rearrange("b t d -> t b d")).then_inc(txt_in, 16)
            pool.wait_ge(txt_in, 16)

        @block.tensor
        def _(pe):
            pe.wait_ge(consts_in, 32)
            pe.wait_ge(w_in, 16)
            for par in range(2):
                for o in range(D):
                    last = nc.tensor.matmul(p_fold[par * C:par * C + C, o * 8:o * 8 + 8], w_raw[:, o, :],
                                            dft[:, par * 8:par * 8 + 8], start=True, stop=True)
            last.then_inc(fold_done, 1)
            pe.wait_ge(fold_copied, 1)
            with pe.Fori(0, B // 2) as i:
                for s in range(2):
                    pe.wait_ge(x_in[s], 64 * i + 64)
                    pe.wait_ge(evacuated, 2 * i + s)
                    for k in range(8):
                        for half in range(2):
                            col = xt[s][:, k // 4:k // 4 + WIN, k % 4, half * 32:half * 32 + 32]
                            last = nc.tensor.matmul(p_tok[half * D:half * D + D, :], w_fold[:, k % 4, k // 4, :],
                                                    col.rearrange("p n v -> p v n"), start=(k == 0), stop=(k == 7),
                                                    skip_group_check=True)
                    last.then_inc(projected, 1)
                    pe.wait_ge(evacuated, 2 * i + s + 1)
                    pe.wait_ge(stored, 2 * i + s)
                    for q in range(4):
                        last = nc.tensor.transpose(p_turn[:, q, :, :].rearrange("p a d -> p (a d)"),
                                                   tokT[:, q * P:q * P + P], g.eye[:])
                    last.then_inc(turned, 1)

        @block.vector
        def _(dve):
            nc.vector.memset(hid[:, :, FULL, :], 0.0).then_inc(zeroed, 1)
            nc.vector.memset(g.minus_half[:], -0.5)
            nc.vector.memset(g.eps[:], LN_EPS)
            dve.wait_ge(consts_in, 32)
            nc.vector.tensor_copy(g.eye_bf[:], g.eye[:]).then_inc(eye_ready, 1)
            dve.wait_ge(fold_done, 1)
            nc.vector.tensor_copy(w_fold[:].rearrange("p j s o -> p o s j"),
                                  p_fold[:, :].rearrange("p (o s j) -> p o s j", s=2, j=4)).then_inc(fold_copied, 1)
            with dve.Fori(0, B) as b:
                dve.wait_ge(turned, b + 1)
                nc.vector.tensor_copy(hid[:, b, 0:FULL, :].rearrange("p (h q) d -> p q h d", h=2),
                                      p_turn[:, :, :, :]).then_inc(stored, 1)

        @block.scalar
        def _(act):
            with act.Fori(0, B // 2) as i:
                for s in range(2):
                    act.wait_ge(projected, 2 * i + s + 1)
                    act.wait_ge(turned, 2 * i + s)
                    nc.scalar.copy(tokT[:, :], p_tok[:, :]).then_inc(evacuated, 1)
                    act.sem_inc(x_used[s], 1)


def wait_alone(engine, sem, value, alone):
    engine.wait_ge(sem, value)
    engine.sem_inc(alone, 1)


def layernorm_dve(nc, dve, n, src, dst, st, mv, sems, rows_done, twice=False):
    stats_done, moments_done, rstd_done, alone = sems
    for t in range(NT):
        nc.vector.bn_stats(st[:, t, :], src(t)).then_inc(stats_done, 1)
    wait_alone(dve, stats_done, NT * (n + 1), alone)
    for t in range(NT):
        nc.vector.bn_aggr(mv[:, t, 0:2], st[:, t, :]).then_inc(moments_done, 1)
    dve.wait_ge(rstd_done, 2 * n + 2)
    for t in range(NT):
        rows = src(t) if not twice else src(t).unsqueeze(1).to_broadcast([P, 2, D])
        nc.vector.tensor_scalar(dst(t), rows, mv[:, t, 0:1], mv[:, t, 2:3], ALU.subtract, ALU.mult)\
            .then_inc(rows_done, 1)


def layernorm_pool(g, pool, n, mv, sems):
    nc = g.nc
    stats_done, moments_done, rstd_done, alone = sems
    pool.wait_ge(moments_done, NT * (n + 1))
    nc.gpsimd.tensor_tensor(mv[:, :, 3], mv[:, :, 1], g.eps[:, :], ALU.add).then_inc(rstd_done, 1)
    pool.wait_ge(rstd_done, 2 * n + 1)
    nc.gpsimd.tensor_tensor(mv[:, :, 2], mv[:, :, 3], g.minus_half[:, :], ALU.pow).then_inc(rstd_done, 1)


def project_stage(g):
    nc, arg, hid = g.nc, g.arg, g.hid
    ln = [g.sem(n) for n in ("a_stats", "a_moments", "a_rstd", "a_alone")]
    w_in, set_up, w_ready = g.sem("a_w_in"), g.sem("a_set_up"), g.sem("a_w_ready")
    normed, turned, xT_ready = g.sem("a_normed"), g.sem("a_turned"), g.sem("a_xT_ready")
    qk_done, v_done, v_copied = g.sem("a_qk_done"), g.sem("a_v_done"), g.sem("a_v_copied")
    part = [g.sem(f"a_part{i}") for i in range(PARTS)]
    rest, pe_alone = g.sem("a_rest"), g.sem("a_pe_alone")
    parts_sent, v_sent = g.sem("a_parts_sent"), g.sem("a_v_sent")
    with ExitStack() as c:
        sb = lambda n, s, d=F32: c.enter_context(nc.sbuf_tensor(n, s, d))
        ps = lambda n, s: c.enter_context(nc.psum_tensor(n, s, F32))
        st, mv = sb("a_st", [P, NT, 6]), sb("a_mv", [P, NT, 4])
        xn = sb("a_xn", [P, NT, D])
        xT = sb("a_xT", [P, NT * P])
        w_qkv = sb("a_w_qkv", [P, 3 * D])
        qk_part = [sb(f"a_qk_part{i}", [P, SEQ], BF16) for i in range(PARTS)]
        qk_rest = sb("a_qk_rest", [P, SEQ])
        vw = sb("a_vw", [P, NT, HEADS, 32])
        p_turn = ps("a_p_turn", [P, 3, 512])
        p_qk = ps("a_p_qk", [P, 3, 512])
        p_v = ps("a_p_v", [P, 2, 512])
        block = c.enter_context(nc.Block())
        xT_flat = p_turn[0:D, :, 0:3 * P]

        @block.sync
        def _(sp):
            sp.wait_ge(set_up, 2)
            sp.dma_start(w_qkv[0:D, :], arg["L0_attn_w_qkv"]).then_inc(w_in, 16)
            sp.dma_start(w_qkv[D:D + 1, :], arg["L0_attn_b_qkv"].rearrange("(a n) -> a n", a=1)).then_inc(w_in, 16)
            with sp.Fori(0, B) as b:
                for i in range(PARTS):
                    sp.wait_ge(part[i], b + 1)
                    sp.dma_start(g.qk_scr[b, :, :, i, :, :].rearrange("a h d t -> (a h) d t"), qk_part[i][:, :]).then_inc(parts_sent, 16)
                sp.wait_ge(v_copied, (QUAD + 1) * (b + 1))
                sp.dma_start(g.v_scr[b, :, :], vw[:].rearrange("p t h d -> p (t h d)")).then_inc(v_sent, 16)
            sp.wait_ge(parts_sent, 16 * PARTS * B)
            sp.wait_ge(v_sent, 16 * B)

        @block.gpsimd
        def _(pool):
            nc.gpsimd.memset(w_qkv[D:P, :], 0.0).then_inc(set_up, 1)
            nc.gpsimd.memset(xT[D:P, :], 0.0).then_inc(set_up, 1)
            pool.wait_ge(set_up, 2)
            nc.gpsimd.memset(xT[D:D + 1, :], 1.0).then_inc(set_up, 1)
            pool.wait_ge(set_up, 3)
            nc.gpsimd.memset(vw[:], 0.0).then_inc(set_up, 1)
            pool.wait_ge(set_up, 4)
            nc.gpsimd.memset(vw[:, 0:FULL, :, DH:DH + 1], 1.0).then_inc(set_up, 1)
            for h in range(HEADS):
                r = 32 * (h % QUAD)
                pool.wait_ge(set_up, 5 + h)
                nc.gpsimd.memset(vw[r:r + 32, FULL, h, DH:DH + 1], 1.0).then_inc(set_up, 1)
            with pool.Fori(0, B) as b:
                layernorm_pool(g, pool, b, mv, ln)

        @block.vector
        def _(dve):
            dve.wait_ge(set_up, 5 + HEADS)
            with dve.Fori(0, B) as b:
                dve.wait_ge(turned, b)
                layernorm_dve(nc, dve, b, lambda t: hid[:, b, t, :], lambda t: xn[:, t, :], st, mv, ln, normed)
                dve.wait_ge(turned, b + 1)
                nc.vector.tensor_copy(xT[0:D, :].rearrange("p (a n) -> p a n", a=3), xT_flat).then_inc(xT_ready, 1)
                dve.wait_ge(part[0], b + 1)
                dve.wait_ge(part[2], b)
                nc.vector.tensor_tensor(qk_rest[:, :].rearrange("p (a n) -> p a n", a=NC), p_qk[:, :, 0:CH],
                                        qk_part[0][:, :].rearrange("p (a n) -> p a n", a=NC), ALU.subtract).then_inc(rest, 1)
                dve.wait_ge(parts_sent, 16 * PARTS * b)
                dve.wait_ge(part[1], b + 1)
                nc.vector.tensor_tensor(qk_part[2][:, :], qk_rest[:, :], qk_part[1][:, :], ALU.subtract).then_inc(part[2], 1)
                dve.wait_ge(v_done, b + 1)
                dve.wait_ge(v_sent, 16 * b)
                nc.vector.tensor_copy(vw[:, 0:FULL, :, 0:DH].rearrange("p t h d -> p (t h) d"),
                                      p_v[:, 0, :].rearrange("p (t h d) -> p (t h) d", h=HEADS, d=DH)).then_inc(v_copied, 1)
                for q in range(QUAD):
                    r = slice(32 * q, 32 * q + 32)
                    nc.vector.tensor_copy(vw[r, FULL, :, 0:DH].rearrange("p (a q) d -> p a q d", q=QUAD)[:, :, q, :],
                                          p_v[r, 1, 0:D].rearrange("p (a q d) -> p a q d", q=QUAD, d=DH)[:, :, q, :])\
                        .then_inc(v_copied, 1)

        @block.scalar
        def _(act):
            with act.Fori(0, B) as b:
                act.wait_ge(qk_done, b + 1)
                act.wait_ge(parts_sent, 16 * PARTS * b)
                nc.scalar.copy(qk_part[0][:, :].rearrange("p (a n) -> p a n", a=NC), p_qk[:, :, 0:CH]).then_inc(part[0], 1)
                act.wait_ge(rest, b + 1)
                nc.scalar.copy(qk_part[1][:, :], qk_rest[:, :]).then_inc(part[1], 1)

        @block.tensor
        def _(pe):
            pe.wait_ge(w_in, 32)
            with pe.Fori(0, B) as b:
                pe.wait_ge(xT_ready, b)
                for t in range(NT):
                    wait_alone(pe, normed, NT * b + t + 1, pe_alone)
                    last = nc.tensor.transpose(p_turn[0:D, t // 3, (t % 3) * P:(t % 3) * P + P], xn[:, t, :], g.eye[:])
                last.then_inc(turned, 1)
                pe.wait_ge(xT_ready, b + 1)
                pe.wait_ge(rest, b)
                for a in range(NC):
                    last = nc.tensor.matmul(p_qk[:, a, 0:CH], w_qkv[:, 0:2 * D], xT[:, a * CH:a * CH + CH],
                                            start=True, stop=True)
                last.then_inc(qk_done, 1)
                pe.wait_ge(v_copied, (QUAD + 1) * b)
                for t in range(FULL):
                    nc.tensor.matmul(p_v[:, 0, t * D:t * D + D], xT[:, t * P:t * P + P], w_qkv[:, 2 * D:3 * D],
                                     start=True, stop=True)
                for q in range(QUAD):
                    last = nc.tensor.matmul(p_v[32 * q:32 * q + 32, 1, 0:D], xT[:, TOK:SEQ], w_qkv[:, 2 * D:3 * D],
                                            start=True, stop=True)
                last.then_inc(v_done, 1)


def attend_stage(g):
    nc = g.nc
    NSUM = HG * NC
    UNITS = FULL * 2 + 1
    NU = NSUM * UNITS
    chunks = [(hq, t, a) for quad in range(HG)
              for hq, t in [(quad * QUAD + q, t) for q in range(QUAD) for t in range(FULL)] + [(quad, FULL)]
              for a in range(NC)]
    NCH = len(chunks)
    MROWS = HEADS * FULL + HG
    ERING = 3
    half_in = [[g.sem(f"b_half_in{s}{q}") for q in range(HG)] for s in range(2)]
    v_in = [g.sem(f"b_v_in{s}") for s in range(2)]
    set_up, max_in = g.sem("b_set_up"), [g.software_dma_sem(f"b_max_in{s}") for s in range(2)]
    rows_done, rows_reduced = g.sem("b_rows_done"), g.sem("b_rows_reduced")
    max_step, max_turned, max_copied, max_sent = g.sem("b_max_step"), g.sem("b_max_turned"), g.sem("b_max_copied"), g.software_dma_sem("b_max_sent")
    scored, exp_done, pv_done = g.sem("b_scored"), g.sem("b_exp_done"), g.sem("b_pv_done")
    sum_copied, sum_sent = g.sem("b_sum_copied"), [g.software_dma_sem(f"b_sum_sent{n}") for n in range(2)]
    pool_alone = g.sem("b_pool_alone")
    with ExitStack() as c:
        sb = lambda n, s, d=F32: c.enter_context(nc.sbuf_tensor(n, s, d))
        ps = lambda n, s: c.enter_context(nc.psum_tensor(n, s, F32))
        q_st = [sb(f"b_q{s}", [P, HEADS, SEQ], BF16) for s in range(2)]
        k_st = [sb(f"b_k{s}", [P, HEADS, SEQ], BF16) for s in range(2)]
        vw = [sb(f"b_v{s}", [P, NT, HEADS, 32]) for s in range(2)]
        prob = sb("b_prob", [P, ERING, 2, CH])
        sums = sb("b_sums", [P, 2, CH])
        m3 = sb("b_m3", [P, MROWS, NC])
        neg_max = sb("b_neg_max", [P, MROWS])
        max_rest = sb("b_max_rest", [P, MROWS])
        max_part = sb("b_max_part", [P, PARTS, MROWS], BF16)
        max_row = sb("b_max_row", [MROWS, PARTS, P], BF16)
        p_s = ps("b_p_s", [P, 2, 2, 512])
        p_m = ps("b_p_m", [P, 3, 512])
        p_o = ps("b_p_o", [P, 512])
        p_turn = p_m[0:MROWS, 0, :].bitcast(BF16)
        block = c.enter_context(nc.Block())

        def load_half(sp, b, s, quad):
            heads = slice(quad * QUAD, quad * QUAD + QUAD)
            for kb in range(PARTS):
                sp.dma_start(q_st[s][kb * 24:kb * 24 + 24, heads, :],
                             g.qk_scr[b, 0, heads, :, :, :].rearrange("h a d t -> (a d) h t"))\
                    .then_inc(half_in[s][quad], 16)
                for qa in range(PARTS):
                    r = kb * 24 + qa * DH
                    sp.dma_start(k_st[s][r:r + DH, heads, :],
                                 g.qk_scr[b, 1, heads, kb, :, :].rearrange("h d t -> d h t"))\
                        .then_inc(half_in[s][quad], 16)

        HALF_IN = 16 * (PARTS + PARTS * PARTS)

        @block.sync
        def _(sp):
            sp.wait_ge(set_up, 8)
            for s in range(2):
                for quad in range(HG):
                    load_half(sp, s, s, quad)
                sp.dma_start(vw[s][:].rearrange("p t h d -> p (t h d)"), g.v_scr[s, :, :]).then_inc(v_in[s], 16)
            with sp.Fori(0, B // 2 - 1) as i:
                for s in range(2):
                    for quad in range(HG):
                        sp.wait_ge(pv_done, NU * (2 * i + s) + NC * UNITS * (quad + 1))
                        load_half(sp, 2 * i + s + 2, s, quad)
                    sp.dma_start(vw[s][:].rearrange("p t h d -> p (t h d)"), g.v_scr[2 * i + s + 2, :, :])\
                        .then_inc(v_in[s], 16)

        @block.gpsimd
        def _(pool):
            for s in range(2):
                nc.gpsimd.memset(q_st[s][64:P, :, :], 0.0).then_inc(set_up, 1)
                nc.gpsimd.memset(k_st[s][64:P, :, :], 0.0).then_inc(set_up, 1)
            pool.wait_ge(set_up, 4)
            for s in range(2):
                nc.gpsimd.memset(k_st[s][KPAD:P, :, :], 1.0).then_inc(set_up, 2)

            def send_max(b, s):
                wait_alone(pool, max_copied, b + 1, pool_alone)
                pool.dma_start(g.max_scr[b, :, :, :].rearrange("a r i -> r a i"), max_row[:, :, :]).then_inc(max_sent, 16)
                wait_alone(pool, max_sent, 16 * b + 16, pool_alone)
                for a in range(PARTS):
                    pool.dma_start(q_st[s][KPAD + a:KPAD + a + 1, :, 0:TOK],
                                   g.max_scr[b, a:a + 1, 0:HEADS * FULL, :].rearrange("a (h t) i -> a h (t i)", t=FULL))\
                        .then_inc(max_in[s], 16)
                for quad in range(HG):
                    pool.dma_start(q_st[s][KPAD:KMAX, quad * QUAD:quad * QUAD + QUAD, TOK:SEQ],
                                   g.max_scr[b, :, HEADS * FULL + quad, :].rearrange("a (q i) -> a q i", q=QUAD))\
                        .then_inc(max_in[s], 16)

            def send_sums(b, n):
                quad, a = divmod(n, NC)
                wait_alone(pool, sum_copied, NSUM * b + n + 1, pool_alone)
                pool.dma_start(g.sum_scr[b, :, quad * SEQ + a * CH:quad * SEQ + a * CH + CH], sums[:, n % 2, :])\
                    .then_inc(sum_sent[n % 2], 16)

            def step(b, s, with_max):
                for n in range(NSUM - 1):
                    send_sums(b, n)
                if with_max:
                    send_max(b + 1, 1 - s)
                send_sums(b, NSUM - 1)

            send_max(0, 0)
            with pool.Fori(0, B // 2 - 1) as i:
                for s in range(2):
                    step(2 * i + s, s, True)
            step(B - 2, 0, True)
            step(B - 1, 1, False)
            for n in range(2):
                pool.wait_ge(sum_sent[n], 16 * NSUM // 2 * B)

        MAX_IN = 16 * (PARTS + HG)

        @block.scalar
        def _(act):
            def copy_sums(b, n):
                act.wait_ge(pv_done, NU * b + UNITS * (n + 1))
                act.wait_ge(sum_sent[n % 2], 16 * (NSUM // 2 * b + n // 2))
                nc.scalar.copy(sums[:, n % 2, :], p_o[:, 0:CH]).then_inc(sum_copied, 1)

            def step(b):
                for u in range(NU):
                    act.wait_ge(scored, NU * b + u + 1)
                    act.wait_ge(pv_done, NU * b + max(u - ERING + 1, 0))
                    heads = 2 if u % UNITS < UNITS - 1 else 1
                    nc.scalar.activation(prob[:, u % ERING, 0:heads, :], p_s[:, u % 2, 0:heads, 0:CH], ACT.Exp,
                                         scale=float(D) ** -0.5).then_inc(exp_done, 1)
                    if u % UNITS == 1 and u > UNITS:
                        copy_sums(b, u // UNITS - 1)
                copy_sums(b, NSUM - 1)

            with act.Fori(0, B) as b:
                step(b)

        @block.vector
        def _(dve):
            def maxima(b):
                for k, (hq, t, a) in enumerate(chunks):
                    row = hq * FULL + t if t < FULL else HEADS * FULL + hq
                    dve.wait_ge(rows_done, NCH * b + k + 1)
                    nc.vector.tensor_reduce(m3[:, row, a:a + 1], p_m[:, k % 3, 0:CH], axis=AX.X, op=ALU.max)\
                        .then_inc(rows_reduced, 1)
                dve.wait_ge(rows_reduced, NCH * b + NCH)
                nc.vector.tensor_reduce(neg_max[:, :], m3[:, :, :], axis=AX.X, op=ALU.max, negate=True).then_inc(max_step, 1)
                dve.wait_ge(max_step, 6 * b + 1)
                nc.vector.tensor_copy(max_part[:, 0, :], neg_max[:, :]).then_inc(max_step, 1)
                dve.wait_ge(max_step, 6 * b + 2)
                nc.vector.tensor_tensor(max_rest[:, :], neg_max[:, :], max_part[:, 0, :], ALU.subtract).then_inc(max_step, 1)
                dve.wait_ge(max_step, 6 * b + 3)
                nc.vector.tensor_copy(max_part[:, 1, :], max_rest[:, :]).then_inc(max_step, 1)
                dve.wait_ge(max_step, 6 * b + 4)
                nc.vector.tensor_tensor(max_part[:, 2, :], max_rest[:, :], max_part[:, 1, :], ALU.subtract).then_inc(max_step, 2)
                dve.wait_ge(max_turned, b + 1)
                dve.wait_ge(max_sent, 16 * b)
                nc.vector.tensor_copy(max_row[:, :, :].rearrange("r a i -> r (a i)"), p_turn[:, 0:PARTS * P])\
                    .then_inc(max_copied, 1)

            with dve.Fori(0, B) as b:
                maxima(b)

        @block.tensor
        def _(pe):
            def row_chunk(b, s, k):
                hq, t, a = chunks[k]
                if k == 0:
                    pe.wait_ge(max_copied, b)
                pe.wait_ge(rows_reduced, NCH * b + max(k - 2, 0))
                cols = slice(a * CH, a * CH + CH)
                if t < FULL:
                    last = nc.tensor.matmul(p_m[:, k % 3, 0:CH], q_st[s][0:KPAD, hq, t * P:t * P + P],
                                            k_st[s][0:KPAD, hq, cols], start=True, stop=True)
                else:
                    for q in range(QUAD):
                        h = hq * QUAD + q
                        last = nc.tensor.matmul(p_m[32 * q:32 * q + 32, k % 3, 0:CH], q_st[s][0:KPAD, h, TOK:SEQ],
                                                k_st[s][0:KPAD, h, cols], start=True, stop=True)
                last.then_inc(rows_done, 1)

            def turn_max(b):
                pe.wait_ge(max_step, 6 * b + 6)
                pe.wait_ge(rows_reduced, NCH * b + NCH)
                for a in range(PARTS):
                    last = nc.tensor.transpose(p_turn[:, a * P:a * P + P], max_part[:, a, :], g.eye_bf[:])
                last.then_inc(max_turned, 1)

            def unit(u):
                n, r = divmod(u, UNITS)
                return (n, FULL, 0) if r == UNITS - 1 else (n, r // 2, r % 2)

            def score(b, s, u):
                n, jt, pair = unit(u)
                quad, a = divmod(n, NC)
                cols = slice(a * CH, a * CH + CH)
                pe.wait_ge(exp_done, NU * b + max(u - 1, 0))
                if jt < FULL:
                    for e in range(2):
                        h = quad * QUAD + 2 * pair + e
                        last = nc.tensor.matmul(p_s[:, u % 2, e, 0:CH], k_st[s][0:KMAX, h, jt * P:jt * P + P],
                                                q_st[s][0:KMAX, h, cols], start=True, stop=True)
                else:
                    for q in range(QUAD):
                        h = quad * QUAD + q
                        last = nc.tensor.matmul(p_s[32 * q:32 * q + 32, u % 2, 0, 0:CH], k_st[s][0:KMAX, h, TOK:SEQ],
                                                q_st[s][0:KMAX, h, cols], start=True, stop=True)
                last.then_inc(scored, 1)
                return last

            def weigh(b, s, u):
                n, jt, pair = unit(u)
                quad = n // NC
                if u % UNITS == 0:
                    pe.wait_ge(sum_copied, NSUM * b + n)
                pe.wait_ge(exp_done, NU * b + u + 1)
                for e in range(2 if jt < FULL else QUAD):
                    q = 2 * pair + e
                    h = quad * QUAD + q
                    last = nc.tensor.matmul(p_o[32 * q:32 * q + 32, 0:CH], vw[s][:, jt, h, :],
                                            prob[:, u % ERING, e if jt < FULL else 0, :],
                                            start=(jt == 0), stop=(jt == FULL), skip_group_check=True)
                last.then_inc(pv_done, 1)

            def step(b, i, s, i_next):
                pe.wait_ge(max_in[s], MAX_IN * (i + 1))
                pe.wait_ge(v_in[s], 16 * (i + 1))
                score(b, s, 0)
                k = 0
                until = NU - 14
                for u in range(NU):
                    if u + 1 < NU:
                        score(b, s, u + 1)
                    if i_next is not None:
                        while k < NCH and k < (u + 1) * NCH / until:
                            if k == 0 or k == NCH // 2:
                                pe.wait_ge(half_in[1 - s][k // (NCH // 2)], HALF_IN * (i_next + 1))
                            row_chunk(b + 1, 1 - s, k)
                            k += 1
                        if u == NU - 10:
                            turn_max(b + 1)
                    weigh(b, s, u)

            for k in range(NCH):
                if k == 0 or k == NCH // 2:
                    pe.wait_ge(half_in[0][k // (NCH // 2)], HALF_IN)
                row_chunk(0, 0, k)
            turn_max(0)
            with pe.Fori(0, B // 2 - 1) as i:
                step(2 * i, i, 0, i)
                step(2 * i + 1, i, 1, i + 1)
            step(B - 2, B // 2 - 1, 0, B // 2 - 1)
            step(B - 1, B // 2 - 1, 1, None)


def join_stage(g):
    nc, arg, hid = g.nc, g.arg, g.hid
    w_in, set_up = g.sem("c_w_in"), g.sem("c_set_up")
    sums_in = [g.sem(f"c_sums_in{s}") for s in range(2)]
    turned, inverted, scaled = g.sem("c_turned"), g.sem("c_inverted"), g.sem("c_scaled")
    back, back_copied, projected, added = g.sem("c_back"), g.sem("c_back_copied"), g.sem("c_projected"), g.sem("c_added")
    pe_alone = g.sem("c_pe_alone")
    W = HEADS * 32
    with ExitStack() as c:
        sb = lambda n, s, d=F32: c.enter_context(nc.sbuf_tensor(n, s, d))
        ps = lambda n, s: c.enter_context(nc.psum_tensor(n, s, F32))
        sums = [sb(f"c_sums{s}", [P, HG, SEQ]) for s in range(2)]
        inv = sb("c_inv", [P, NT, HEADS])
        att = sb("c_att", [P, NT, HEADS, DH])
        attT = sb("c_attT", [P, NT * P])
        w_out = sb("c_w_out", [P, D])
        p_turn = ps("c_p_turn", [P, FULL // 2, 2, HEADS, 32])
        p_last = ps("c_p_last", [P, 512])
        p_back = ps("c_p_back", [P, 1, 512])
        p_out = ps("c_p_out", [P, 2, 512])
        block = c.enter_context(nc.Block())
        p_last_h = p_last[0:TXT, 0:W].rearrange("p (h d) -> p h d", h=HEADS)
        p_full = p_turn[:].rearrange("p a b h d -> p (a b) h d")

        @block.sync
        def _(sp):
            sp.wait_ge(set_up, 2)
            sp.dma_start(w_out[0:D, :], arg["L0_attn_w_out"]).then_inc(w_in, 16)
            sp.dma_start(w_out[D:D + 1, :], arg["L0_attn_b_out"].rearrange("(a n) -> a n", a=1)).then_inc(w_in, 16)
            with sp.Fori(0, B // 2) as i:
                for s in range(2):
                    sp.wait_ge(turned, NT * (2 * i))
                    sp.dma_start(sums[s][:].rearrange("p a t -> p (a t)"), g.sum_scr[2 * i + s, :, :]).then_inc(sums_in[s], 16)

        @block.gpsimd
        def _(pool):
            nc.gpsimd.memset(w_out[D:P, :], 0.0).then_inc(set_up, 1)
            nc.gpsimd.memset(attT[D:P, :], 0.0).then_inc(set_up, 1)
            pool.wait_ge(set_up, 2)
            nc.gpsimd.memset(attT[D:D + 1, :], 1.0).then_inc(set_up, 1)
            pool.wait_ge(set_up, 3)
            nc.gpsimd.memset(att[:, FULL, :, :], 0.0).then_inc(set_up, 1)

        @block.tensor
        def _(pe):
            pe.wait_ge(w_in, 32)
            with pe.Fori(0, B // 2) as i:
                for s in range(2):
                    b = 2 * i + s
                    pe.wait_ge(sums_in[s], 16 * i + 16)
                    pe.wait_ge(scaled, 2 * b)
                    for t in range(NT):
                        for quad in range(HG):
                            if t < FULL:
                                dst = p_turn[:, t // 2, t % 2, quad * QUAD:quad * QUAD + QUAD, :].rearrange("p h d -> p (h d)")
                                last = nc.tensor.transpose(dst, sums[s][:, quad, t * P:t * P + P], g.eye[:])
                            else:
                                last = nc.tensor.transpose(p_last[0:TXT, quad * P:quad * P + P],
                                                           sums[s][:, quad, TOK:SEQ], g.eye[:])
                        last.then_inc(turned, 1)
                    for a in range(3):
                        wait_alone(pe, scaled, 2 * b + (1 if a < 2 else 2), pe_alone)
                        wait_alone(pe, back_copied, 3 * b + a, pe_alone)
                        for t in range(3 * a, 3 * a + 3):
                            last = nc.tensor.transpose(p_back[0:D, 0, (t % 3) * P:(t % 3) * P + P],
                                                       att[:, t, :, :].rearrange("p h d -> p (h d)"), g.eye[:])
                        last.then_inc(back, 1)
                    pe.wait_ge(back_copied, 3 * b + 3)
                    pe.wait_ge(added, 2 * b)
                    for t in range(NT):
                        last = nc.tensor.matmul(p_out[:, t // FULL, (t % FULL) * D:(t % FULL) * D + D],
                                                attT[:, t * P:t * P + P], w_out[:, :], start=True, stop=True)
                    last.then_inc(projected, 1)

        @block.scalar
        def _(act):
            act.wait_ge(set_up, 4)
            with act.Fori(0, B) as b:
                for a in range(3):
                    act.wait_ge(back, 3 * b + a + 1)
                    act.wait_ge(projected, b)
                    nc.scalar.copy(attT[0:D, 3 * a * P:3 * a * P + 3 * P], p_back[0:D, 0, 0:3 * P]).then_inc(back_copied, 1)

        @block.vector
        def _(dve):
            dve.wait_ge(set_up, 4)
            with dve.Fori(0, B) as b:
                dve.wait_ge(turned, NT * b + NT)
                nc.vector.reciprocal(inv[:, 0:FULL, :], p_full[:, :, :, DH]).then_inc(inverted, 1)
                nc.vector.reciprocal(inv[0:TXT, FULL, :], p_last_h[:, :, DH]).then_inc(inverted, 1)
                dve.wait_ge(inverted, 2 * b + 2)
                dve.wait_ge(back, 3 * b)
                nc.vector.tensor_tensor(att[:, 0:FULL, :, :].rearrange("p t h d -> p (t h) d"),
                                        p_full[:, :, :, 0:DH].rearrange("p t h d -> p (t h) d"),
                                        inv[:, 0:FULL, :].rearrange("p t h -> p (t h)").unsqueeze(2)
                                        .to_broadcast([P, FULL * HEADS, DH]), ALU.mult).then_inc(scaled, 1)
                nc.vector.tensor_tensor(att[0:TXT, FULL, :, :], p_last_h[:, :, 0:DH],
                                        inv[0:TXT, FULL, :].unsqueeze(2).to_broadcast([TXT, HEADS, DH]), ALU.mult).then_inc(scaled, 1)
                dve.wait_ge(projected, b + 1)
                nc.vector.tensor_tensor(hid[:, b, 0:FULL, :].rearrange("p t d -> p (t d)"),
                                        hid[:, b, 0:FULL, :].rearrange("p t d -> p (t d)"), p_out[:, 0, :], ALU.add).then_inc(added, 1)
                nc.vector.tensor_tensor(hid[0:TXT, b, FULL, :], hid[0:TXT, b, FULL, :], p_out[0:TXT, 1, 0:D], ALU.add).then_inc(added, 1)


def split_parts(nc, eng, value, part, rest, done, count):
    nc.vector.tensor_copy(part[0], value).then_inc(done, 1)
    eng.wait_ge(done, count + 1)
    nc.vector.tensor_tensor(rest, value, part[0], ALU.subtract).then_inc(done, 1)
    eng.wait_ge(done, count + 2)
    nc.vector.tensor_copy(part[1], rest).then_inc(done, 1)
    eng.wait_ge(done, count + 3)
    nc.vector.tensor_tensor(part[2], rest, part[1], ALU.subtract).then_inc(done, 2)


def gate_block(g, pre, E, gate_w, gate_b, keep, xT_all, cT_all):
    nc, hid = g.nc, g.hid
    ln = [g.sem(pre + n) for n in ("stats", "moments", "rstd", "alone")]
    w_in, set_up, normed, kept = g.sem(pre + "w_in"), g.sem(pre + "set_up"), g.sem(pre + "normed"), g.sem(pre + "kept")
    turned, xT_ready, xT_kept = g.sem(pre + "turned"), g.sem(pre + "xT_ready"), g.sem(pre + "xT_kept")
    logits_done, step, gap_ready, gap_exp = g.sem(pre + "logits"), g.sem(pre + "step"), g.sem(pre + "gap"), g.sem(pre + "gap_exp")
    best, split = g.sem(pre + "best"), g.sem(pre + "split")
    stacked, c_turned, c_kept, pe_alone = g.sem(pre + "stacked"), g.sem(pre + "c_turned"), g.sem(pre + "c_kept"), g.sem(pre + "pe_alone")
    with ExitStack() as c:
        sb = lambda n, s, d=F32: c.enter_context(nc.sbuf_tensor(pre + n, s, d))
        ps = lambda n, s: c.enter_context(nc.psum_tensor(pre + n, s, F32))
        st, mv, xn = sb("st", [P, NT, 6]), sb("mv", [P, NT, 4]), sb("xn", [P, NT, 2, D])
        xT = sb("xT", [P, NT * P])
        gw, gb, number = sb("gw", [P, E]), sb("gb", [P, E]), sb("number", [P, EINS])
        logit = sb("logit", [P, NT, E])
        top, top_at, at = sb("top", [P, NT, 8]), sb("top_at", [P, NT, 8], U32), sb("at", [P, NT, 2])
        gap, gap_e, w1, w2, den = (sb(n, [P, NT]) for n in ("gap", "gap_e", "w1", "w2", "den"))
        is1, is2, cw, c_rest = (sb(n, [P, NT, E]) for n in ("is1", "is2", "cw", "c_rest"))
        c_part = [sb(f"c_part{i}", [P, NT, E], BF16) for i in range(PARTS)]
        c_stack = sb("c_stack", [P, NT, len(PAIRS), EINS], BF16)
        p_turn = ps("p_turn", [P, 3, 512])
        p_log = ps("p_log", [P, NT, E])
        p_c = ps("p_c", [P, 2, 512])
        block = c.enter_context(nc.Block())
        p_ct = [p_c[0:GK, k, :].bitcast(BF16) for k in range(2)]

        @block.sync
        def _(sp):
            sp.wait_ge(set_up, 1)
            sp.dma_start(gw[0:D, :], gate_w, allow_slow_non_contiguous=True).then_inc(w_in, 16)
            sp.dma_start(gb[:, :], gate_b.rearrange("(a e) -> a e", a=1).to_broadcast([P, E])).then_inc(w_in, 16)
            sp.dma_start(number[:, :], g.const["number"].to_broadcast([P, EINS])).then_inc(w_in, 16)

        @block.gpsimd
        def _(pool):
            nc.gpsimd.memset(gw[D:P, :], 0.0).then_inc(set_up, 1)
            pool.wait_ge(set_up, 1)
            nc.gpsimd.memset(c_stack[:], 0.0).then_inc(set_up, 1)
            with pool.Fori(0, B) as b:
                layernorm_pool(g, pool, b, mv, ln)

        @block.tensor
        def _(pe):
            pe.wait_ge(w_in, 48)
            with pe.Fori(0, B) as b:
                pe.wait_ge(xT_ready, b)
                wait_alone(pe, normed, NT * b + NT, pe_alone)
                for t in range(NT):
                    last = nc.tensor.transpose(p_turn[:, t // 3, (t % 3) * P:(t % 3) * P + P],
                                               xn[:, t, :, :].rearrange("p q d -> p (q d)"), g.eye[:])
                last.then_inc(turned, 1)
                pe.wait_ge(xT_ready, b + 1)
                pe.wait_ge(step, 10 * b)
                for t in range(NT):
                    last = nc.tensor.matmul(p_log[:, t, :], xT[:, t * P:t * P + P], gw[:, :], start=True, stop=True)
                last.then_inc(logits_done, 1)
                pe.wait_ge(stacked, len(PAIRS) * (b + 1))
                wait_alone(pe, c_kept, 2 * b, pe_alone)
                for t in range(NT):
                    last = nc.tensor.transpose(p_ct[t // FULL][:, (t % FULL) * P:(t % FULL) * P + P],
                                               c_stack[:, t, :, :].rearrange("p k e -> p (k e)"), g.eye_bf[:])
                last.then_inc(c_turned, 1)

        @block.scalar
        def _(act):
            act.wait_ge(set_up, 2)
            with act.Fori(0, B) as b:
                act.wait_ge(turned, b + 1)
                act.wait_ge(logits_done, b)
                act.wait_ge(xT_kept, b)
                nc.scalar.copy(xT[:, :].rearrange("p (a n) -> p a n", a=3), p_turn[:, :, 0:3 * P]).then_inc(xT_ready, 1)
                act.wait_ge(xT_ready, b + 1)
                nc.scalar.copy(xT_all[:, b, :], xT[:, 0:SEQ]).then_inc(xT_kept, 1)
                if keep is not None:
                    nc.scalar.copy(keep[:, b, :, :], xn[:, :, 0, :]).then_inc(kept, 1)
                act.wait_ge(gap_ready, b + 1)
                nc.scalar.activation(gap_e[:, :], gap[:, :], ACT.Exp).then_inc(gap_exp, 1)
                act.wait_ge(split, 5 * b + 5)
                act.wait_ge(c_turned, b)
                for k, (ci, _) in enumerate(PAIRS):
                    nc.scalar.copy(c_stack[:, :, k, 0:E], c_part[ci][:, :, :]).then_inc(stacked, 1)
                act.wait_ge(c_turned, b + 1)
                nc.scalar.copy(cT_all[:, b, 0:TOK], p_ct[0][:, :]).then_inc(c_kept, 1)
                nc.scalar.copy(cT_all[:, b, TOK:SEQ], p_ct[1][:, 0:TXT]).then_inc(c_kept, 1)

        @block.vector
        def _(dve):
            dve.wait_ge(w_in, 48)

            def norm(b):
                dve.wait_ge(turned, b)
                if keep is not None:
                    dve.wait_ge(kept, b)
                layernorm_dve(nc, dve, b, lambda t: hid[:, b, t, :], lambda t: xn[:, t, :, :], st, mv, ln, normed, twice=True)

            def choose(b):
                wide = lambda v: v.unsqueeze(2).to_broadcast([P, NT, E])
                dve.wait_ge(logits_done, b + 1)
                nc.vector.tensor_tensor(logit[:, :, :], p_log[:, :, :], gb[:, :].unsqueeze(1).to_broadcast([P, NT, E]),
                                        ALU.add).then_inc(step, 1)
                wait_alone(dve, step, 10 * b + 1, ln[3])
                for t in range(NT):
                    nc.vector.max(top[:, t, :], logit[:, t, :]).then_inc(best, 1)
                wait_alone(dve, best, 2 * NT * b + NT, ln[3])
                for t in range(NT):
                    nc.vector.max_index(top_at[:, t, :], top[:, t, :], logit[:, t, :]).then_inc(best, 1)
                nc.vector.tensor_tensor(gap[:, :], top[:, :, 1], top[:, :, 0], ALU.subtract).then_inc(gap_ready, 1)
                dve.wait_ge(best, 2 * NT * b + 2 * NT)
                nc.vector.tensor_copy(at[:, :, :], top_at[:, :, 0:2]).then_inc(step, 1)
                dve.wait_ge(gap_exp, b + 1)
                nc.vector.tensor_scalar(den[:, :], gap_e[:, :], 1.0, None, ALU.add).then_inc(step, 1)
                dve.wait_ge(step, 10 * b + 3)
                nc.vector.reciprocal(w1[:, :], den[:, :]).then_inc(step, 1)
                nc.vector.tensor_tensor(is1[:, :, :], number[:, 0:E].unsqueeze(1).to_broadcast([P, NT, E]), wide(at[:, :, 0]),
                                        ALU.is_equal).then_inc(step, 1)
                nc.vector.tensor_tensor(is2[:, :, :], number[:, 0:E].unsqueeze(1).to_broadcast([P, NT, E]), wide(at[:, :, 1]),
                                        ALU.is_equal).then_inc(step, 1)
                dve.wait_ge(step, 10 * b + 6)
                nc.vector.tensor_tensor(w2[:, :], gap_e[:, :], w1[:, :], ALU.mult).then_inc(step, 1)
                nc.vector.tensor_tensor(is1[:, :, :], is1[:, :, :], wide(w1[:, :]), ALU.mult).then_inc(step, 1)
                dve.wait_ge(step, 10 * b + 8)
                nc.vector.tensor_tensor(is2[:, :, :], is2[:, :, :], wide(w2[:, :]), ALU.mult).then_inc(step, 1)
                dve.wait_ge(step, 10 * b + 9)
                nc.vector.tensor_tensor(cw[:, :, :], is1[:, :, :], is2[:, :, :], ALU.add).then_inc(step, 1)
                dve.wait_ge(step, 10 * b + 10)
                dve.wait_ge(stacked, len(PAIRS) * b)
                split_parts(nc, dve, cw[:, :, :], [v[:, :, :] for v in c_part], c_rest[:, :, :], split, 5 * b)

            norm(0)
            with dve.Fori(0, B - 1) as b:
                norm(b + 1)
                choose(b)
            choose(B - 1)


def experts_block(g, pre, E, H, w1_arg, b1_arg, w2_arg, b2_arg, turned_weights, xT_all, cT_all, acc, send):
    nc = g.nc
    HALVES = H // P
    NP = E // 2
    w_in, set_up, w_turned, w_copied = g.sem(pre + "w_in"), g.sem(pre + "set_up"), g.sem(pre + "w_turned"), g.sem(pre + "w_copied")
    bias_step, w_ready = g.sem(pre + "bias_step"), g.sem(pre + "w_ready")
    spread, scaled = g.sem(pre + "spread"), g.sem(pre + "scaled")
    hidden_done, relu_done, summed, sum_copied = g.sem(pre + "hidden"), g.sem(pre + "relu"), g.sem(pre + "summed"), g.sem(pre + "sum_copied")
    y_turned, added, sent, pe_alone = g.sem(pre + "y_turned"), g.sem(pre + "added"), g.sem(pre + "sent"), g.sem(pre + "pe_alone")
    dve_alone = g.sem(pre + "dve_alone")
    ZR, HR = 3, 3
    HID = NP * 2 * HALVES
    assert (NC * HID) % ZR == 0 and (NC * HID) % HR == 0 and NP % 2 == 0
    with ExitStack() as c:
        sb = lambda n, s, d=F32: c.enter_context(nc.sbuf_tensor(pre + n, s, d))
        ps = lambda n, s: c.enter_context(nc.psum_tensor(pre + n, s, F32))
        w1 = sb("w1", [P, E, HALVES, P])
        w2 = sb("w2", [P, E, HALVES, D])
        pick = sb("pick", [GK, EINS // 2, P])
        pick_bf = sb("pick_bf", [GK, EINS // 2, P], BF16)
        part_of, own = sb("part_of", [GK, PARTS]), sb("own", [GK, EINS])
        b_raw, b_rest, b_sel = (sb(n, [GK, H + D]) for n in ("b_raw", "b_rest", "b_sel"))
        b_part = [sb(f"b_part{i}", [GK, H + D], BF16) for i in range(PARTS)]
        b1s = sb("b1s", [GK, E, HALVES, P], BF16)
        b2s = sb("b2s", [GK, D], BF16)
        xs = sb("xs", [P, 2, CH])
        hidden = sb("hidden", [P, HR, CH])
        yT = sb("yT", [P, NT * P])
        if turned_weights:
            w1_raw = sb("w1_raw", [P, NP, HALVES, 2, D])
            w2_raw = sb("w2_raw", [P, NP, H])
        p_c = ps("p_c", [P, 2, 512])
        p_z = ps("p_z", [P, ZR, 512])
        p_y = ps("p_y", [P, 2, 512])
        p_t = ps("p_t", [P, 3, 2, D])
        block = c.enter_context(nc.Block())
        N_IN = 3 + 2 * len(PAIRS) + (E + 1 if turned_weights else 3)
        WQ = NP * HALVES

        @block.sync
        def _(sp):
            sp.dma_start(pick[:], g.const["pick"]).then_inc(w_in, 16)
            sp.dma_start(part_of[:], g.const["part_of"]).then_inc(w_in, 16)
            sp.dma_start(own[:], g.const["own"]).then_inc(w_in, 16)
            sp.wait_ge(set_up, 2)
            n = 3
            for k in range(len(PAIRS)):
                sp.dma_start(b_raw[k * EINS:k * EINS + E, 0:H], b1_arg).then_inc(w_in, 16)
                sp.dma_start(b_raw[k * EINS:k * EINS + E, H:H + D], b2_arg).then_inc(w_in, 16)
                n += 2
            if turned_weights:
                for e in range(E):
                    sp.dma_start(w1_raw[:, e // 2, :, e % 2, :], w1_arg[e, :, :].rearrange("(f h) d -> h f d", h=P)).then_inc(w_in, 16)
                    n += 1
                sp.dma_start(w2_raw[:], w2_arg.rearrange("(n q) d h -> (q d) n h", q=2)).then_inc(w_in, 16)
                n += 1
            else:
                for q in range(2):
                    sp.dma_start(w1[q * D:q * D + D, :, :, :].rearrange("p (n q) f h -> p n q (f h)", q=2)[:, :, q, :],
                                 w1_arg.rearrange("(n q) d h -> q d n h", q=2)[q]).then_inc(w_in, 16)
                sp.dma_start(w2[:].rearrange("p e f d -> p (e f) d"), w2_arg.rearrange("e h d -> h e d")).then_inc(w_in, 16)
                n += 3
            assert n == N_IN
            if send:
                with sp.Fori(0, B) as b:
                    sp.wait_ge(added, 6 * b + 6)
                    sp.dma_start(g.out[b, 0:TOK, :].rearrange("(t p) d -> p t d", p=P), acc[:, b, 0:FULL, :]).then_inc(sent, 16)
                    sp.dma_start(g.out[b, TOK:SEQ, :], acc[0:TXT, b, FULL, :]).then_inc(sent, 16)
                sp.wait_ge(sent, 32 * B)

        @block.gpsimd
        def _(pool):
            nc.gpsimd.memset(w1[:], 0.0).then_inc(set_up, 1)
            pool.wait_ge(set_up, 1)
            nc.gpsimd.memset(b_raw[:], 0.0).then_inc(set_up, 1)
            pool.wait_ge(set_up, 2)
            nc.gpsimd.memset(yT[:, SEQ:NT * P], 0.0).then_inc(set_up, 1)

        @block.tensor
        def _(pe):
            pe.wait_ge(w_in, 16 * N_IN)
            if turned_weights:
                for k in range(2 * WQ):
                    n, f = divmod(k // 2, HALVES)
                    if k >= 2:
                        pe.wait_ge(w_copied, k - 1)
                    src = w1_raw[:, n, f, :, :].rearrange("p q d -> p (q d)") if k % 2 == 0 else w2_raw[:, n, f * P:f * P + P]
                    nc.tensor.transpose(p_z[:, k % 2, 0:P], src, g.eye[:]).then_inc(w_turned, 1)
                pe.wait_ge(w_copied, 2 * WQ)
            pe.wait_ge(w_ready, 1)

            def rows_of(b, a):
                return cT_all[:, b, a * CH:a * CH + CH]

            def spread_gates(b, a, n):
                m = NC * NP * b + a * NP + n
                pe.wait_ge(scaled, m - 1 if a * NP + n else NC * NP * b)
                nc.tensor.matmul(p_c[:, n % 2, 0:CH], pick_bf[:, n, :], rows_of(b, a), start=True, stop=True)\
                    .then_inc(spread, 1)

            def first(b, a, k):
                e, f = divmod(k, HALVES)
                m = a * HID + k
                pe.wait_ge(relu_done, NC * HID * b + max(m - ZR + 1, 0))
                if k % (2 * HALVES) == 0:
                    pe.wait_ge(scaled, NC * NP * b + a * NP + e // 2 + 1)
                nc.tensor.matmul(p_z[:, m % ZR, 0:CH], w1[:, e, f, :], xs[:, (e // 2) % 2, :], start=True, stop=False)
                nc.tensor.matmul(p_z[:, m % ZR, 0:CH], b1s[:, e, f, :], rows_of(b, a), start=False, stop=True)\
                    .then_inc(hidden_done, 1)

            def second(b, a, k):
                e, f = divmod(k, HALVES)
                m = a * HID + k
                half = slice(e % 2 * D, e % 2 * D + D)
                bank = a % 2
                if k == 0:
                    wait_alone(pe, sum_copied, NC * b + max(a - 1, 0), pe_alone)
                    nc.tensor.matmul(p_y[0:D, bank, 0:CH], b2s[:, :], rows_of(b, a), start=True, stop=False,
                                     skip_group_check=True)
                pe.wait_ge(relu_done, NC * HID * b + m + 1)
                last = nc.tensor.matmul(p_y[half, bank, 0:CH], w2[:, e, f, :], hidden[:, m % HR, :],
                                        start=(e % 2 == 1 and k == HALVES), stop=(k >= HID - HALVES - 1),
                                        skip_group_check=True)
                last.then_inc(summed, 1)

            with pe.Fori(0, B) as b:
                for a in range(NC):
                    if a == 0:
                        spread_gates(b, 0, 0)
                    for k in range(HID + 1):
                        if k < HID:
                            if k % (2 * HALVES) == 0:
                                if k // (2 * HALVES) + 1 < NP:
                                    spread_gates(b, a, k // (2 * HALVES) + 1)
                                elif a + 1 < NC:
                                    spread_gates(b, a + 1, 0)
                            first(b, a, k)
                        if k > 0:
                            second(b, a, k - 1)
                for r in range(3):
                    pe.wait_ge(sum_copied, NC * b + NC)
                    wait_alone(pe, added, 6 * b + 2 * r, pe_alone)
                    for t in range(3 * r, 3 * r + 3):
                        last = nc.tensor.transpose(p_t[:, t % 3, :, :].rearrange("p q d -> p (q d)"), yT[:, t * P:t * P + P], g.eye[:])
                    last.then_inc(y_turned, 1)

        @block.scalar
        def _(act):
            act.wait_ge(set_up, 3)
            with act.Fori(0, B) as b:
                def copy_sum(a):
                    act.wait_ge(summed, NC * HID * b + (a + 1) * HID)
                    act.wait_ge(y_turned, 3 * b)
                    nc.scalar.copy(yT[:, a * CH:a * CH + CH], p_y[:, a % 2, 0:CH]).then_inc(sum_copied, 1)

                for m in range(NC * HID):
                    act.wait_ge(hidden_done, NC * HID * b + m + 1)
                    act.wait_ge(summed, NC * HID * b + max(m - HR + 1, 0))
                    nc.scalar.activation(hidden[:, m % HR, :], p_z[:, m % ZR, 0:CH], ACT.Relu).then_inc(relu_done, 1)
                    if m % HID == 1 and m > HID:
                        copy_sum(m // HID - 1)
                copy_sum(NC - 1)

        @block.vector
        def _(dve):
            dve.wait_ge(w_in, 16 * N_IN)
            nc.vector.tensor_copy(pick_bf[:], pick[:]).then_inc(bias_step, 1)
            if turned_weights:
                for k in range(2 * WQ):
                    n, f = divmod(k // 2, HALVES)
                    dve.wait_ge(w_turned, k + 1)
                    if k % 2 == 0:
                        nc.vector.tensor_copy(w1[0:D, 2 * n, f, :], p_z[0:D, 0, 0:P])
                        nc.vector.tensor_copy(w1[D:P, 2 * n + 1, f, :], p_z[D:P, 0, 0:P]).then_inc(w_copied, 1)
                    else:
                        nc.vector.tensor_copy(w2[:, 2 * n:2 * n + 2, f, :], p_z[:, 1, 0:P].rearrange("p (q d) -> p q d", q=2))\
                            .then_inc(w_copied, 1)
            split_parts(nc, dve, b_raw[:, :], [v[:, :] for v in b_part], b_rest[:, :], bias_step, 1)
            dve.wait_ge(bias_step, 6)
            nc.vector.tensor_scalar(b_sel[:, :], b_part[0][:, :], part_of[:, 0:1], None, ALU.mult).then_inc(bias_step, 1)
            for i in range(1, PARTS):
                dve.wait_ge(bias_step, 6 + i)
                nc.vector.scalar_tensor_tensor(b_sel[:, :], b_part[i][:, :], part_of[:, i:i + 1], b_sel[:, :],
                                               ALU.mult, ALU.add).then_inc(bias_step, 1)
            dve.wait_ge(bias_step, 6 + PARTS)
            nc.vector.tensor_copy(b2s[:, :], b_sel[:, H:H + D])
            for e in range(E):
                last = nc.vector.tensor_scalar(b1s[:, e, :, :].rearrange("p f h -> p (f h)"), b_sel[:, 0:H],
                                               own[:, e:e + 1], None, ALU.mult)
            last.then_inc(w_ready, 1)
            with dve.Fori(0, B) as b:
                for a in range(NC):
                    for n in range(NP):
                        m = a * NP + n
                        dve.wait_ge(spread, NC * NP * b + m + 1)
                        dve.wait_ge(hidden_done, NC * HID * b + max(m - 1, 0) * 2 * HALVES)
                        nc.vector.tensor_tensor(xs[:, n % 2, :], xT_all[:, b, a * CH:a * CH + CH], p_c[:, n % 2, 0:CH],
                                                ALU.mult).then_inc(scaled, 1)
                for r in range(3):
                    rows = acc[:, b, 3 * r:3 * r + 3, :]
                    dve.wait_ge(y_turned, 3 * b + r + 1)
                    for q in range(2):
                        if q:
                            dve.wait_ge(added, 6 * b + 2 * r + 1)
                        nc.vector.tensor_tensor(rows, rows, p_t[:, :, q, :], ALU.add).then_inc(added, 1)


def affine_block(g, pre, xn_all, gamma_arg, beta_arg):
    nc, hid = g.nc, g.hid
    ln = [g.sem(pre + n) for n in ("stats", "moments", "rstd", "alone")]
    w_in, normed, step = g.sem(pre + "w_in"), g.sem(pre + "normed"), g.sem(pre + "step")
    with ExitStack() as c:
        sb = lambda n, s, d=F32: c.enter_context(nc.sbuf_tensor(pre + n, s, d))
        st, mv, y = sb("st", [P, NT, 6]), sb("mv", [P, NT, 4]), sb("y", [P, NT, D])
        gamma, beta = sb("gamma", [P, D]), sb("beta", [P, D])
        block = c.enter_context(nc.Block())

        @block.sync
        def _(sp):
            sp.dma_start(gamma[:, :], gamma_arg.rearrange("(a d) -> a d", a=1).to_broadcast([P, D])).then_inc(w_in, 16)
            sp.dma_start(beta[:, :], beta_arg.rearrange("(a d) -> a d", a=1).to_broadcast([P, D])).then_inc(w_in, 16)

        @block.gpsimd
        def _(pool):
            with pool.Fori(0, B) as b:
                layernorm_pool(g, pool, b, mv, ln)

        @block.vector
        def _(dve):
            dve.wait_ge(w_in, 32)
            wide = lambda v: v[:, :].unsqueeze(1).to_broadcast([P, NT, D])
            with dve.Fori(0, B) as b:
                layernorm_dve(nc, dve, b, lambda t: xn_all[:, b, t, :], lambda t: y[:, t, :], st, mv, ln, normed)
                dve.wait_ge(normed, NT * b + NT)
                nc.vector.tensor_tensor(y[:, :, :], y[:, :, :], wide(gamma), ALU.mult).then_inc(step, 1)
                dve.wait_ge(step, 4 * b + 1)
                nc.vector.tensor_tensor(y[:, :, :], y[:, :, :], wide(beta), ALU.add).then_inc(step, 1)
                dve.wait_ge(step, 4 * b + 2)
                nc.vector.tensor_tensor(hid[:, b, 0:FULL, :], hid[:, b, 0:FULL, :], y[:, 0:FULL, :], ALU.add).then_inc(step, 1)
                nc.vector.tensor_tensor(hid[0:TXT, b, FULL, :], hid[0:TXT, b, FULL, :], y[0:TXT, FULL, :], ALU.add).then_inc(step, 1)
                dve.wait_ge(step, 4 * b + 4)


def drive_block(g, u_all, vn_all, level):
    nc, hid, arg = g.nc, g.hid, g.arg
    ln = [[g.sem(f"h_{n}{k}") for n in ("stats", "moments", "rstd", "alone")] for k in range(2)]
    w_in, w_turned, w_ready, set_up = g.sem("h_w_in"), g.sem("h_w_turned"), g.sem("h_w_ready"), g.sem("h_set_up")
    normed, normed_again, turned, vT_ready = g.sem("h_normed"), g.sem("h_normed_again"), g.sem("h_turned"), g.sem("h_vT_ready")
    driven, relu_done, picked, summed, pe_alone = g.sem("h_driven"), g.sem("h_relu"), g.sem("h_picked"), g.sem("h_summed"), g.sem("h_pe_alone")
    with ExitStack() as c:
        sb = lambda n, s, d=F32: c.enter_context(nc.sbuf_tensor("h_" + n, s, d))
        ps = lambda n, s: c.enter_context(nc.psum_tensor("h_" + n, s, F32))
        st, mv, v = sb("st", [P, NT, 6]), sb("mv", [P, NT, 4]), sb("v", [P, NT, D])
        st2, mv2 = sb("st2", [P, NT, 6]), sb("mv2", [P, NT, 4])
        vT = sb("vT", [P, NT * P])
        dx, dxT = sb("dx", [P, 2, D]), sb("dxT", [P, 2, P])
        column = sb("column", [P, B, B])
        col = sb("col", [P, B])
        u = sb("u", [P, 2, SEQ])
        p_turn = ps("p_turn", [P, 2, 512])
        p_u = ps("p_u", [P, 3, 512])
        p_sum = ps("p_sum", [P, 3, 512])
        block = c.enter_context(nc.Block())

        @block.sync
        def _(sp):
            sp.dma_start(dx[:], arg["L1_attn_Dx"].rearrange("(a n) d -> n a d", a=2)).then_inc(w_in, 16)
            sp.dma_start(column[:], g.const["column"].to_broadcast([P, B, B])).then_inc(w_in, 16)

        @block.gpsimd
        def _(pool):
            nc.gpsimd.memset(vT[D:P, :], 0.0).then_inc(set_up, 1)
            pool.wait_ge(set_up, 1)
            nc.gpsimd.memset(dxT[D:P, :, :], 0.0).then_inc(set_up, 1)
            with pool.Fori(0, B) as b:
                layernorm_pool(g, pool, b, mv, ln[0])
                layernorm_pool(g, pool, b, mv2, ln[1])

        @block.tensor
        def _(pe):
            pe.wait_ge(w_in, 32)
            pe.wait_ge(set_up, 2)
            for a in range(2):
                last = nc.tensor.transpose(p_turn[0:D, a, 0:P], dx[:, a, :], g.eye[:])
            last.then_inc(w_turned, 1)
            pe.wait_ge(w_ready, 1)
            with pe.Fori(0, B) as b:
                wait_alone(pe, normed, NT * b + NT, pe_alone)
                for a in range(3):
                    wait_alone(pe, vT_ready, 3 * b + max(a - 1, 0), pe_alone)
                    for t in range(3 * a, 3 * a + 3):
                        last = nc.tensor.transpose(p_turn[0:D, a % 2, t % 3 * P:t % 3 * P + P], v[:, t, :], g.eye[:])
                    last.then_inc(turned, 1)
                pe.wait_ge(vT_ready, 3 * b + 3)
                for k in range(2 * NC):
                    f, a = divmod(k, NC)
                    pe.wait_ge(relu_done, 2 * NC * b + max(k - 2, 0))
                    nc.tensor.matmul(p_u[:, k % 3, 0:CH], dxT[:, f, :], vT[:, a * CH:a * CH + CH], start=True, stop=True)\
                        .then_inc(driven, 1)
                pe.wait_ge(relu_done, 2 * NC * b + 2 * NC)
                pe.wait_ge(picked, b + 1)
                for f in range(2):
                    for a in range(NC):
                        last = nc.tensor.matmul(p_sum[0:B, a, 0:CH], col[:, :], u[:, f, a * CH:a * CH + CH],
                                                start=(f == 0), stop=(f == 1), skip_group_check=True)
                last.then_inc(summed, 1)

        @block.scalar
        def _(act):
            with act.Fori(0, B) as b:
                for a in range(3):
                    act.wait_ge(turned, 3 * b + a + 1)
                    act.wait_ge(driven, 2 * NC * b)
                    nc.scalar.copy(vT[0:D, 3 * a * P:3 * a * P + 3 * P], p_turn[0:D, a % 2, 0:3 * P]).then_inc(vT_ready, 1)
                act.wait_ge(summed, b)
                for k in range(2 * NC):
                    f, a = divmod(k, NC)
                    act.wait_ge(driven, 2 * NC * b + k + 1)
                    nc.scalar.activation(u[:, f, a * CH:a * CH + CH], p_u[:, k % 3, 0:CH], ACT.Relu).then_inc(relu_done, 1)
                act.wait_ge(relu_done, 2 * NC * b + 2 * NC)
                nc.scalar.copy(u_all[:, b, :, :], u[:, :, :])

        @block.vector
        def _(dve):
            dve.wait_ge(w_turned, 1)
            dve.wait_ge(w_in, 32)
            nc.vector.tensor_copy(dxT[0:D, :, :], p_turn[0:D, :, 0:P]).then_inc(w_ready, 1)
            nc.vector.memset(level[:, :], 0.0)
            with dve.Fori(0, B) as b:
                dve.wait_ge(turned, 3 * b)
                layernorm_dve(nc, dve, b, lambda t: hid[:, b, t, :], lambda t: v[:, t, :], st, mv, ln[0], normed)
                dve.wait_ge(summed, b)
                nc.vector.tensor_copy(col[:, :], column[:, b, :]).then_inc(picked, 1)
                wait_alone(dve, normed, NT * b + NT, ln[0][3])
                layernorm_dve(nc, dve, b, lambda t: v[:, t, :], lambda t: vn_all[:, b, t, :], st2, mv2, ln[1], normed_again)
                dve.wait_ge(summed, b + 1)
                nc.vector.tensor_tensor(level[0:B, :].rearrange("p (a n) -> p a n", a=NC), level[0:B, :].rearrange("p (a n) -> p a n", a=NC),
                                        p_sum[0:B, :, 0:CH], ALU.add)
                dve.wait_ge(normed_again, NT * b + NT)


def level_block(g, level, rate):
    nc = g.nc
    done = g.sem("i_done")
    G = DECAY / L1_EPS
    with ExitStack() as c:
        sb = lambda n, s, d=F32: c.enter_context(nc.sbuf_tensor("i_" + n, s, d))
        small, scaled, total = sb("small", [B, SEQ]), sb("scaled", [B, SEQ]), sb("total", [B, SEQ + 1])
        block = c.enter_context(nc.Block())

        @block.vector
        def _(dve):
            U = level[0:B, :]
            nc.vector.tensor_scalar(scaled[:, :], U, 1.0 / L1_EPS, 1.0, ALU.mult, ALU.min).then_inc(done, 1)
            nc.vector.memset(total[:, 0:1], 0.0).then_inc(done, 1)
            dve.wait_ge(done, 2)
            nc.vector.tensor_scalar(small[:, :], scaled[:, :], 1.0, G, ALU.is_lt, ALU.mult).then_inc(done, 1)
            dve.wait_ge(done, 3)
            nc.vector.tensor_tensor_scan(total[:, 1:SEQ + 1], small[:, :], scaled[:, :], 0.0, ALU.mult, ALU.add).then_inc(done, 1)
            dve.wait_ge(done, 4)
            nc.vector.tensor_scalar(total[:, 1:SEQ + 1], total[:, 1:SEQ + 1], 1.0, None, ALU.min).then_inc(done, 1)
            dve.wait_ge(done, 5)
            nc.vector.scalar_tensor_tensor(scaled[:, :], total[:, 0:SEQ], DECAY, U, ALU.mult, ALU.add).then_inc(done, 1)
            dve.wait_ge(done, 6)
            nc.vector.tensor_scalar(scaled[:, :], scaled[:, :], L1_EPS, None, ALU.max).then_inc(done, 1)
            dve.wait_ge(done, 7)
            nc.vector.reciprocal(rate[:, :], scaled[:, :]).then_inc(done, 1)
            dve.wait_ge(done, 8)


def state_block(g, u_all, rate):
    nc = g.nc
    row_in, picked, spread, decayed, scaled, scanned, pe_alone = (g.sem("j_" + n) for n in
                                                        ("row_in", "picked", "spread", "decayed", "scaled", "scanned", "pe_alone"))
    with ExitStack() as c:
        sb = lambda n, s, d=F32: c.enter_context(nc.sbuf_tensor("j_" + n, s, d))
        rows = sb("rows", [B, B, P])
        row = sb("row", [B, 2, P])
        decay = sb("decay", [P, SEQ])
        ru = sb("ru", [P, 2, SEQ])
        p_r = c.enter_context(nc.psum_tensor("j_p_r", [P, 2, 4, 512], F32))
        block = c.enter_context(nc.Block())

        @block.sync
        def _(sp):
            sp.dma_start(rows[:], g.const["rows"]).then_inc(row_in, 16)

        @block.tensor
        def _(pe):
            with pe.Fori(0, B // 2) as i:
                for s in range(2):
                    b = 2 * i + s
                    wait_alone(pe, scaled, 4 * i, pe_alone)
                    wait_alone(pe, picked, b + 1, pe_alone)
                    for a in range(NC):
                        last = nc.tensor.matmul(p_r[:, s, a, 0:CH], row[:, s, :], rate[:, a * CH:a * CH + CH], start=True, stop=True)
                    last.then_inc(spread, 1)

        @block.scalar
        def _(act):
            with act.Fori(0, B // 2) as i:
                for s in range(2):
                    b = 2 * i + s
                    act.wait_ge(scaled, 2 * b + 2)
                    act.wait_ge(scanned, 2 * b)
                    nc.scalar.mul(decay[:, :].rearrange("p (a n) -> p a n", a=NC), p_r[:, s, 0:NC, 0:CH], DECAY).then_inc(decayed, 1)

        @block.vector
        def _(dve):
            dve.wait_ge(row_in, 16)
            with dve.Fori(0, B // 2) as i:
                for s in range(2):
                    b = 2 * i + s
                    dve.wait_ge(spread, 2 * i)
                    nc.vector.tensor_copy(row[:, s, :], rows[:, b, :]).then_inc(picked, 1)
                    dve.wait_ge(spread, b + 1)
                    dve.wait_ge(decayed, b)
                    for f in range(2):
                        nc.vector.tensor_tensor(ru[:, f, :].rearrange("p (a n) -> p a n", a=NC),
                                                u_all[:, b, f, :].rearrange("p (a n) -> p a n", a=NC),
                                                p_r[:, s, 0:NC, 0:CH], ALU.mult).then_inc(scaled, 1)
                    dve.wait_ge(scaled, 2 * b + 2)
                    dve.wait_ge(decayed, b + 1)
                    for f in range(2):
                        nc.vector.tensor_tensor_scan(u_all[:, b, f, :], decay[:, :], ru[:, f, :], 0.0, ALU.mult, ALU.add)\
                            .then_inc(scanned, 1)
                    dve.wait_ge(scanned, 2 * b + 2)


def pieces():
    out = []
    for lo in range(0, SEQ, 512):
        hi = min(lo + 512, SEQ)
        for s in range(NT):
            at = max(lo, s * P)
            if at < hi:
                out.append((s, at, hi - at))
    return out


def recall_block(g, x_all, vn_all, aT_all):
    nc = g.nc
    parts = pieces()
    NPC = len(parts)
    d_in, set_up = g.sem("k_d_in"), g.sem("k_set_up")
    x_ready, vn_ready = g.sem("k_x_ready"), g.sem("k_vn_ready")
    alike, masked, recalled, copied = g.sem("k_alike"), g.sem("k_masked"), g.sem("k_recalled"), g.sem("k_copied")
    R = 3
    assert NPC % R == 0
    with ExitStack() as c:
        sb = lambda n, s, d=F32: c.enter_context(nc.sbuf_tensor("k_" + n, s, d))
        ps = lambda n, s: c.enter_context(nc.psum_tensor("k_" + n, s, F32))
        x = sb("x", [P, 2, 2, SEQ])
        vn = sb("vn", [P, 2, NT, D])
        decay = sb("decay", [P, SEQ])
        pm = sb("pm", [P, R, 512])
        p_s = ps("p_s", [P, R, 512])
        p_a = ps("p_a", [D, 3, 512])
        block = c.enter_context(nc.Block())
        bank_end = [max(i for i, (_, at, n) in enumerate(parts) if at // 512 == k) for k in range(3)]

        @block.sync
        def _(sp):
            sp.dma_start(decay[:], g.const["decay"]).then_inc(d_in, 16)

        @block.gpsimd
        def _(pool):
            with pool.Fori(0, B // 2) as i:
                for s in range(2):
                    pool.wait_ge(recalled, NPC * 2 * i)
                    nc.gpsimd.tensor_copy(vn[:, s, :, :], vn_all[:, 2 * i + s, :, :]).then_inc(vn_ready, 1)

        @block.scalar
        def _(act):
            def load(b, s):
                nc.scalar.copy(x[:, s, :, :], x_all[:, b, :, :]).then_inc(x_ready, 1)

            def store(b, k):
                act.wait_ge(recalled, NPC * b + bank_end[k] + 1)
                n = min(512, SEQ - 512 * k)
                nc.scalar.copy(aT_all[0:D, b, 512 * k:512 * k + n], p_a[:, k, 0:n]).then_inc(copied, 1)

            load(0, 0)
            with act.Fori(0, B // 2 - 1) as i:
                for s in range(2):
                    b = 2 * i + s
                    act.wait_ge(recalled, NPC * b)
                    load(b + 1, 1 - s)
                    for k in range(3):
                        store(b, k)
            act.wait_ge(recalled, NPC * (B - 2))
            load(B - 1, 1)
            for b in (B - 2, B - 1):
                for k in range(3):
                    store(b, k)

        @block.vector
        def _(dve):
            dve.wait_ge(d_in, 16)
            with dve.Fori(0, B) as b:
                for k, (s, at, n) in enumerate(parts):
                    rows = min(P, SEQ - s * P)
                    dve.wait_ge(alike, NPC * b + k + 1)
                    dve.wait_ge(recalled, NPC * b + max(k - R + 1, 0))
                    nc.vector.tensor_tensor(pm[0:rows, k % R, 0:n], p_s[0:rows, k % R, 0:n],
                                            decay[0:rows, at - s * P:at - s * P + n], ALU.mult).then_inc(masked, 1)

        @block.tensor
        def _(pe):
            def score(b, slot, k):
                s, at, n = parts[k]
                rows = min(P, SEQ - s * P)
                pe.wait_ge(masked, NPC * b + max(k - R + 1, 0))
                for f in range(2):
                    last = nc.tensor.matmul(p_s[0:rows, k % R, 0:n], x[:, slot, f, s * P:s * P + rows],
                                            x[:, slot, f, at:at + n], start=(f == 0), stop=(f == 1))
                last.then_inc(alike, 1)

            def weigh(b, slot, k):
                s, at, n = parts[k]
                rows = min(P, SEQ - s * P)
                bank = at // 512
                if k in (0, bank_end[0] + 1, bank_end[1] + 1):
                    pe.wait_ge(copied, 3 * b)
                pe.wait_ge(masked, NPC * b + k + 1)
                nc.tensor.matmul(p_a[:, bank, at % 512:at % 512 + n], vn[0:rows, slot, s, :], pm[0:rows, k % R, 0:n],
                                 start=(s == 0), stop=(k == bank_end[bank]), skip_group_check=True).then_inc(recalled, 1)

            with pe.Fori(0, B // 2) as i:
                for slot in range(2):
                    b = 2 * i + slot
                    pe.wait_ge(x_ready, b + 1)
                    pe.wait_ge(vn_ready, b + 1)
                    score(b, slot, 0)
                    for k in range(NPC):
                        if k + 1 < NPC:
                            score(b, slot, k + 1)
                        weigh(b, slot, k)


def answer_block(g, x_all, aT_all):
    nc, hid, arg = g.nc, g.hid, g.arg
    ln = [[g.sem(f"l_{n}{k}") for n in ("stats", "moments", "rstd", "alone")] for k in range(2)]
    (w_in, w_turned, w_ready, set_up, aT_ready, a_turned, normed, la_turned, laT_ready, cored, gated, answered, normed2, added, pe_alone) = (
        g.sem("l_" + n) for n in ("w_in", "w_turned", "w_ready", "set_up", "aT_ready", "a_turned", "normed", "la_turned",
                                  "laT_ready", "cored", "gated", "answered", "normed2", "added", "pe_alone"))
    with ExitStack() as c:
        sb = lambda n, s, d=F32: c.enter_context(nc.sbuf_tensor("l_" + n, s, d))
        ps = lambda n, s: c.enter_context(nc.psum_tensor("l_" + n, s, F32))
        st, mv, la = sb("st", [P, NT, 6]), sb("mv", [P, NT, 4]), sb("la", [P, NT, D])
        st2, mv2, vs = sb("st2", [P, NT, 6]), sb("mv2", [P, NT, 4]), sb("vs", [P, NT, D])
        aT, laT, yT = sb("aT", [D, NT * P]), sb("laT", [P, NT * P]), sb("yT", [P, 2, NT * P])
        dy, dyT, e_raw, eT = sb("dy", [P, 2, D]), sb("dyT", [P, 2, P]), sb("e_raw", [D, NN]), sb("eT", [P, 2, D])
        p_a = ps("p_a", [P, 2, FULL, D])
        p_la = ps("p_la", [P, 1, 512])
        p_y = ps("p_y", [P, 3, 512])
        p_v = ps("p_v", [P, 2, FULL, D])
        block = c.enter_context(nc.Block())
        a_of = lambda t: p_a[:, t // FULL, t % FULL, :]
        v_of = lambda t: p_v[:, t // FULL, t % FULL, :]

        @block.sync
        def _(sp):
            sp.dma_start(dy[:], arg["L1_attn_Dy"].rearrange("(a n) d -> n a d", a=2)).then_inc(w_in, 16)
            sp.dma_start(e_raw[:], arg["L1_attn_E"]).then_inc(w_in, 16)

        @block.gpsimd
        def _(pool):
            for n, v in enumerate((laT[D:P, :], dyT[D:P, :, :], aT[:, SEQ:NT * P], yT[:, :, SEQ:NT * P])):
                if n:
                    pool.wait_ge(set_up, n)
                nc.gpsimd.memset(v, 0.0).then_inc(set_up, 1)
            with pool.Fori(0, B) as b:
                layernorm_pool(g, pool, b, mv, ln[0])
                layernorm_pool(g, pool, b, mv2, ln[1])

        @block.tensor
        def _(pe):
            pe.wait_ge(w_in, 32)
            pe.wait_ge(set_up, 4)
            for a in range(2):
                nc.tensor.transpose(p_y[0:D, a, 0:P], dy[:, a, :], g.eye[:])
                last = nc.tensor.transpose(p_y[:, 2, a * D:a * D + D], e_raw[:, a * P:a * P + P], g.eye[0:D, 0:D])
            last.then_inc(w_turned, 1)
            pe.wait_ge(w_ready, 2)
            with pe.Fori(0, B) as b:
                pe.wait_ge(aT_ready, b + 1)
                wait_alone(pe, normed, NT * b, pe_alone)
                for t in range(NT):
                    last = nc.tensor.transpose(a_of(t), aT[:, t * P:t * P + P], g.eye[0:D, 0:D])
                last.then_inc(a_turned, 1)
                wait_alone(pe, normed, NT * b + NT, pe_alone)
                for a in range(3):
                    wait_alone(pe, laT_ready, 3 * b + a, pe_alone)
                    for t in range(3 * a, 3 * a + 3):
                        last = nc.tensor.transpose(p_la[0:D, 0, t % 3 * P:t % 3 * P + P], la[:, t, :], g.eye[:])
                    last.then_inc(la_turned, 1)
                pe.wait_ge(laT_ready, 3 * b + 3)
                for k in range(2 * NC):
                    f, a = divmod(k, NC)
                    pe.wait_ge(gated, 2 * NC * b + max(k - 2, 0))
                    nc.tensor.matmul(p_y[:, k % 3, 0:CH], dyT[:, f, :], laT[:, a * CH:a * CH + CH], start=True, stop=True)\
                        .then_inc(cored, 1)
                pe.wait_ge(gated, 2 * NC * b + 2 * NC)
                wait_alone(pe, normed2, NT * b, pe_alone)
                for t in range(NT):
                    for f in range(2):
                        last = nc.tensor.matmul(v_of(t), yT[:, f, t * P:t * P + P], eT[:, f, :], start=(f == 0), stop=(f == 1))
                last.then_inc(answered, 1)

        @block.scalar
        def _(act):
            act.wait_ge(w_turned, 1)
            nc.scalar.copy(eT[:, :, :], p_y[:, 2, 0:2 * D].rearrange("p (a d) -> p a d", a=2)).then_inc(w_ready, 1)
            with act.Fori(0, B) as b:
                act.wait_ge(a_turned, b)
                nc.scalar.copy(aT[:, 0:SEQ], aT_all[0:D, b, :]).then_inc(aT_ready, 1)
                for a in range(3):
                    act.wait_ge(la_turned, 3 * b + a + 1)
                    act.wait_ge(cored, 2 * NC * b)
                    nc.scalar.copy(laT[0:D, 3 * a * P:3 * a * P + 3 * P], p_la[0:D, 0, 0:3 * P]).then_inc(laT_ready, 1)

        @block.vector
        def _(dve):
            dve.wait_ge(w_turned, 1)
            nc.vector.tensor_copy(dyT[0:D, :, :], p_y[0:D, 0:2, 0:P]).then_inc(w_ready, 1)
            with dve.Fori(0, B) as b:
                dve.wait_ge(a_turned, b + 1)
                dve.wait_ge(la_turned, 3 * b)
                layernorm_dve(nc, dve, b, a_of, lambda t: la[:, t, :], st, mv, ln[0], normed)
                for k in range(2 * NC):
                    f, a = divmod(k, NC)
                    cols = slice(a * CH, a * CH + CH)
                    dve.wait_ge(cored, 2 * NC * b + k + 1)
                    dve.wait_ge(answered, b)
                    nc.vector.scalar_tensor_tensor(yT[:, f, cols], p_y[:, k % 3, 0:CH], 0.0, x_all[:, b, f, cols],
                                                   ALU.max, ALU.mult).then_inc(gated, 1)
                dve.wait_ge(answered, b + 1)
                layernorm_dve(nc, dve, b, v_of, lambda t: vs[:, t, :], st2, mv2, ln[1], normed2)
                dve.wait_ge(normed2, NT * b + NT)
                nc.vector.tensor_tensor(hid[:, b, :, :], hid[:, b, :, :], vs[:, :, :], ALU.add).then_inc(added, 1)
                dve.wait_ge(added, b + 1)


def memory_stage(g):
    nc = g.nc
    with ExitStack() as c:
        sb = lambda n, s, d=F32: c.enter_context(nc.sbuf_tensor(n, s, d))
        x_all = sb("m_x_all", [P, B, 2, SEQ])
        with ExitStack() as c2:
            vn_all = c2.enter_context(nc.sbuf_tensor("m_vn_all", [P, B, NT, D], F32))
            with ExitStack() as c3:
                level = c3.enter_context(nc.sbuf_tensor("m_level", [B, SEQ], F32))
                rate = c3.enter_context(nc.sbuf_tensor("m_rate", [B, SEQ], F32))
                drive_block(g, x_all, vn_all, level)
                level_block(g, level, rate)
                state_block(g, x_all, rate)
            aT_all = c2.enter_context(nc.sbuf_tensor("m_aT_all", [D, B, SEQ], F32))
            recall_block(g, x_all, vn_all, aT_all)
            answer_block(g, x_all, aT_all)


def experts0_stage(g):
    nc, arg = g.nc, g.arg
    with ExitStack() as c:
        sb = lambda n, s, d=F32: c.enter_context(nc.sbuf_tensor(n, s, d))
        xn_all = sb("d_xn_all", [P, B, NT, D])
        with ExitStack() as c2:
            xT_all = c2.enter_context(nc.sbuf_tensor("d_xT_all", [P, B, SEQ], F32))
            cT_all = c2.enter_context(nc.sbuf_tensor("d_cT_all", [GK, B, SEQ], BF16))
            gate_block(g, "d_", 16, arg["L0_ffn_gate_w"], arg["L0_ffn_gate_b"], xn_all, xT_all, cT_all)
            experts_block(g, "e_", 16, 128, arg["L0_ffn_w1"], arg["L0_ffn_b1"], arg["L0_ffn_w2"], arg["L0_ffn_b2"],
                          False, xT_all, cT_all, xn_all, False)
        affine_block(g, "f_", xn_all, arg["L0_ffn_gamma"], arg["L0_ffn_beta"])


def experts1_stage(g):
    nc, arg = g.nc, g.arg
    with ExitStack() as c:
        xT_all = c.enter_context(nc.sbuf_tensor("n_xT_all", [P, B, SEQ], F32))
        cT_all = c.enter_context(nc.sbuf_tensor("n_cT_all", [GK, B, SEQ], BF16))
        gate_block(g, "n_", 8, arg["L1_ffn_Wg"].rearrange("e d -> d e"), arg["L1_ffn_bg"], None, xT_all, cT_all)
        experts_block(g, "o_", 8, 256, arg["L1_ffn_W1"], arg["L1_ffn_b1"], arg["L1_ffn_W2"], arg["L1_ffn_b2"],
                      True, xT_all, cT_all, g.hid, True)


def build(nc, arg, const, out, stages):
    with ExitStack() as ctx:
        g = Program(nc, ctx, arg, const, out)
        for stage in stages:
            stage(g)
            if stage in (attend_stage, experts0_stage):
                g.free_sems()
        g.sem_ctx.close()


STAGES = [tokens_stage, project_stage, attend_stage, join_stage, experts0_stage, memory_stage, experts1_stage]
_INS = ["x", "txt", "L0_tok_W", "L0_attn_w_qkv", "L0_attn_b_qkv", "L0_attn_w_out", "L0_attn_b_out",
        "L0_ffn_gate_w", "L0_ffn_gate_b", "L0_ffn_w1", "L0_ffn_b1", "L0_ffn_w2", "L0_ffn_b2", "L0_ffn_gamma",
        "L0_ffn_beta", "L1_attn_E", "L1_attn_Dx", "L1_attn_Dy", "L1_ffn_Wg", "L1_ffn_bg", "L1_ffn_W1",
        "L1_ffn_b1", "L1_ffn_W2", "L1_ffn_b2"]


def kernel(**inputs):
    import concourse.bacc as _bacc
    from concourse.bass_utils import run_bass_kernel_spmd as _run

    nc = _bacc.Bacc("TRN2", target_bir_lowering=False, num_devices=1)
    arrays, arg, const = {}, {}, {}
    for name in _INS:
        a = np.ascontiguousarray(inputs[name])
        arrays[f"in_{name}"] = a
        arg[name] = nc.dram_tensor(f"in_{name}", a.shape, mybir.dt.from_np(a.dtype), kind="ExternalInput").ap()
    for name, a in shape_constants().items():
        arrays[f"const_{name}"] = a
        const[name] = nc.dram_tensor(f"const_{name}", a.shape, mybir.dt.from_np(a.dtype), kind="ExternalInput").ap()
    out = nc.dram_tensor("out", (B, SEQ, D), F32, kind="ExternalOutput").ap()
    build(nc, arg, const, out, STAGES)
    r = _run(nc, [arrays], core_ids=[0])
    return np.asarray(r.results[0]["out"])
```

```python
from contextlib import ExitStack

import numpy as np

import concourse.bass as bass
from concourse import mybir
from concourse.alu_op_type import AluOpType as ALU

F32 = mybir.dt.float32
BF16 = mybir.dt.bfloat16
U32 = mybir.dt.uint32
ACT = mybir.ActivationFunctionType
AX = mybir.AxisListType

P = 128
B, C, T, V, D = 8, 64, 128, 64, 64
STRIDE, PATCH = 8, 16
WIN = T // STRIDE
TXT = 32
TOK = V * WIN
SEQ = TOK + TXT
NT = -(-SEQ // P)
FULL = SEQ // P
CH = SEQ // 3
NC = SEQ // CH
HEADS, DH = 8, 8
QUAD = 4
HG = HEADS // QUAD
PARTS = 3
KS = PARTS * PARTS * DH
KPAD = 96
KMAX = KPAD + PARTS
LN_EPS = 1e-5
DECAY = 0.97
NN = 256
L1_EPS = 1e-12
EINS = 16
PAIRS = [(0, 0), (0, 1), (1, 0), (0, 2), (2, 0), (1, 1)]
GK = len(PAIRS) * EINS


def shape_constants():
    f = np.arange(PATCH // 2 + 1)[:, None]
    t = np.arange(PATCH)[None, :]
    turn = (f * t) % PATCH
    cos, sin = np.cos(2 * np.pi * turn / PATCH) / 4, -np.sin(2 * np.pi * turn / PATCH) / 4
    sin[(2 * turn) % PATCH == 0] = 0
    dft = np.concatenate([cos, sin])
    dft = dft.reshape(-1, 2, 2, 4).transpose(0, 2, 1, 3)
    p, x = np.arange(P)[:, None], np.arange(SEQ)[None, :]
    lag = x - 1 - p
    decay = np.where(lag >= 0, DECAY ** np.maximum(lag, 0).astype(np.float64), 0.0)
    first = [PAIRS.index((0, 0)), PAIRS.index((1, 0)), PAIRS.index((2, 0))]
    pick = np.zeros((GK, EINS, P))
    for e in range(EINS):
        for k in first:
            pick[k * EINS + e, e, :] = 1
    part_of = np.repeat(np.eye(PARTS)[[bi for _, bi in PAIRS]], EINS, axis=0)
    return {
        "dft": dft.reshape(18, 16).astype(np.float32),
        "eye": np.eye(P, dtype=np.float32),
        "decay": decay.astype(np.float32),
        "part_of": part_of.astype(np.float32),
        "column": np.eye(B, dtype=np.float32)[None],
        "rows": np.repeat(np.eye(B, dtype=np.float32)[:, :, None], P, axis=2),
        "number": np.arange(EINS, dtype=np.float32)[None, :],
        "pick": pick.astype(np.float32),
    }


class Program:

    def __init__(self, nc, ctx, arg, const, out):
        self.nc, self.ctx, self.arg, self.const, self.out = nc, ctx, arg, const, out
        self.hid = ctx.enter_context(nc.sbuf_tensor("hid", [P, B, NT, D], F32))
        self.eye = ctx.enter_context(nc.sbuf_tensor("eye", [P, P], F32))
        self.eye_bf = ctx.enter_context(nc.sbuf_tensor("eye_bf", [P, P], BF16))
        self.eps = ctx.enter_context(nc.sbuf_tensor("eps", [P, NT], F32))
        self.minus_half = ctx.enter_context(nc.sbuf_tensor("minus_half", [P, NT], F32))

        self.qk_scr = nc.dram_tensor("qk_scr", (B, 2, HEADS, PARTS, DH, SEQ), BF16, kind="Internal").ap()
        self.v_scr = nc.dram_tensor("v_scr", (B, P, NT * HEADS * 32), F32, kind="Internal").ap()
        self.sum_scr = nc.dram_tensor("sum_scr", (B, P, HG * SEQ), F32, kind="Internal").ap()
        self.max_scr = nc.dram_tensor("max_scr", (B, PARTS, HEADS * FULL + HG, P), BF16, kind="Internal").ap()

        self.sems, self.sem_ctx = [], ExitStack()

    def sem(self, name):
        self.sems.append(self.sem_ctx.enter_context(self.nc.semaphore(name)))
        return self.sems[-1]

    def software_dma_sem(self, name):
        return self.ctx.enter_context(self.nc.semaphore(name))

    def free_sems(self):
        with self.nc.Block() as block:
            @block.gpsimd
            def _(pool):
                for sem in self.sems:
                    pool.sem_clear(sem)
        self.sem_ctx.close()
        self.sems = []


def tokens_stage(g):
    nc, arg, hid = g.nc, g.arg, g.hid
    x, W = arg["x"], arg["L0_tok_W"]
    consts_in, w_in, txt_in = g.sem("consts_in"), g.sem("w_in"), g.software_dma_sem("txt_in")
    fold_done, fold_copied = g.sem("fold_done"), g.sem("fold_copied")
    x_in = [g.sem(f"x_in{s}") for s in range(2)]
    x_used = [g.sem(f"x_used{s}") for s in range(2)]
    projected, evacuated = g.sem("projected"), g.sem("evacuated")
    turned, stored, zeroed, eye_ready = g.sem("turned"), g.sem("stored"), g.sem("zeroed"), g.sem("eye_ready")
    NR = 2 * (PATCH // 2 + 1)
    with ExitStack() as c:
        sb = lambda n, s, d=F32: c.enter_context(nc.sbuf_tensor(n, s, d))
        dft = sb("dft", [NR, 16])
        w_raw = sb("w_raw", [NR, D, C])
        w_fold = sb("w_fold", [P, 4, 2, D])
        xt = [sb(f"xt{s}", [P, WIN + 1, 4, V]) for s in range(2)]
        tokT = sb("tokT", [P, 512])
        p_fold = c.enter_context(nc.psum_tensor("p_fold", [P, 512], F32))
        p_tok = c.enter_context(nc.psum_tensor("p_tok", [P, 512], F32))
        p_turn = c.enter_context(nc.psum_tensor("p_turn", [P, 4, 2, D], F32))
        block = c.enter_context(nc.Block())

        @block.sync
        def _(sp):
            sp.dma_start(dft[:], g.const["dft"]).then_inc(consts_in, 16)
            sp.dma_start(w_raw[:], W.rearrange("o (r c) -> r o c", c=C)).then_inc(w_in, 16)
            sp.dma_start(g.eye[:], g.const["eye"]).then_inc(consts_in, 16)
            with sp.Fori(0, B // 2) as i:
                for s in range(2):
                    sp.wait_ge(x_used[s], i)
                    for par in range(2):
                        rows = slice(par * C, par * C + C)
                        src = x[2 * i + s, :, :, :].rearrange("c (n q j) v -> q c n (j v)", q=2, j=4)
                        sp.dma_start(xt[s][rows, 0:WIN, :, :].rearrange("p n j v -> p n (j v)"),
                                     src[par, :, :, :]).then_inc(x_in[s], 16)
                        sp.dma_start(xt[s][rows, WIN, :, :],
                                     x[2 * i + s, :, T - 1:T, :].to_broadcast([C, 4, V])).then_inc(x_in[s], 16)

        @block.gpsimd
        def _(pool):
            pool.wait_ge(zeroed, 1)
            pool.dma_start(hid[0:TXT, :, FULL, :], arg["txt"].rearrange("b t d -> t b d")).then_inc(txt_in, 16)
            pool.wait_ge(txt_in, 16)

        @block.tensor
        def _(pe):
            pe.wait_ge(consts_in, 32)
            pe.wait_ge(w_in, 16)
            for par in range(2):
                for o in range(D):
                    last = nc.tensor.matmul(p_fold[par * C:par * C + C, o * 8:o * 8 + 8], w_raw[:, o, :],
                                            dft[:, par * 8:par * 8 + 8], start=True, stop=True)
            last.then_inc(fold_done, 1)
            pe.wait_ge(fold_copied, 1)
            with pe.Fori(0, B // 2) as i:
                for s in range(2):
                    pe.wait_ge(x_in[s], 64 * i + 64)
                    pe.wait_ge(evacuated, 2 * i + s)
                    for k in range(8):
                        for half in range(2):
                            col = xt[s][:, k // 4:k // 4 + WIN, k % 4, half * 32:half * 32 + 32]
                            last = nc.tensor.matmul(p_tok[half * D:half * D + D, :], w_fold[:, k % 4, k // 4, :],
                                                    col.rearrange("p n v -> p v n"), start=(k == 0), stop=(k == 7),
                                                    skip_group_check=True)
                    last.then_inc(projected, 1)
                    pe.wait_ge(evacuated, 2 * i + s + 1)
                    pe.wait_ge(stored, 2 * i + s)
                    for q in range(4):
                        last = nc.tensor.transpose(p_turn[:, q, :, :].rearrange("p a d -> p (a d)"),
                                                   tokT[:, q * P:q * P + P], g.eye[:])
                    last.then_inc(turned, 1)

        @block.vector
        def _(dve):
            nc.vector.memset(hid[:, :, FULL, :], 0.0).then_inc(zeroed, 1)
            nc.vector.memset(g.minus_half[:], -0.5)
            nc.vector.memset(g.eps[:], LN_EPS)
            dve.wait_ge(consts_in, 32)
            nc.vector.tensor_copy(g.eye_bf[:], g.eye[:]).then_inc(eye_ready, 1)
            dve.wait_ge(fold_done, 1)
            nc.vector.tensor_copy(w_fold[:].rearrange("p j s o -> p o s j"),
                                  p_fold[:, :].rearrange("p (o s j) -> p o s j", s=2, j=4)).then_inc(fold_copied, 1)
            with dve.Fori(0, B) as b:
                dve.wait_ge(turned, b + 1)
                nc.vector.tensor_copy(hid[:, b, 0:FULL, :].rearrange("p (h q) d -> p q h d", h=2),
                                      p_turn[:, :, :, :]).then_inc(stored, 1)

        @block.scalar
        def _(act):
            with act.Fori(0, B // 2) as i:
                for s in range(2):
                    act.wait_ge(projected, 2 * i + s + 1)
                    act.wait_ge(turned, 2 * i + s)
                    nc.scalar.copy(tokT[:, :], p_tok[:, :]).then_inc(evacuated, 1)
                    act.sem_inc(x_used[s], 1)


def wait_alone(engine, sem, value, alone):
    engine.wait_ge(sem, value)
    engine.sem_inc(alone, 1)


def layernorm_stats(nc, dve, n, src, st, mv, sems):
    stats_done, moments_done, rstd_done, alone = sems
    for t in range(NT):
        nc.vector.bn_stats(st[:, t, :], src(t)).then_inc(stats_done, 1)
    wait_alone(dve, stats_done, NT * (n + 1), alone)
    for t in range(NT):
        nc.vector.bn_aggr(mv[:, t, 0:2], st[:, t, :]).then_inc(moments_done, 1)


def layernorm_apply(nc, dve, n, src, dst, mv, sems, rows_done, twice=False):
    dve.wait_ge(sems[2], 2 * n + 2)
    for t in range(NT):
        rows = src(t) if not twice else src(t).unsqueeze(1).to_broadcast([P, 2, D])
        nc.vector.tensor_scalar(dst(t), rows, mv[:, t, 0:1], mv[:, t, 2:3], ALU.subtract, ALU.mult)\
            .then_inc(rows_done, 1)


def layernorm_dve(nc, dve, n, src, dst, st, mv, sems, rows_done):
    layernorm_stats(nc, dve, n, src, st, mv, sems)
    layernorm_apply(nc, dve, n, src, dst, mv, sems, rows_done)


def layernorm_pool(g, pool, n, mv, sems):
    nc = g.nc
    stats_done, moments_done, rstd_done, alone = sems
    pool.wait_ge(moments_done, NT * (n + 1))
    nc.gpsimd.tensor_tensor(mv[:, :, 3], mv[:, :, 1], g.eps[:, :], ALU.add).then_inc(rstd_done, 1)
    pool.wait_ge(rstd_done, 2 * n + 1)
    nc.gpsimd.tensor_tensor(mv[:, :, 2], mv[:, :, 3], g.minus_half[:, :], ALU.pow).then_inc(rstd_done, 1)


def project_stage(g):
    nc, arg, hid = g.nc, g.arg, g.hid
    ln = [g.sem(n) for n in ("a_stats", "a_moments", "a_rstd", "a_alone")]
    w_in, set_up, w_ready = g.sem("a_w_in"), g.sem("a_set_up"), g.sem("a_w_ready")
    normed, turned, xT_ready = g.sem("a_normed"), g.sem("a_turned"), g.sem("a_xT_ready")
    qk_done, v_done, v_copied = g.sem("a_qk_done"), g.sem("a_v_done"), g.sem("a_v_copied")
    part = [g.sem(f"a_part{i}") for i in range(PARTS)]
    rest, pe_alone = g.sem("a_rest"), g.sem("a_pe_alone")
    parts_sent, v_sent = g.sem("a_parts_sent"), g.sem("a_v_sent")
    with ExitStack() as c:
        sb = lambda n, s, d=F32: c.enter_context(nc.sbuf_tensor(n, s, d))
        ps = lambda n, s: c.enter_context(nc.psum_tensor(n, s, F32))
        st, mv = sb("a_st", [P, NT, 6]), sb("a_mv", [P, NT, 4])
        xn = sb("a_xn", [P, NT, D])
        xT = sb("a_xT", [P, NT * P])
        w_qkv = sb("a_w_qkv", [P, 3 * D])
        qk_part = [sb(f"a_qk_part{i}", [P, SEQ], BF16) for i in range(PARTS)]
        qk_rest = sb("a_qk_rest", [P, SEQ])
        vw = sb("a_vw", [P, NT, HEADS, 32])
        p_turn = ps("a_p_turn", [P, 3, 512])
        p_qk = ps("a_p_qk", [P, 3, 512])
        p_v = ps("a_p_v", [P, 2, 512])
        block = c.enter_context(nc.Block())
        xT_flat = p_turn[0:D, :, 0:3 * P]

        @block.sync
        def _(sp):
            sp.wait_ge(set_up, 2)
            sp.dma_start(w_qkv[0:D, :], arg["L0_attn_w_qkv"]).then_inc(w_in, 16)
            sp.dma_start(w_qkv[D:D + 1, :], arg["L0_attn_b_qkv"].rearrange("(a n) -> a n", a=1)).then_inc(w_in, 16)
            with sp.Fori(0, B) as b:
                for i in range(PARTS):
                    sp.wait_ge(part[i], b + 1)
                    sp.dma_start(g.qk_scr[b, :, :, i, :, :].rearrange("a h d t -> (a h) d t"), qk_part[i][:, :]).then_inc(parts_sent, 16)
                sp.wait_ge(v_copied, (QUAD + 1) * (b + 1))
                sp.dma_start(g.v_scr[b, :, :], vw[:].rearrange("p t h d -> p (t h d)")).then_inc(v_sent, 16)
            sp.wait_ge(parts_sent, 16 * PARTS * B)
            sp.wait_ge(v_sent, 16 * B)

        @block.gpsimd
        def _(pool):
            nc.gpsimd.memset(w_qkv[D:P, :], 0.0).then_inc(set_up, 1)
            nc.gpsimd.memset(xT[D:P, :], 0.0).then_inc(set_up, 1)
            pool.wait_ge(set_up, 2)
            nc.gpsimd.memset(xT[D:D + 1, :], 1.0).then_inc(set_up, 1)
            pool.wait_ge(set_up, 3)
            nc.gpsimd.memset(vw[:], 0.0).then_inc(set_up, 1)
            pool.wait_ge(set_up, 4)
            nc.gpsimd.memset(vw[:, 0:FULL, :, DH:DH + 1], 1.0).then_inc(set_up, 1)
            for h in range(HEADS):
                r = 32 * (h % QUAD)
                pool.wait_ge(set_up, 5 + h)
                nc.gpsimd.memset(vw[r:r + 32, FULL, h, DH:DH + 1], 1.0).then_inc(set_up, 1)
            with pool.Fori(0, B) as b:
                layernorm_pool(g, pool, b, mv, ln)

        @block.vector
        def _(dve):
            dve.wait_ge(set_up, 5 + HEADS)

            def stats(b):
                layernorm_stats(nc, dve, b, lambda t: hid[:, b, t, :], st, mv, ln)

            def norm(b):
                dve.wait_ge(turned, b)
                layernorm_apply(nc, dve, b, lambda t: hid[:, b, t, :], lambda t: xn[:, t, :], mv, ln, normed)

            def parts_and_v(b):
                dve.wait_ge(part[0], b + 1)
                dve.wait_ge(part[2], b)
                nc.vector.tensor_tensor(qk_rest[:, :].rearrange("p (a n) -> p a n", a=NC), p_qk[:, :, 0:CH],
                                        qk_part[0][:, :].rearrange("p (a n) -> p a n", a=NC), ALU.subtract).then_inc(rest, 1)
                dve.wait_ge(v_done, b + 1)
                dve.wait_ge(v_sent, 16 * b)
                nc.vector.tensor_copy(vw[:, 0:FULL, :, 0:DH].rearrange("p t h d -> p (t h) d"),
                                      p_v[:, 0, :].rearrange("p (t h d) -> p (t h) d", h=HEADS, d=DH)).then_inc(v_copied, 1)
                for q in range(QUAD):
                    r = slice(32 * q, 32 * q + 32)
                    nc.vector.tensor_copy(vw[r, FULL, :, 0:DH].rearrange("p (a q) d -> p a q d", q=QUAD)[:, :, q, :],
                                          p_v[r, 1, 0:D].rearrange("p (a q d) -> p a q d", q=QUAD, d=DH)[:, :, q, :])\
                        .then_inc(v_copied, 1)
                dve.wait_ge(parts_sent, 16 * PARTS * b)
                dve.wait_ge(part[1], b + 1)
                nc.vector.tensor_tensor(qk_part[2][:, :], qk_rest[:, :], qk_part[1][:, :], ALU.subtract).then_inc(part[2], 1)

            stats(0)
            norm(0)
            with dve.Fori(0, B - 1) as b:
                stats(b + 1)
                norm(b + 1)
                parts_and_v(b)
            parts_and_v(B - 1)

        @block.scalar
        def _(act):
            with act.Fori(0, B) as b:
                act.wait_ge(turned, b + 1)
                act.wait_ge(v_done, b)
                nc.scalar.copy(xT[0:D, :].rearrange("p (a n) -> p a n", a=3), xT_flat).then_inc(xT_ready, 1)
                act.wait_ge(qk_done, b + 1)
                act.wait_ge(parts_sent, 16 * PARTS * b)
                nc.scalar.copy(qk_part[0][:, :].rearrange("p (a n) -> p a n", a=NC), p_qk[:, :, 0:CH]).then_inc(part[0], 1)
                act.wait_ge(rest, b + 1)
                nc.scalar.copy(qk_part[1][:, :], qk_rest[:, :]).then_inc(part[1], 1)

        @block.tensor
        def _(pe):
            pe.wait_ge(w_in, 32)
            with pe.Fori(0, B) as b:
                pe.wait_ge(xT_ready, b)
                for t in range(NT):
                    wait_alone(pe, normed, NT * b + t + 1, pe_alone)
                    last = nc.tensor.transpose(p_turn[0:D, t // 3, (t % 3) * P:(t % 3) * P + P], xn[:, t, :], g.eye[:])
                last.then_inc(turned, 1)
                pe.wait_ge(xT_ready, b + 1)
                pe.wait_ge(rest, b)
                for a in range(NC):
                    last = nc.tensor.matmul(p_qk[:, a, 0:CH], w_qkv[:, 0:2 * D], xT[:, a * CH:a * CH + CH],
                                            start=True, stop=True)
                last.then_inc(qk_done, 1)
                pe.wait_ge(v_copied, (QUAD + 1) * b)
                for t in range(FULL):
                    nc.tensor.matmul(p_v[:, 0, t * D:t * D + D], xT[:, t * P:t * P + P], w_qkv[:, 2 * D:3 * D],
                                     start=True, stop=True)
                for q in range(QUAD):
                    last = nc.tensor.matmul(p_v[32 * q:32 * q + 32, 1, 0:D], xT[:, TOK:SEQ], w_qkv[:, 2 * D:3 * D],
                                            start=True, stop=True)
                last.then_inc(v_done, 1)


def attend_stage(g):
    nc = g.nc
    NSUM = HG * NC
    UNITS = FULL * 2 + 1
    NU = NSUM * UNITS
    chunks = [(hq, t, a) for quad in range(HG)
              for hq, t in [(quad * QUAD + q, t) for q in range(QUAD) for t in range(FULL)] + [(quad, FULL)]
              for a in range(NC)]
    NCH = len(chunks)
    MROWS = HEADS * FULL + HG
    GROUPS = [[n * UNITS + 2 * j, n * UNITS + 2 * j + 1] if j < FULL else [n * UNITS + 2 * j]
              for n in range(NSUM) for j in range(FULL + 1)]
    ERING = 6
    assert NU % ERING == 0
    half_in = [[g.sem(f"b_half_in{s}{q}") for q in range(HG)] for s in range(2)]
    v_in = [g.sem(f"b_v_in{s}") for s in range(2)]
    set_up, max_in = [g.sem(f"b_set_up{s}") for s in range(2)], [g.software_dma_sem(f"b_max_in{s}") for s in range(2)]
    rows_done, rows_reduced = g.sem("b_rows_done"), g.sem("b_rows_reduced")
    max_step, max_turned, max_copied, max_sent = g.sem("b_max_step"), g.sem("b_max_turned"), g.sem("b_max_copied"), g.software_dma_sem("b_max_sent")
    scored, exp_done, pv_done = g.sem("b_scored"), g.sem("b_exp_done"), g.sem("b_pv_done")
    sum_copied, sum_sent = g.sem("b_sum_copied"), [g.software_dma_sem(f"b_sum_sent{n}") for n in range(2)]
    pool_alone = g.sem("b_pool_alone")
    with ExitStack() as c:
        sb = lambda n, s, d=F32: c.enter_context(nc.sbuf_tensor(n, s, d))
        ps = lambda n, s: c.enter_context(nc.psum_tensor(n, s, F32))
        q_st = [sb(f"b_q{s}", [P, HEADS, SEQ], BF16) for s in range(2)]
        k_st = [sb(f"b_k{s}", [P, HEADS, SEQ], BF16) for s in range(2)]
        vw = [sb(f"b_v{s}", [P, NT, HEADS, 32]) for s in range(2)]
        prob = sb("b_prob", [P, ERING, 2, CH])
        sums = sb("b_sums", [P, 2, CH])
        m3 = sb("b_m3", [P, MROWS, NC])
        neg_max = sb("b_neg_max", [P, MROWS])
        max_rest = sb("b_max_rest", [P, MROWS])
        max_part = sb("b_max_part", [P, PARTS, MROWS], BF16)
        max_row = sb("b_max_row", [MROWS, PARTS, P], BF16)
        p_s = ps("b_p_s", [P, 2, 2, 512])
        p_m = ps("b_p_m", [P, 3, 512])
        p_o = ps("b_p_o", [P, 512])
        p_turn = p_m[0:MROWS, 0, :].bitcast(BF16)
        block = c.enter_context(nc.Block())

        def pad_rows(do, engine, s):
            flat = lambda st, lo, hi: st[s][lo:hi, :, :].rearrange("p h t -> p (h t)").bitcast(U32)
            for n, (rows, value) in enumerate(((flat(q_st, 64, KPAD), 0), (flat(k_st, 64, KPAD), 0), (flat(k_st, KPAD, P), 0x3F803F80))):
                if n:
                    engine.wait_ge(set_up[s], n)
                do.memset(rows, value).then_inc(set_up[s], 1)

        def load_half(sp, b, s, quad):
            heads = slice(quad * QUAD, quad * QUAD + QUAD)
            for kb in range(PARTS):
                sp.dma_start(q_st[s][kb * 24:kb * 24 + 24, heads, :],
                             g.qk_scr[b, 0, heads, :, :, :].rearrange("h a d t -> (a d) h t"))\
                    .then_inc(half_in[s][quad], 16)
                for qa in range(PARTS):
                    r = kb * 24 + qa * DH
                    sp.dma_start(k_st[s][r:r + DH, heads, :],
                                 g.qk_scr[b, 1, heads, kb, :, :].rearrange("h d t -> d h t"))\
                        .then_inc(half_in[s][quad], 16)

        HALF_IN = 16 * (PARTS + PARTS * PARTS)

        @block.sync
        def _(sp):
            for s in range(2):
                sp.wait_ge(set_up[s], 3)
                for quad in range(HG):
                    load_half(sp, s, s, quad)
                sp.dma_start(vw[s][:].rearrange("p t h d -> p (t h d)"), g.v_scr[s, :, :]).then_inc(v_in[s], 16)
            with sp.Fori(0, B // 2 - 1) as i:
                for s in range(2):
                    for quad in range(HG):
                        sp.wait_ge(pv_done, NU * (2 * i + s) + NC * UNITS * (quad + 1))
                        load_half(sp, 2 * i + s + 2, s, quad)
                    sp.dma_start(vw[s][:].rearrange("p t h d -> p (t h d)"), g.v_scr[2 * i + s + 2, :, :])\
                        .then_inc(v_in[s], 16)

        @block.gpsimd
        def _(pool):
            pad_rows(nc.gpsimd, pool, 1)

            def send_max(b, s):
                wait_alone(pool, max_copied, b + 1, pool_alone)
                pool.dma_start(g.max_scr[b, :, :, :].rearrange("a r i -> r a i"), max_row[:, :, :]).then_inc(max_sent, 16)
                wait_alone(pool, max_sent, 16 * b + 16, pool_alone)
                for a in range(PARTS):
                    pool.dma_start(q_st[s][KPAD + a:KPAD + a + 1, :, 0:TOK],
                                   g.max_scr[b, a:a + 1, 0:HEADS * FULL, :].rearrange("a (h t) i -> a h (t i)", t=FULL))\
                        .then_inc(max_in[s], 16)
                for quad in range(HG):
                    pool.dma_start(q_st[s][KPAD:KMAX, quad * QUAD:quad * QUAD + QUAD, TOK:SEQ],
                                   g.max_scr[b, :, HEADS * FULL + quad, :].rearrange("a (q i) -> a q i", q=QUAD))\
                        .then_inc(max_in[s], 16)

            def send_sums(b, n):
                quad, a = divmod(n, NC)
                wait_alone(pool, sum_copied, NSUM * b + n + 1, pool_alone)
                pool.dma_start(g.sum_scr[b, :, quad * SEQ + a * CH:quad * SEQ + a * CH + CH], sums[:, n % 2, :])\
                    .then_inc(sum_sent[n % 2], 16)

            def step(b, s, with_max):
                for n in range(NSUM - 1):
                    send_sums(b, n)
                if with_max:
                    send_max(b + 1, 1 - s)
                send_sums(b, NSUM - 1)

            send_max(0, 0)
            with pool.Fori(0, B // 2 - 1) as i:
                for s in range(2):
                    step(2 * i + s, s, True)
            step(B - 2, 0, True)
            step(B - 1, 1, False)
            for n in range(2):
                pool.wait_ge(sum_sent[n], 16 * NSUM // 2 * B)

        MAX_IN = 16 * (PARTS + HG)

        @block.scalar
        def _(act):
            def copy_sums(b, n):
                act.wait_ge(pv_done, NU * b + UNITS * (n + 1))
                act.wait_ge(sum_sent[n % 2], 16 * (NSUM // 2 * b + n // 2))
                nc.scalar.copy(sums[:, n % 2, :], p_o[:, 0:CH]).then_inc(sum_copied, 1)

            def step(b):
                for u in range(NU):
                    act.wait_ge(scored, NU * b + u + 1)
                    act.wait_ge(pv_done, NU * b + max(u - ERING + 1, 0))
                    heads = 2 if u % UNITS < UNITS - 1 else 1
                    nc.scalar.activation(prob[:, u % ERING, 0:heads, :], p_s[:, u % 2, 0:heads, 0:CH], ACT.Exp,
                                         scale=float(D) ** -0.5).then_inc(exp_done, 1)
                    if u % UNITS == 1 and u > UNITS:
                        copy_sums(b, u // UNITS - 1)
                copy_sums(b, NSUM - 1)

            with act.Fori(0, B) as b:
                step(b)

        @block.vector
        def _(dve):
            def maxima(b):
                for k, (hq, t, a) in enumerate(chunks):
                    row = hq * FULL + t if t < FULL else HEADS * FULL + hq
                    dve.wait_ge(rows_done, NCH * b + k + 1)
                    nc.vector.tensor_reduce(m3[:, row, a:a + 1], p_m[:, k % 3, 0:CH], axis=AX.X, op=ALU.max)\
                        .then_inc(rows_reduced, 1)
                dve.wait_ge(rows_reduced, NCH * b + NCH)
                nc.vector.tensor_reduce(neg_max[:, :], m3[:, :, :], axis=AX.X, op=ALU.max, negate=True).then_inc(max_step, 1)
                dve.wait_ge(max_step, 6 * b + 1)
                nc.vector.tensor_copy(max_part[:, 0, :], neg_max[:, :]).then_inc(max_step, 1)
                dve.wait_ge(max_step, 6 * b + 2)
                nc.vector.tensor_tensor(max_rest[:, :], neg_max[:, :], max_part[:, 0, :], ALU.subtract).then_inc(max_step, 1)
                dve.wait_ge(max_step, 6 * b + 3)
                nc.vector.tensor_copy(max_part[:, 1, :], max_rest[:, :]).then_inc(max_step, 1)
                dve.wait_ge(max_step, 6 * b + 4)
                nc.vector.tensor_tensor(max_part[:, 2, :], max_rest[:, :], max_part[:, 1, :], ALU.subtract).then_inc(max_step, 2)
                dve.wait_ge(max_turned, b + 1)
                dve.wait_ge(max_sent, 16 * b)
                nc.vector.tensor_copy(max_row[:, :, :].rearrange("r a i -> r (a i)"), p_turn[:, 0:PARTS * P])\
                    .then_inc(max_copied, 1)

            pad_rows(nc.vector, dve, 0)
            with dve.Fori(0, B) as b:
                maxima(b)

        @block.tensor
        def _(pe):
            def row_chunk(b, s, k):
                hq, t, a = chunks[k]
                if k == 0:
                    pe.wait_ge(max_copied, b)
                pe.wait_ge(rows_reduced, NCH * b + max(k - 2, 0))
                cols = slice(a * CH, a * CH + CH)
                if t < FULL:
                    last = nc.tensor.matmul(p_m[:, k % 3, 0:CH], q_st[s][0:KPAD, hq, t * P:t * P + P],
                                            k_st[s][0:KPAD, hq, cols], start=True, stop=True)
                else:
                    for q in range(QUAD):
                        h = hq * QUAD + q
                        last = nc.tensor.matmul(p_m[32 * q:32 * q + 32, k % 3, 0:CH], q_st[s][0:KPAD, h, TOK:SEQ],
                                                k_st[s][0:KPAD, h, cols], start=True, stop=True)
                last.then_inc(rows_done, 1)

            def turn_max(b):
                pe.wait_ge(max_step, 6 * b + 6)
                pe.wait_ge(rows_reduced, NCH * b + NCH)
                for a in range(PARTS):
                    last = nc.tensor.transpose(p_turn[:, a * P:a * P + P], max_part[:, a, :], g.eye_bf[:])
                last.then_inc(max_turned, 1)

            def unit(u):
                n, r = divmod(u, UNITS)
                return (n, FULL, 0) if r == UNITS - 1 else (n, r // 2, r % 2)

            def score(b, s, u, between=None):
                n, jt, pair = unit(u)
                quad, a = divmod(n, NC)
                cols = slice(a * CH, a * CH + CH)
                pe.wait_ge(exp_done, NU * b + max(u - 1, 0))
                if jt < FULL:
                    for e in range(2):
                        if between:
                            between(e)
                        h = quad * QUAD + 2 * pair + e
                        last = nc.tensor.matmul(p_s[:, u % 2, e, 0:CH], k_st[s][0:KMAX, h, jt * P:jt * P + P],
                                                q_st[s][0:KMAX, h, cols], start=True, stop=True)
                else:
                    for q in range(QUAD):
                        h = quad * QUAD + q
                        last = nc.tensor.matmul(p_s[32 * q:32 * q + 32, u % 2, 0, 0:CH], k_st[s][0:KMAX, h, TOK:SEQ],
                                                q_st[s][0:KMAX, h, cols], start=True, stop=True)
                last.then_inc(scored, 1)

            def weigh(b, s, units):
                for u in units:
                    n, jt, pair = unit(u)
                    quad = n // NC
                    if u % UNITS == 0:
                        pe.wait_ge(sum_copied, NSUM * b + n)
                    pe.wait_ge(exp_done, NU * b + u + 1)
                    for e in range(2 if jt < FULL else QUAD):
                        q = 2 * pair + e
                        h = quad * QUAD + q
                        last = nc.tensor.matmul(p_o[32 * q:32 * q + 32, 0:CH], vw[s][:, jt, h, :],
                                                prob[:, u % ERING, e if jt < FULL else 0, :],
                                                start=(jt == 0), stop=(jt == FULL), skip_group_check=True)
                    last.then_inc(pv_done, 1)

            def step(b, i, s, i_next):
                pe.wait_ge(max_in[s], MAX_IN * (i + 1))
                pe.wait_ge(v_in[s], 16 * (i + 1))
                k, turned = 0, False

                def row_chunks(share):
                    nonlocal k, turned
                    while i_next is not None and k < NCH and k < share * NCH:
                        if k == 0 or k == NCH // 2:
                            pe.wait_ge(half_in[1 - s][k // (NCH // 2)], HALF_IN * (i_next + 1))
                        row_chunk(b + 1, 1 - s, k)
                        k += 1

                score(b, s, 0)
                score(b, s, 1)
                for n, group in enumerate(GROUPS):
                    until = group[-1] / (NU - 14)
                    following = GROUPS[n + 1] if n + 1 < len(GROUPS) else []
                    for m, u in enumerate(following):
                        score(b, s, u, lambda e: row_chunks(until - (2 * (len(following) - 1 - m) + 1 - e) / 2 / (NU - 14)))
                    row_chunks(until)
                    if i_next is not None and not turned and group[-1] >= NU - 10:
                        turn_max(b + 1)
                        turned = True
                    weigh(b, s, group)

            for k in range(NCH):
                if k == 0 or k == NCH // 2:
                    pe.wait_ge(half_in[0][k // (NCH // 2)], HALF_IN)
                row_chunk(0, 0, k)
            turn_max(0)
            with pe.Fori(0, B // 2 - 1) as i:
                step(2 * i, i, 0, i)
                step(2 * i + 1, i, 1, i + 1)
            step(B - 2, B // 2 - 1, 0, B // 2 - 1)
            step(B - 1, B // 2 - 1, 1, None)


def join_stage(g):
    nc, arg, hid = g.nc, g.arg, g.hid
    w_in, set_up = g.sem("c_w_in"), g.sem("c_set_up")
    sums_in = [g.sem(f"c_sums_in{s}") for s in range(2)]
    turned, inverted, scaled = g.sem("c_turned"), g.sem("c_inverted"), g.sem("c_scaled")
    back, back_copied, projected, added = g.sem("c_back"), g.sem("c_back_copied"), g.sem("c_projected"), g.sem("c_added")
    pe_alone = g.sem("c_pe_alone")
    W = HEADS * 32
    with ExitStack() as c:
        sb = lambda n, s, d=F32: c.enter_context(nc.sbuf_tensor(n, s, d))
        ps = lambda n, s: c.enter_context(nc.psum_tensor(n, s, F32))
        sums = [sb(f"c_sums{s}", [P, HG, SEQ]) for s in range(2)]
        inv = sb("c_inv", [P, NT, HEADS])
        att = sb("c_att", [P, NT, HEADS, DH])
        attT = sb("c_attT", [P, NT * P])
        w_out = sb("c_w_out", [P, D])
        p_turn = ps("c_p_turn", [P, FULL // 2, 2, HEADS, 32])
        p_last = ps("c_p_last", [P, 512])
        p_back = ps("c_p_back", [P, 1, 512])
        p_out = ps("c_p_out", [P, 2, 512])
        block = c.enter_context(nc.Block())
        p_last_h = p_last[0:TXT, 0:W].rearrange("p (h d) -> p h d", h=HEADS)
        p_full = p_turn[:].rearrange("p a b h d -> p (a b) h d")

        @block.sync
        def _(sp):
            sp.wait_ge(set_up, 2)
            sp.dma_start(w_out[0:D, :], arg["L0_attn_w_out"]).then_inc(w_in, 16)
            sp.dma_start(w_out[D:D + 1, :], arg["L0_attn_b_out"].rearrange("(a n) -> a n", a=1)).then_inc(w_in, 16)
            with sp.Fori(0, B // 2) as i:
                for s in range(2):
                    sp.wait_ge(turned, NT * (2 * i))
                    sp.dma_start(sums[s][:].rearrange("p a t -> p (a t)"), g.sum_scr[2 * i + s, :, :]).then_inc(sums_in[s], 16)

        @block.gpsimd
        def _(pool):
            nc.gpsimd.memset(w_out[D:P, :], 0.0).then_inc(set_up, 1)
            nc.gpsimd.memset(attT[D:P, :], 0.0).then_inc(set_up, 1)
            pool.wait_ge(set_up, 2)
            nc.gpsimd.memset(attT[D:D + 1, :], 1.0).then_inc(set_up, 1)
            pool.wait_ge(set_up, 3)
            nc.gpsimd.memset(att[:, FULL, :, :], 0.0).then_inc(set_up, 1)

        @block.tensor
        def _(pe):
            pe.wait_ge(w_in, 32)
            with pe.Fori(0, B // 2) as i:
                for s in range(2):
                    b = 2 * i + s
                    pe.wait_ge(sums_in[s], 16 * i + 16)
                    pe.wait_ge(scaled, 2 * b)
                    for t in range(NT):
                        for quad in range(HG):
                            if t < FULL:
                                dst = p_turn[:, t // 2, t % 2, quad * QUAD:quad * QUAD + QUAD, :].rearrange("p h d -> p (h d)")
                                last = nc.tensor.transpose(dst, sums[s][:, quad, t * P:t * P + P], g.eye[:])
                            else:
                                last = nc.tensor.transpose(p_last[0:TXT, quad * P:quad * P + P],
                                                           sums[s][:, quad, TOK:SEQ], g.eye[:])
                        last.then_inc(turned, 1)
                    for a in range(3):
                        wait_alone(pe, scaled, 2 * b + (1 if a < 2 else 2), pe_alone)
                        wait_alone(pe, back_copied, 3 * b + a, pe_alone)
                        for t in range(3 * a, 3 * a + 3):
                            last = nc.tensor.transpose(p_back[0:D, 0, (t % 3) * P:(t % 3) * P + P],
                                                       att[:, t, :, :].rearrange("p h d -> p (h d)"), g.eye[:])
                        last.then_inc(back, 1)
                    pe.wait_ge(back_copied, 3 * b + 3)
                    pe.wait_ge(added, 2 * b)
                    for t in range(NT):
                        last = nc.tensor.matmul(p_out[:, t // FULL, (t % FULL) * D:(t % FULL) * D + D],
                                                attT[:, t * P:t * P + P], w_out[:, :], start=True, stop=True)
                    last.then_inc(projected, 1)

        @block.scalar
        def _(act):
            act.wait_ge(set_up, 4)
            with act.Fori(0, B) as b:
                for a in range(3):
                    act.wait_ge(back, 3 * b + a + 1)
                    act.wait_ge(projected, b)
                    nc.scalar.copy(attT[0:D, 3 * a * P:3 * a * P + 3 * P], p_back[0:D, 0, 0:3 * P]).then_inc(back_copied, 1)

        @block.vector
        def _(dve):
            dve.wait_ge(set_up, 4)
            with dve.Fori(0, B) as b:
                dve.wait_ge(turned, NT * b + NT)
                nc.vector.reciprocal(inv[:, 0:FULL, :], p_full[:, :, :, DH]).then_inc(inverted, 1)
                nc.vector.reciprocal(inv[0:TXT, FULL, :], p_last_h[:, :, DH]).then_inc(inverted, 1)
                dve.wait_ge(inverted, 2 * b + 2)
                dve.wait_ge(back, 3 * b)
                nc.vector.tensor_tensor(att[:, 0:FULL, :, :].rearrange("p t h d -> p (t h) d"),
                                        p_full[:, :, :, 0:DH].rearrange("p t h d -> p (t h) d"),
                                        inv[:, 0:FULL, :].rearrange("p t h -> p (t h)").unsqueeze(2)
                                        .to_broadcast([P, FULL * HEADS, DH]), ALU.mult).then_inc(scaled, 1)
                nc.vector.tensor_tensor(att[0:TXT, FULL, :, :], p_last_h[:, :, 0:DH],
                                        inv[0:TXT, FULL, :].unsqueeze(2).to_broadcast([TXT, HEADS, DH]), ALU.mult).then_inc(scaled, 1)
                dve.wait_ge(projected, b + 1)
                nc.vector.tensor_tensor(hid[:, b, 0:FULL, :].rearrange("p t d -> p (t d)"),
                                        hid[:, b, 0:FULL, :].rearrange("p t d -> p (t d)"), p_out[:, 0, :], ALU.add).then_inc(added, 1)
                nc.vector.tensor_tensor(hid[0:TXT, b, FULL, :], hid[0:TXT, b, FULL, :], p_out[0:TXT, 1, 0:D], ALU.add).then_inc(added, 1)


def split_parts(nc, eng, value, part, rest, done, count):
    nc.vector.tensor_copy(part[0], value).then_inc(done, 1)
    eng.wait_ge(done, count + 1)
    nc.vector.tensor_tensor(rest, value, part[0], ALU.subtract).then_inc(done, 1)
    eng.wait_ge(done, count + 2)
    nc.vector.tensor_copy(part[1], rest).then_inc(done, 1)
    eng.wait_ge(done, count + 3)
    nc.vector.tensor_tensor(part[2], rest, part[1], ALU.subtract).then_inc(done, 2)


def gate_block(g, pre, E, gate_w, gate_b, keep, x12_all, x13_all, cT_all):
    nc, hid = g.nc, g.hid
    ln = [g.sem(pre + n) for n in ("stats", "moments", "rstd", "alone")]
    w_in, set_up, normed, kept = g.sem(pre + "w_in"), g.sem(pre + "set_up"), g.sem(pre + "normed"), g.sem(pre + "kept")
    turned, xT_ready, xT_kept = g.sem(pre + "turned"), g.sem(pre + "xT_ready"), g.sem(pre + "xT_kept")
    logits_done, step, gap_ready, gap_exp = g.sem(pre + "logits"), g.sem(pre + "step"), g.sem(pre + "gap"), g.sem(pre + "gap_exp")
    best, split = g.sem(pre + "best"), g.sem(pre + "split")
    alone = g.sem(pre + "pool_alone")
    first_ready, rest_ready, second_ready = g.sem(pre + "first_ready"), g.sem(pre + "rest_ready"), g.sem(pre + "second_ready")
    stacked, c_turned, c_kept, pe_alone = g.sem(pre + "stacked"), g.sem(pre + "c_turned"), g.sem(pre + "c_kept"), g.sem(pre + "pe_alone")
    with ExitStack() as c:
        sb = lambda n, s, d=F32: c.enter_context(nc.sbuf_tensor(pre + n, s, d))
        ps = lambda n, s: c.enter_context(nc.psum_tensor(pre + n, s, F32))
        st, mv, xn = sb("st", [P, NT, 6]), sb("mv", [P, NT, 4]), sb("xn", [P, NT, 2, D])
        xT = sb("xT", [P, NT * P])
        gw, gb, number = sb("gw", [P, E]), sb("gb", [P, E]), sb("number", [P, EINS])
        logit = sb("logit", [P, NT, E])
        top, top_at, at = sb("top", [P, NT, 8]), sb("top_at", [P, NT, 8], U32), sb("at", [P, NT, 2])
        gap, gap_e, w1, w2, den = (sb(n, [P, NT]) for n in ("gap", "gap_e", "w1", "w2", "den"))
        is1, is2, cw, c_rest = (sb(n, [P, NT, E]) for n in ("is1", "is2", "cw", "c_rest"))
        c_part = [sb(f"c_part{i}", [P, NT, E], BF16) for i in range(PARTS)]
        c_stack = sb("c_stack", [P, NT, len(PAIRS), EINS], BF16)
        x_first, x_rest = sb("x_first", [P, SEQ], BF16), sb("x_rest", [P, SEQ])
        p_turn = ps("p_turn", [P, 3, 512])
        p_log = ps("p_log", [P, NT, E])
        p_c = ps("p_c", [P, 2, 512])
        block = c.enter_context(nc.Block())
        p_ct = [p_c[0:GK, k, :].bitcast(BF16) for k in range(2)]

        @block.sync
        def _(sp):
            sp.wait_ge(set_up, 1)
            sp.dma_start(gw[0:D, :], gate_w, allow_slow_non_contiguous=True).then_inc(w_in, 16)
            sp.dma_start(gb[:, :], gate_b.rearrange("(a e) -> a e", a=1).to_broadcast([P, E])).then_inc(w_in, 16)
            sp.dma_start(number[:, :], g.const["number"].to_broadcast([P, EINS])).then_inc(w_in, 16)

        @block.gpsimd
        def _(pool):
            nc.gpsimd.memset(gw[D:P, :], 0.0).then_inc(set_up, 1)
            pool.wait_ge(set_up, 1)
            nc.gpsimd.memset(c_stack[:], 0.0).then_inc(set_up, 1)

            def other_parts(b, powers):
                wait_alone(pool, ln[2], 2 * powers, alone)
                wait_alone(pool, first_ready, b + 1, alone)
                wait_alone(pool, second_ready, b, alone)
                nc.gpsimd.tensor_tensor(x_rest[D:P, :], xT[D:P, 0:SEQ], x_first[D:P, :], ALU.subtract).then_inc(rest_ready, 1)
                wait_alone(pool, second_ready, b + 1, alone)
                nc.gpsimd.tensor_tensor(x13_all[D:P, b, :], x_rest[D:P, :], x12_all[D:P, b, :], ALU.subtract).then_inc(rest_ready, 1)

            layernorm_pool(g, pool, 0, mv, ln)
            with pool.Fori(0, B - 1) as b:
                wait_alone(pool, rest_ready, 2 * b, alone)
                layernorm_pool(g, pool, b + 1, mv, ln)
                other_parts(b, b + 2)
            other_parts(B - 1, B)

        @block.tensor
        def _(pe):
            pe.wait_ge(w_in, 48)
            with pe.Fori(0, B) as b:
                pe.wait_ge(xT_ready, b)
                wait_alone(pe, normed, NT * b + NT, pe_alone)
                for t in range(NT):
                    last = nc.tensor.transpose(p_turn[:, t // 3, (t % 3) * P:(t % 3) * P + P],
                                               xn[:, t, :, :].rearrange("p q d -> p (q d)"), g.eye[:])
                last.then_inc(turned, 1)
                pe.wait_ge(xT_ready, b + 1)
                pe.wait_ge(step, 10 * b)
                for t in range(NT):
                    last = nc.tensor.matmul(p_log[:, t, :], xT[:, t * P:t * P + P], gw[:, :], start=True, stop=True)
                last.then_inc(logits_done, 1)
                pe.wait_ge(stacked, len(PAIRS) * (b + 1))
                wait_alone(pe, c_kept, 2 * b, pe_alone)
                for t in range(NT):
                    last = nc.tensor.transpose(p_ct[t // FULL][:, (t % FULL) * P:(t % FULL) * P + P],
                                               c_stack[:, t, :, :].rearrange("p k e -> p (k e)"), g.eye_bf[:])
                last.then_inc(c_turned, 1)

        @block.scalar
        def _(act):
            act.wait_ge(set_up, 2)
            with act.Fori(0, B) as b:
                act.wait_ge(turned, b + 1)
                act.wait_ge(logits_done, b)
                act.wait_ge(rest_ready, 2 * b)
                nc.scalar.copy(xT[:, :].rearrange("p (a n) -> p a n", a=3), p_turn[:, :, 0:3 * P]).then_inc(xT_ready, 1)
                act.wait_ge(xT_ready, b + 1)
                nc.scalar.copy(x12_all[0:D, b, :], xT[0:D, 0:SEQ]).then_inc(xT_kept, 1)
                nc.scalar.copy(x13_all[0:D, b, :], xT[0:D, 0:SEQ]).then_inc(xT_kept, 1)
                act.wait_ge(rest_ready, 2 * b)
                nc.scalar.copy(x_first[D:P, :], xT[D:P, 0:SEQ]).then_inc(first_ready, 1)
                act.wait_ge(rest_ready, 2 * b + 1)
                nc.scalar.copy(x12_all[D:P, b, :], x_rest[D:P, :]).then_inc(second_ready, 1)
                if keep is not None:
                    nc.scalar.copy(keep[:, b, :, :], xn[:, :, 0, :]).then_inc(kept, 1)
                act.wait_ge(gap_ready, b + 1)
                nc.scalar.activation(gap_e[:, :], gap[:, :], ACT.Exp).then_inc(gap_exp, 1)
                act.wait_ge(split, 5 * b + 5)
                act.wait_ge(c_turned, b)
                for k, (ci, _) in enumerate(PAIRS):
                    nc.scalar.copy(c_stack[:, :, k, 0:E], c_part[ci][:, :, :]).then_inc(stacked, 1)
                act.wait_ge(c_turned, b + 1)
                nc.scalar.copy(cT_all[:, b, 0:TOK], p_ct[0][:, :]).then_inc(c_kept, 1)
                nc.scalar.copy(cT_all[:, b, TOK:SEQ], p_ct[1][:, 0:TXT]).then_inc(c_kept, 1)

        @block.vector
        def _(dve):
            dve.wait_ge(w_in, 48)

            def stats(b):
                layernorm_stats(nc, dve, b, lambda t: hid[:, b, t, :], st, mv, ln)

            def norm(b):
                dve.wait_ge(turned, b)
                if keep is not None:
                    dve.wait_ge(kept, b)
                layernorm_apply(nc, dve, b, lambda t: hid[:, b, t, :], lambda t: xn[:, t, :, :], mv, ln, normed, twice=True)

            def choose(b):
                wide = lambda v: v.unsqueeze(2).to_broadcast([P, NT, E])
                dve.wait_ge(logits_done, b + 1)
                nc.vector.tensor_tensor(logit[:, :, :], p_log[:, :, :], gb[:, :].unsqueeze(1).to_broadcast([P, NT, E]),
                                        ALU.add).then_inc(step, 1)
                wait_alone(dve, step, 10 * b + 1, ln[3])
                for t in range(NT):
                    nc.vector.max(top[:, t, :], logit[:, t, :]).then_inc(best, 1)
                wait_alone(dve, best, 2 * NT * b + NT, ln[3])
                for t in range(NT):
                    nc.vector.max_index(top_at[:, t, :], top[:, t, :], logit[:, t, :]).then_inc(best, 1)
                nc.vector.tensor_tensor(gap[:, :], top[:, :, 1], top[:, :, 0], ALU.subtract).then_inc(gap_ready, 1)
                dve.wait_ge(best, 2 * NT * b + 2 * NT)
                nc.vector.tensor_copy(at[:, :, :], top_at[:, :, 0:2]).then_inc(step, 1)
                dve.wait_ge(gap_exp, b + 1)
                nc.vector.tensor_scalar(den[:, :], gap_e[:, :], 1.0, None, ALU.add).then_inc(step, 1)
                dve.wait_ge(step, 10 * b + 3)
                nc.vector.reciprocal(w1[:, :], den[:, :]).then_inc(step, 1)
                nc.vector.tensor_tensor(is1[:, :, :], number[:, 0:E].unsqueeze(1).to_broadcast([P, NT, E]), wide(at[:, :, 0]),
                                        ALU.is_equal).then_inc(step, 1)
                nc.vector.tensor_tensor(is2[:, :, :], number[:, 0:E].unsqueeze(1).to_broadcast([P, NT, E]), wide(at[:, :, 1]),
                                        ALU.is_equal).then_inc(step, 1)
                dve.wait_ge(step, 10 * b + 6)
                nc.vector.tensor_tensor(w2[:, :], gap_e[:, :], w1[:, :], ALU.mult).then_inc(step, 1)
                nc.vector.tensor_tensor(is1[:, :, :], is1[:, :, :], wide(w1[:, :]), ALU.mult).then_inc(step, 1)
                dve.wait_ge(step, 10 * b + 8)
                nc.vector.tensor_tensor(is2[:, :, :], is2[:, :, :], wide(w2[:, :]), ALU.mult).then_inc(step, 1)
                dve.wait_ge(step, 10 * b + 9)
                nc.vector.tensor_tensor(cw[:, :, :], is1[:, :, :], is2[:, :, :], ALU.add).then_inc(step, 1)
                dve.wait_ge(step, 10 * b + 10)
                dve.wait_ge(stacked, len(PAIRS) * b)
                split_parts(nc, dve, cw[:, :, :], [v[:, :, :] for v in c_part], c_rest[:, :, :], split, 5 * b)

            stats(0)
            norm(0)
            with dve.Fori(0, B - 1) as b:
                stats(b + 1)
                choose(b)
                norm(b + 1)
            choose(B - 1)


def experts_block(g, pre, E, H, w1_arg, b1_arg, w2_arg, b2_arg, turned_weights, x12_all, x13_all, cT_all, acc, send):
    nc = g.nc
    HALVES = H // P
    HID = E * HALVES
    ALL = NC * HID
    ZR, RR, HR = 3, 4, 6
    AHEAD = 4
    assert ALL % ZR == 0 and ALL % RR == 0 and ALL % HR == 0
    w_in, set_up, w_turned, w_copied = g.sem(pre + "w_in"), g.sem(pre + "set_up"), g.sem(pre + "w_turned"), g.sem(pre + "w_copied")
    split, w_ready, b1_turned, b1_ready = g.sem(pre + "split"), g.sem(pre + "w_ready"), g.sem(pre + "b1_turned"), g.sem(pre + "b1_ready")
    spread, hidden_done, relu_done, weighted = g.sem(pre + "spread"), g.sem(pre + "hidden"), g.sem(pre + "relu"), g.sem(pre + "weighted")
    summed, sum_copied = g.sem(pre + "summed"), g.sem(pre + "sum_copied")
    y_turned, added, sent, pe_alone = g.sem(pre + "y_turned"), g.sem(pre + "added"), g.sem(pre + "sent"), g.sem(pre + "pe_alone")
    with ExitStack() as c:
        sb = lambda n, s, d=F32: c.enter_context(nc.sbuf_tensor(pre + n, s, d))
        ps = lambda n, s: c.enter_context(nc.psum_tensor(pre + n, s, F32))
        w1_11, w1_22, w1_31 = (sb(n, [P, HID, P], BF16) for n in ("w1_11", "w1_22", "w1_31"))
        w2 = sb("w2", [P, HID, D])
        pick_bf = sb("pick_bf", [GK, EINS, P], BF16)
        part_of = sb("part_of", [GK, PARTS])
        b2_raw, b2_rest, b2_sel = (sb(n, [GK, D]) for n in ("b2_raw", "b2_rest", "b2_sel"))
        b2_part = [sb(f"b2_part{i}", [GK, D], BF16) for i in range(PARTS)]
        b2s = sb("b2s", [GK, D], BF16)
        b1_row, b1 = sb("b1_row", [HID, P]), sb("b1", [P, HID])
        raw = sb("raw", [P, RR, CH])
        hidden = sb("hidden", [P, HR, CH])
        yT = sb("yT", [P, NT * P])
        p_c = ps("p_c", [P, 2, 512])
        p_z = ps("p_z", [P, ZR, 512])
        p_y = ps("p_y", [P, 2, 512])
        p_t = ps("p_t", [P, 3, 2, D])

        def tile_of(m):
            a, k = divmod(m, HID)
            n, r = divmod(k, 2 * HALVES)
            return a, 2 * n + r % 2, r // 2

        N_IN = 3 + len(PAIRS) + (2 * E + 1 if turned_weights else 3)
        with ExitStack() as c2:
            sb2 = lambda n, s, d=F32: c2.enter_context(nc.sbuf_tensor(pre + n, s, d))
            pick = sb2("pick", [GK, EINS, P])
            w1 = sb2("w1", [P, HID, P])
            w1_rest, w1_p3 = sb2("w1_rest", [P, HID, P]), sb2("w1_p3", [P, HID, P], BF16)
            if turned_weights:
                w1_raw = sb2("w1_raw", [P, E, HALVES, 2, D])
                w2_raw = sb2("w2_raw", [P, E // 2, H])
                WQ = HID + HID // 2
            block = c2.enter_context(nc.Block())

            @block.sync
            def _(sp):
                sp.dma_start(pick[:], g.const["pick"]).then_inc(w_in, 16)
                sp.dma_start(part_of[:], g.const["part_of"]).then_inc(w_in, 16)
                sp.dma_start(b1_row[:], b1_arg.rearrange("e (f h) -> (e f) h", h=P)).then_inc(w_in, 16)
                sp.wait_ge(set_up, 1)
                for k in range(len(PAIRS)):
                    sp.dma_start(b2_raw[k * EINS:k * EINS + E, :], b2_arg).then_inc(w_in, 16)
                if turned_weights:
                    for e in range(E):
                        for q in range(2):
                            sp.dma_start(w1_raw[:, e, :, q, :], w1_arg[e, :, :].rearrange("(f h) d -> h f d", h=P)).then_inc(w_in, 16)
                    sp.dma_start(w2_raw[:], w2_arg.rearrange("(n q) d h -> (q d) n h", q=2)).then_inc(w_in, 16)
                else:
                    for q in range(2):
                        sp.dma_start(w1[q * D:q * D + D, :, :], w1_arg.rearrange("e d h -> d e h")).then_inc(w_in, 16)
                    sp.dma_start(w2[:], w2_arg.rearrange("e h d -> h e d")).then_inc(w_in, 16)

            @block.gpsimd
            def _(pool):
                nc.gpsimd.memset(b2_raw[:], 0.0).then_inc(set_up, 1)
                pool.wait_ge(set_up, 1)
                nc.gpsimd.memset(yT[:, SEQ:NT * P], 0.0).then_inc(set_up, 1)

            @block.tensor
            def _(pe):
                pe.wait_ge(w_in, 16 * N_IN)
                nc.tensor.transpose(p_y[:, 0, 0:HID], b1_row[:, :], g.eye[0:HID, 0:HID]).then_inc(b1_turned, 1)
                if turned_weights:
                    for k in range(WQ):
                        if k >= 2:
                            pe.wait_ge(w_copied, k - 1)
                        src = w1_raw[:, k // HALVES, k % HALVES, :, :].rearrange("p q d -> p (q d)") if k < HID else \
                            w2_raw[:, (k - HID) // HALVES, (k - HID) % HALVES * P:(k - HID) % HALVES * P + P]
                        nc.tensor.transpose(p_z[:, k % 2, 0:P], src, g.eye[:]).then_inc(w_turned, 1)

            @block.scalar
            def _(act):
                act.wait_ge(b1_turned, 1)
                nc.scalar.copy(b1[:, :], p_y[:, 0, 0:HID]).then_inc(b1_ready, 1)

            @block.vector
            def _(dve):
                dve.wait_ge(w_in, 16 * N_IN)
                nc.vector.tensor_copy(pick_bf[:], pick[:])
                if turned_weights:
                    for k in range(WQ):
                        dve.wait_ge(w_turned, k + 1)
                        if k < HID:
                            nc.vector.tensor_copy(w1[:, k, :], p_z[:, k % 2, 0:P]).then_inc(w_copied, 1)
                        else:
                            n, f = divmod(k - HID, HALVES)
                            nc.vector.tensor_copy(w2[:].rearrange("p (n q f) d -> p n q f d", q=2, f=HALVES)[:, n, :, f, :],
                                                  p_z[:, k % 2, 0:P].rearrange("p (q d) -> p q d", q=2)).then_inc(w_copied, 1)
                    dve.wait_ge(w_copied, WQ)
                split_parts(nc, dve, w1[:, :, :], [w1_11[:, :, :], w1_22[:, :, :], w1_p3[:, :, :]], w1_rest[:, :, :], split, 0)
                dve.wait_ge(split, 5)
                nc.vector.tensor_copy(w1_31[0:D, :, :], w1_p3[0:D, :, :])
                nc.vector.tensor_copy(w1_31[D:P, :, :], w1_11[D:P, :, :])
                split_parts(nc, dve, b2_raw[:, :], [v[:, :] for v in b2_part], b2_rest[:, :], split, 5)
                dve.wait_ge(split, 10)
                nc.vector.tensor_scalar(b2_sel[:, :], b2_part[0][:, :], part_of[:, 0:1], None, ALU.mult).then_inc(split, 1)
                for i in range(1, PARTS):
                    dve.wait_ge(split, 10 + i)
                    nc.vector.scalar_tensor_tensor(b2_sel[:, :], b2_part[i][:, :], part_of[:, i:i + 1], b2_sel[:, :],
                                                   ALU.mult, ALU.add).then_inc(split, 1)
                dve.wait_ge(split, 10 + PARTS)
                nc.vector.tensor_copy(b2s[:, :], b2_sel[:, :])

        block = c.enter_context(nc.Block())

        @block.sync
        def _(sp):
            if send:
                with sp.Fori(0, B) as b:
                    sp.wait_ge(added, 6 * b + 6)
                    sp.dma_start(g.out[b, 0:TOK, :].rearrange("(t p) d -> p t d", p=P), acc[:, b, 0:FULL, :]).then_inc(sent, 16)
                    sp.dma_start(g.out[b, TOK:SEQ, :], acc[0:TXT, b, FULL, :]).then_inc(sent, 16)
                sp.wait_ge(sent, 32 * B)

        @block.tensor
        def _(pe):
            def cols(rows, b, a):
                return rows[:, b, a * CH:a * CH + CH]

            def first(b, m):
                a, e, f = tile_of(m)
                pe.wait_ge(relu_done, ALL * b + max(m - ZR + 1, 0))
                out = p_z[:, m % ZR, 0:CH]
                nc.tensor.matmul(out, w1_31[:, e * HALVES + f, :], cols(x13_all, b, a), start=True, stop=False)
                nc.tensor.matmul(out, w1_22[:, e * HALVES + f, :], cols(x12_all, b, a), start=False, stop=False)
                nc.tensor.matmul(out, w1_11[:, e * HALVES + f, :], cols(x12_all, b, a), start=False, stop=True)\
                    .then_inc(hidden_done, 1)

            def spread_gates(b, m):
                if tile_of(m)[2]:
                    return
                for j in (m, m + 1):
                    a, e, _ = tile_of(j)
                    pe.wait_ge(weighted, ALL * b + max(j - 1, 0))
                    nc.tensor.matmul(p_c[:, e % 2, 0:CH], pick_bf[:, e, :], cols(cT_all, b, a), start=True, stop=True)\
                        .then_inc(spread, 1)

            def second(b, m):
                a, k = divmod(m, HID)
                if k == 0:
                    wait_alone(pe, sum_copied, NC * b + max(a - 1, 0), pe_alone)
                    nc.tensor.matmul(p_y[0:D, a % 2, 0:CH], b2s[:, :], cols(cT_all, b, a), start=True, stop=False,
                                     skip_group_check=True)
                pe.wait_ge(weighted, ALL * b + m + 2)
                for j in (m, m + 1):
                    _, e, f = tile_of(j)
                    nc.tensor.matmul(p_y[e % 2 * D:e % 2 * D + D, a % 2, 0:CH], w2[:, e * HALVES + f, :],
                                     hidden[:, j % HR, :], start=(k == 0 and j == m + 1), stop=(k >= HID - 2),
                                     skip_group_check=True).then_inc(summed, 1)

            with pe.Fori(0, B) as b:
                for m in range(0, ALL + AHEAD, 2):
                    if m < ALL:
                        first(b, m)
                        first(b, m + 1)
                        spread_gates(b, m)
                    if m >= AHEAD:
                        second(b, m - AHEAD)
                for r in range(3):
                    pe.wait_ge(sum_copied, NC * b + NC)
                    wait_alone(pe, added, 6 * b + 2 * r, pe_alone)
                    for t in range(3 * r, 3 * r + 3):
                        last = nc.tensor.transpose(p_t[:, t % 3, :, :].rearrange("p q d -> p (q d)"), yT[:, t * P:t * P + P], g.eye[:])
                    last.then_inc(y_turned, 1)

        @block.scalar
        def _(act):
            with act.Fori(0, B) as b:
                def copy_sum(a):
                    act.wait_ge(summed, ALL * b + (a + 1) * HID)
                    act.wait_ge(y_turned, 3 * b)
                    nc.scalar.copy(yT[:, a * CH:a * CH + CH], p_y[:, a % 2, 0:CH]).then_inc(sum_copied, 1)

                for m in range(ALL):
                    a, e, f = tile_of(m)
                    act.wait_ge(hidden_done, ALL * b + m + 1)
                    act.wait_ge(weighted, ALL * b + max(m - RR + 1, 0))
                    nc.scalar.activation(raw[:, m % RR, :], p_z[:, m % ZR, 0:CH], ACT.Relu,
                                         bias=b1[:, e * HALVES + f:e * HALVES + f + 1]).then_inc(relu_done, 1)
                    if m % HID == AHEAD + 2 and m > HID:
                        copy_sum(a - 1)
                copy_sum(NC - 1)

        @block.vector
        def _(dve):
            with dve.Fori(0, B) as b:
                for m in range(ALL):
                    a, e, f = tile_of(m)
                    dve.wait_ge(relu_done, ALL * b + m + 1)
                    dve.wait_ge(spread, NC * E * b + a * E + e + 1)
                    dve.wait_ge(summed, ALL * b + max(m - HR + 1, 0))
                    nc.vector.tensor_tensor(hidden[:, m % HR, :], raw[:, m % RR, :], p_c[:, e % 2, 0:CH], ALU.mult)\
                        .then_inc(weighted, 1)
                for r in range(3):
                    rows = acc[:, b, 3 * r:3 * r + 3, :]
                    dve.wait_ge(y_turned, 3 * b + r + 1)
                    for q in range(2):
                        if q:
                            dve.wait_ge(added, 6 * b + 2 * r + 1)
                        nc.vector.tensor_tensor(rows, rows, p_t[:, :, q, :], ALU.add).then_inc(added, 1)


def affine_block(g, pre, xn_all, gamma_arg, beta_arg):
    nc, hid = g.nc, g.hid
    ln = [g.sem(pre + n) for n in ("stats", "moments", "rstd", "alone")]
    w_in, normed, step = g.sem(pre + "w_in"), g.sem(pre + "normed"), g.sem(pre + "step")
    with ExitStack() as c:
        sb = lambda n, s, d=F32: c.enter_context(nc.sbuf_tensor(pre + n, s, d))
        st, mv, y = sb("st", [P, NT, 6]), sb("mv", [P, NT, 4]), sb("y", [P, NT, D])
        gamma, beta = sb("gamma", [P, D]), sb("beta", [P, D])
        block = c.enter_context(nc.Block())

        @block.sync
        def _(sp):
            sp.dma_start(gamma[:, :], gamma_arg.rearrange("(a d) -> a d", a=1).to_broadcast([P, D])).then_inc(w_in, 16)
            sp.dma_start(beta[:, :], beta_arg.rearrange("(a d) -> a d", a=1).to_broadcast([P, D])).then_inc(w_in, 16)

        @block.gpsimd
        def _(pool):
            with pool.Fori(0, B) as b:
                layernorm_pool(g, pool, b, mv, ln)

        @block.vector
        def _(dve):
            dve.wait_ge(w_in, 32)
            wide = lambda v: v[:, :].unsqueeze(1).to_broadcast([P, NT, D])

            def stats(b):
                layernorm_stats(nc, dve, b, lambda t: xn_all[:, b, t, :], st, mv, ln)

            def norm(b):
                layernorm_apply(nc, dve, b, lambda t: xn_all[:, b, t, :], lambda t: y[:, t, :], mv, ln, normed)

            def finish(b):
                dve.wait_ge(normed, NT * b + NT)
                nc.vector.tensor_tensor(y[:, :, :], y[:, :, :], wide(gamma), ALU.mult).then_inc(step, 1)
                dve.wait_ge(step, 4 * b + 1)
                nc.vector.tensor_tensor(y[:, :, :], y[:, :, :], wide(beta), ALU.add).then_inc(step, 1)
                dve.wait_ge(step, 4 * b + 2)
                nc.vector.tensor_tensor(hid[:, b, 0:FULL, :], hid[:, b, 0:FULL, :], y[:, 0:FULL, :], ALU.add).then_inc(step, 1)
                nc.vector.tensor_tensor(hid[0:TXT, b, FULL, :], hid[0:TXT, b, FULL, :], y[0:TXT, FULL, :], ALU.add).then_inc(step, 1)
                dve.wait_ge(step, 4 * b + 4)

            stats(0)
            with dve.Fori(0, B - 1) as b:
                norm(b)
                wait_alone(dve, normed, NT * b + NT, ln[3])
                stats(b + 1)
                finish(b)
            norm(B - 1)
            finish(B - 1)


def drive_block(g, u_all, vn_all, level):
    nc, hid, arg = g.nc, g.hid, g.arg
    ln = [[g.sem(f"h_{n}{k}") for n in ("stats", "moments", "rstd", "alone")] for k in range(2)]
    w_in, w_turned, w_ready, set_up = g.sem("h_w_in"), g.sem("h_w_turned"), g.sem("h_w_ready"), g.sem("h_set_up")
    normed, normed_again, turned, vT_ready = g.sem("h_normed"), g.sem("h_normed_again"), g.sem("h_turned"), g.sem("h_vT_ready")
    driven, relu_done, picked, summed, pe_alone = g.sem("h_driven"), g.sem("h_relu"), g.sem("h_picked"), g.sem("h_summed"), g.sem("h_pe_alone")
    added = g.sem("h_added")
    with ExitStack() as c:
        sb = lambda n, s, d=F32: c.enter_context(nc.sbuf_tensor("h_" + n, s, d))
        ps = lambda n, s: c.enter_context(nc.psum_tensor("h_" + n, s, F32))
        st, mv, v = sb("st", [P, NT, 6]), sb("mv", [P, NT, 4]), sb("v", [P, NT, D])
        st2, mv2 = sb("st2", [P, NT, 6]), sb("mv2", [P, NT, 4])
        vT = sb("vT", [P, NT * P])
        dx, dxT = sb("dx", [P, 2, D]), sb("dxT", [P, 2, P])
        column = sb("column", [P, B, B])
        col = sb("col", [P, B])
        u = sb("u", [P, 2, SEQ])
        p_turn = ps("p_turn", [P, 2, 512])
        p_u = ps("p_u", [P, 3, 512])
        p_sum = ps("p_sum", [P, 3, 512])
        block = c.enter_context(nc.Block())

        @block.sync
        def _(sp):
            sp.dma_start(dx[:], arg["L1_attn_Dx"].rearrange("(a n) d -> n a d", a=2)).then_inc(w_in, 16)
            sp.dma_start(column[:], g.const["column"].to_broadcast([P, B, B])).then_inc(w_in, 16)

        @block.gpsimd
        def _(pool):
            nc.gpsimd.memset(vT[D:P, :], 0.0).then_inc(set_up, 1)
            pool.wait_ge(set_up, 1)
            nc.gpsimd.memset(dxT[D:P, :, :], 0.0).then_inc(set_up, 1)
            with pool.Fori(0, B) as b:
                layernorm_pool(g, pool, b, mv, ln[0])
                layernorm_pool(g, pool, b, mv2, ln[1])

        @block.tensor
        def _(pe):
            pe.wait_ge(w_in, 32)
            pe.wait_ge(set_up, 2)
            for a in range(2):
                last = nc.tensor.transpose(p_turn[0:D, a, 0:P], dx[:, a, :], g.eye[:])
            last.then_inc(w_turned, 1)
            pe.wait_ge(w_ready, 1)
            with pe.Fori(0, B) as b:
                wait_alone(pe, normed, NT * b + NT, pe_alone)
                wait_alone(pe, vT_ready, 3 * b, pe_alone)
                for a in range(3):
                    wait_alone(pe, vT_ready, 3 * b + max(a - 1, 0), pe_alone)
                    for t in range(3 * a, 3 * a + 3):
                        last = nc.tensor.transpose(p_turn[0:D, a % 2, t % 3 * P:t % 3 * P + P], v[:, t, :], g.eye[:])
                    last.then_inc(turned, 1)
                pe.wait_ge(vT_ready, 3 * b + 3)
                for k in range(2 * NC):
                    f, a = divmod(k, NC)
                    pe.wait_ge(relu_done, 2 * NC * b + max(k - 2, 0))
                    nc.tensor.matmul(p_u[:, k % 3, 0:CH], dxT[:, f, :], vT[:, a * CH:a * CH + CH], start=True, stop=True)\
                        .then_inc(driven, 1)
                pe.wait_ge(relu_done, 2 * NC * b + 2 * NC)
                pe.wait_ge(picked, b + 1)
                pe.wait_ge(added, b)
                for f in range(2):
                    for a in range(NC):
                        last = nc.tensor.matmul(p_sum[0:B, a, 0:CH], col[:, :], u[:, f, a * CH:a * CH + CH],
                                                start=(f == 0), stop=(f == 1), skip_group_check=True)
                last.then_inc(summed, 1)

        @block.scalar
        def _(act):
            with act.Fori(0, B) as b:
                for a in range(3):
                    act.wait_ge(turned, 3 * b + a + 1)
                    act.wait_ge(driven, 2 * NC * b)
                    nc.scalar.copy(vT[0:D, 3 * a * P:3 * a * P + 3 * P], p_turn[0:D, a % 2, 0:3 * P]).then_inc(vT_ready, 1)
                act.wait_ge(summed, b)
                for k in range(2 * NC):
                    f, a = divmod(k, NC)
                    act.wait_ge(driven, 2 * NC * b + k + 1)
                    nc.scalar.activation(u[:, f, a * CH:a * CH + CH], p_u[:, k % 3, 0:CH], ACT.Relu).then_inc(relu_done, 1)
                act.wait_ge(relu_done, 2 * NC * b + 2 * NC)
                nc.scalar.copy(u_all[:, b, :, :], u[:, :, :])

        @block.vector
        def _(dve):
            dve.wait_ge(w_turned, 1)
            dve.wait_ge(w_in, 32)
            nc.vector.tensor_copy(dxT[0:D, :, :], p_turn[0:D, :, 0:P]).then_inc(w_ready, 1)
            nc.vector.memset(level[:, :], 0.0)

            def first_norm(b):
                layernorm_stats(nc, dve, b, lambda t: hid[:, b, t, :], st, mv, ln[0])

            def first_apply(b):
                dve.wait_ge(turned, 3 * b)
                layernorm_apply(nc, dve, b, lambda t: hid[:, b, t, :], lambda t: v[:, t, :], mv, ln[0], normed)
                wait_alone(dve, normed, NT * b + NT, ln[0][3])
                layernorm_stats(nc, dve, b, lambda t: v[:, t, :], st2, mv2, ln[1])

            def second_apply(b):
                layernorm_apply(nc, dve, b, lambda t: v[:, t, :], lambda t: vn_all[:, b, t, :], mv2, ln[1], normed_again)
                dve.wait_ge(normed_again, NT * b + NT)

            def pick_column(b):
                dve.wait_ge(summed, b)
                nc.vector.tensor_copy(col[:, :], column[:, b, :]).then_inc(picked, 1)

            def add_sums(b):
                dve.wait_ge(summed, b + 1)
                nc.vector.tensor_tensor(level[0:B, :].rearrange("p (a n) -> p a n", a=NC), level[0:B, :].rearrange("p (a n) -> p a n", a=NC),
                                        p_sum[0:B, :, 0:CH], ALU.add).then_inc(added, 1)
                dve.wait_ge(added, b + 1)

            first_norm(0)
            first_apply(0)
            with dve.Fori(0, B - 1) as b:
                pick_column(b)
                first_norm(b + 1)
                second_apply(b)
                first_apply(b + 1)
                add_sums(b)
            pick_column(B - 1)
            second_apply(B - 1)
            add_sums(B - 1)


def level_block(g, level, rate):
    nc = g.nc
    done = g.sem("i_done")
    G = DECAY / L1_EPS
    with ExitStack() as c:
        sb = lambda n, s, d=F32: c.enter_context(nc.sbuf_tensor("i_" + n, s, d))
        small, scaled, total = sb("small", [B, SEQ]), sb("scaled", [B, SEQ]), sb("total", [B, SEQ + 1])
        block = c.enter_context(nc.Block())

        @block.vector
        def _(dve):
            U = level[0:B, :]
            nc.vector.tensor_scalar(scaled[:, :], U, 1.0 / L1_EPS, 1.0, ALU.mult, ALU.min).then_inc(done, 1)
            nc.vector.memset(total[:, 0:1], 0.0).then_inc(done, 1)
            dve.wait_ge(done, 2)
            nc.vector.tensor_scalar(small[:, :], scaled[:, :], 1.0, G, ALU.is_lt, ALU.mult).then_inc(done, 1)
            dve.wait_ge(done, 3)
            nc.vector.tensor_tensor_scan(total[:, 1:SEQ + 1], small[:, :], scaled[:, :], 0.0, ALU.mult, ALU.add).then_inc(done, 1)
            dve.wait_ge(done, 4)
            nc.vector.tensor_scalar(total[:, 1:SEQ + 1], total[:, 1:SEQ + 1], 1.0, None, ALU.min).then_inc(done, 1)
            dve.wait_ge(done, 5)
            nc.vector.scalar_tensor_tensor(scaled[:, :], total[:, 0:SEQ], DECAY, U, ALU.mult, ALU.add).then_inc(done, 1)
            dve.wait_ge(done, 6)
            nc.vector.tensor_scalar(scaled[:, :], scaled[:, :], L1_EPS, None, ALU.max).then_inc(done, 1)
            dve.wait_ge(done, 7)
            nc.vector.reciprocal(rate[:, :], scaled[:, :]).then_inc(done, 1)
            dve.wait_ge(done, 8)


def state_block(g, u_all, rate):
    nc = g.nc
    row_in, picked, spread, decayed, scaled, scanned, pe_alone = (g.sem("j_" + n) for n in
                                                        ("row_in", "picked", "spread", "decayed", "scaled", "scanned", "pe_alone"))
    with ExitStack() as c:
        sb = lambda n, s, d=F32: c.enter_context(nc.sbuf_tensor("j_" + n, s, d))
        rows = sb("rows", [B, B, P])
        row = sb("row", [B, 2, P])
        decay = sb("decay", [P, 2, SEQ])
        ru = sb("ru", [P, 2, 2, SEQ])
        p_r = c.enter_context(nc.psum_tensor("j_p_r", [P, 2, 4, 512], F32))
        block = c.enter_context(nc.Block())

        @block.sync
        def _(sp):
            sp.dma_start(rows[:], g.const["rows"]).then_inc(row_in, 16)

        @block.tensor
        def _(pe):
            with pe.Fori(0, B // 2) as i:
                for s in range(2):
                    b = 2 * i + s
                    wait_alone(pe, picked, b + 1, pe_alone)
                    for a in range(NC):
                        last = nc.tensor.matmul(p_r[:, s, a, 0:CH], row[:, s, :], rate[:, a * CH:a * CH + CH], start=True, stop=True)
                    last.then_inc(spread, 1)

        @block.scalar
        def _(act):
            with act.Fori(0, B // 2) as i:
                for s in range(2):
                    b = 2 * i + s
                    act.wait_ge(scaled, 2 * b + 2)
                    nc.scalar.mul(decay[:, s, :].rearrange("p (a n) -> p a n", a=NC), p_r[:, s, 0:NC, 0:CH], DECAY).then_inc(decayed, 1)

        @block.vector
        def _(dve):
            def pick(b, s):
                nc.vector.tensor_copy(row[:, s, :], rows[:, b, :]).then_inc(picked, 1)

            def scale(b, s):
                dve.wait_ge(spread, b + 1)
                for f in range(2):
                    nc.vector.tensor_tensor(ru[:, s, f, :].rearrange("p (a n) -> p a n", a=NC),
                                            u_all[:, b, f, :].rearrange("p (a n) -> p a n", a=NC),
                                            p_r[:, s, 0:NC, 0:CH], ALU.mult).then_inc(scaled, 1)

            def scan(b, s):
                dve.wait_ge(scaled, 2 * b + 2)
                for f in range(2):
                    nc.vector.tensor_tensor_scan(u_all[:, b, f, :], decay[:, s, :], ru[:, s, f, :], 0.0, ALU.mult, ALU.add)\
                        .then_inc(scanned, 1)

            dve.wait_ge(row_in, 16)
            pick(0, 0)
            pick(1, 1)
            scale(0, 0)
            with dve.Fori(0, B // 2 - 1) as i:
                for s in range(2):
                    b = 2 * i + s
                    dve.wait_ge(scanned, 2 * b)
                    scale(b + 1, 1 - s)
                    dve.wait_ge(decayed, b + 1)
                    pick(b + 2, s)
                    scan(b, s)
            dve.wait_ge(scanned, 2 * (B - 2))
            scale(B - 1, 1)
            for b in (B - 2, B - 1):
                dve.wait_ge(decayed, b + 1)
                scan(b, b % 2)
            dve.wait_ge(scanned, 2 * B)


def pieces():
    out = []
    for lo in range(0, SEQ, 512):
        hi = min(lo + 512, SEQ)
        for s in range(NT):
            at = max(lo, s * P)
            if at < hi:
                out.append((s, at, hi - at))
    return out


def recall_block(g, x_all, vn_all, aT_all):
    nc = g.nc
    parts = pieces()
    NPC = len(parts)
    d_in, set_up = g.sem("k_d_in"), g.sem("k_set_up")
    x_ready, vn_ready = g.sem("k_x_ready"), g.sem("k_vn_ready")
    alike, masked, recalled, copied = g.sem("k_alike"), g.sem("k_masked"), g.sem("k_recalled"), g.sem("k_copied")
    R = 3
    assert NPC % R == 0
    with ExitStack() as c:
        sb = lambda n, s, d=F32: c.enter_context(nc.sbuf_tensor("k_" + n, s, d))
        ps = lambda n, s: c.enter_context(nc.psum_tensor("k_" + n, s, F32))
        x = sb("x", [P, 2, 2, SEQ])
        vn = sb("vn", [P, 2, NT, D])
        decay = sb("decay", [P, SEQ])
        pm = sb("pm", [P, R, 512])
        p_s = ps("p_s", [P, R, 512])
        p_a = ps("p_a", [D, 3, 512])
        block = c.enter_context(nc.Block())
        bank_end = [max(i for i, (_, at, n) in enumerate(parts) if at // 512 == k) for k in range(3)]

        @block.sync
        def _(sp):
            sp.dma_start(decay[:], g.const["decay"]).then_inc(d_in, 16)

        @block.gpsimd
        def _(pool):
            with pool.Fori(0, B // 2) as i:
                for s in range(2):
                    pool.wait_ge(recalled, NPC * 2 * i)
                    nc.gpsimd.tensor_copy(vn[:, s, :, :], vn_all[:, 2 * i + s, :, :]).then_inc(vn_ready, 1)

        @block.scalar
        def _(act):
            def load(b, s):
                nc.scalar.copy(x[:, s, :, :], x_all[:, b, :, :]).then_inc(x_ready, 1)

            def store(b, k):
                act.wait_ge(recalled, NPC * b + bank_end[k] + 1)
                n = min(512, SEQ - 512 * k)
                nc.scalar.copy(aT_all[0:D, b, 512 * k:512 * k + n], p_a[:, k, 0:n]).then_inc(copied, 1)

            load(0, 0)
            with act.Fori(0, B // 2 - 1) as i:
                for s in range(2):
                    b = 2 * i + s
                    act.wait_ge(recalled, NPC * b)
                    load(b + 1, 1 - s)
                    for k in range(3):
                        store(b, k)
            act.wait_ge(recalled, NPC * (B - 2))
            load(B - 1, 1)
            for b in (B - 2, B - 1):
                for k in range(3):
                    store(b, k)

        @block.vector
        def _(dve):
            dve.wait_ge(d_in, 16)
            with dve.Fori(0, B) as b:
                for k, (s, at, n) in enumerate(parts):
                    rows = min(P, SEQ - s * P)
                    dve.wait_ge(alike, NPC * b + k + 1)
                    dve.wait_ge(recalled, NPC * b + max(k - R + 1, 0))
                    nc.vector.tensor_tensor(pm[0:rows, k % R, 0:n], p_s[0:rows, k % R, 0:n],
                                            decay[0:rows, at - s * P:at - s * P + n], ALU.mult).then_inc(masked, 1)

        @block.tensor
        def _(pe):
            def score(b, slot, k):
                s, at, n = parts[k]
                rows = min(P, SEQ - s * P)
                pe.wait_ge(masked, NPC * b + max(k - R + 1, 0))
                for f in range(2):
                    last = nc.tensor.matmul(p_s[0:rows, k % R, 0:n], x[:, slot, f, s * P:s * P + rows],
                                            x[:, slot, f, at:at + n], start=(f == 0), stop=(f == 1))
                last.then_inc(alike, 1)

            def weigh(b, slot, k):
                s, at, n = parts[k]
                rows = min(P, SEQ - s * P)
                bank = at // 512
                if k in (0, bank_end[0] + 1, bank_end[1] + 1):
                    pe.wait_ge(copied, 3 * b)
                pe.wait_ge(masked, NPC * b + k + 1)
                nc.tensor.matmul(p_a[:, bank, at % 512:at % 512 + n], vn[0:rows, slot, s, :], pm[0:rows, k % R, 0:n],
                                 start=(s == 0), stop=(k == bank_end[bank]), skip_group_check=True).then_inc(recalled, 1)

            with pe.Fori(0, B // 2) as i:
                for slot in range(2):
                    b = 2 * i + slot
                    pe.wait_ge(x_ready, b + 1)
                    pe.wait_ge(vn_ready, b + 1)
                    score(b, slot, 0)
                    for k in range(NPC):
                        if k + 1 < NPC:
                            score(b, slot, k + 1)
                        weigh(b, slot, k)


def answer_block(g, x_all, aT_all):
    nc, hid, arg = g.nc, g.hid, g.arg
    ln = [[g.sem(f"l_{n}{k}") for n in ("stats", "moments", "rstd", "alone")] for k in range(2)]
    (w_in, w_turned, w_ready, set_up, aT_ready, a_turned, normed, la_turned, laT_ready, cored, gated, answered, normed2, added, pe_alone) = (
        g.sem("l_" + n) for n in ("w_in", "w_turned", "w_ready", "set_up", "aT_ready", "a_turned", "normed", "la_turned",
                                  "laT_ready", "cored", "gated", "answered", "normed2", "added", "pe_alone"))
    with ExitStack() as c:
        sb = lambda n, s, d=F32: c.enter_context(nc.sbuf_tensor("l_" + n, s, d))
        ps = lambda n, s: c.enter_context(nc.psum_tensor("l_" + n, s, F32))
        st, mv, la = sb("st", [P, NT, 6]), sb("mv", [P, NT, 4]), sb("la", [P, NT, D])
        st2, mv2, vs = sb("st2", [P, NT, 6]), sb("mv2", [P, NT, 4]), sb("vs", [P, NT, D])
        aT, laT, yT = sb("aT", [D, NT * P]), sb("laT", [P, NT * P]), sb("yT", [P, 2, NT * P])
        dy, dyT, e_raw, eT = sb("dy", [P, 2, D]), sb("dyT", [P, 2, P]), sb("e_raw", [D, NN]), sb("eT", [P, 2, D])
        p_a = ps("p_a", [P, 2, FULL, D])
        p_la = ps("p_la", [P, 1, 512])
        p_y = ps("p_y", [P, 3, 512])
        p_v = ps("p_v", [P, 2, FULL, D])
        block = c.enter_context(nc.Block())
        a_of = lambda t: p_a[:, t // FULL, t % FULL, :]
        v_of = lambda t: p_v[:, t // FULL, t % FULL, :]

        @block.sync
        def _(sp):
            sp.dma_start(dy[:], arg["L1_attn_Dy"].rearrange("(a n) d -> n a d", a=2)).then_inc(w_in, 16)
            sp.dma_start(e_raw[:], arg["L1_attn_E"]).then_inc(w_in, 16)

        @block.gpsimd
        def _(pool):
            for n, v in enumerate((laT[D:P, :], dyT[D:P, :, :], aT[:, SEQ:NT * P], yT[:, :, SEQ:NT * P])):
                if n:
                    pool.wait_ge(set_up, n)
                nc.gpsimd.memset(v, 0.0).then_inc(set_up, 1)
            layernorm_pool(g, pool, 0, mv, ln[0])
            with pool.Fori(0, B - 1) as b:
                layernorm_pool(g, pool, b + 1, mv, ln[0])
                layernorm_pool(g, pool, b, mv2, ln[1])
            layernorm_pool(g, pool, B - 1, mv2, ln[1])

        @block.tensor
        def _(pe):
            pe.wait_ge(w_in, 32)
            pe.wait_ge(set_up, 4)
            for a in range(2):
                nc.tensor.transpose(p_y[0:D, a, 0:P], dy[:, a, :], g.eye[:])
                last = nc.tensor.transpose(p_y[:, 2, a * D:a * D + D], e_raw[:, a * P:a * P + P], g.eye[0:D, 0:D])
            last.then_inc(w_turned, 1)
            pe.wait_ge(w_ready, 2)

            def turn_sums(b):
                pe.wait_ge(aT_ready, b + 1)
                wait_alone(pe, normed, NT * b, pe_alone)
                for t in range(NT):
                    last = nc.tensor.transpose(a_of(t), aT[:, t * P:t * P + P], g.eye[0:D, 0:D])
                last.then_inc(a_turned, 1)

            def answer(b, more):
                wait_alone(pe, normed, NT * b + NT, pe_alone)
                for a in range(3):
                    wait_alone(pe, laT_ready, 3 * b + a, pe_alone)
                    for t in range(3 * a, 3 * a + 3):
                        last = nc.tensor.transpose(p_la[0:D, 0, t % 3 * P:t % 3 * P + P], la[:, t, :], g.eye[:])
                    last.then_inc(la_turned, 1)
                pe.wait_ge(laT_ready, 3 * b + 3)
                for k in range(2 * NC):
                    f, a = divmod(k, NC)
                    pe.wait_ge(gated, 2 * NC * b + max(k - 2, 0))
                    nc.tensor.matmul(p_y[:, k % 3, 0:CH], dyT[:, f, :], laT[:, a * CH:a * CH + CH], start=True, stop=True)\
                        .then_inc(cored, 1)
                if more:
                    turn_sums(b + 1)
                pe.wait_ge(gated, 2 * NC * b + 2 * NC)
                wait_alone(pe, normed2, NT * b, pe_alone)
                for t in range(NT):
                    for f in range(2):
                        last = nc.tensor.matmul(v_of(t), yT[:, f, t * P:t * P + P], eT[:, f, :], start=(f == 0), stop=(f == 1))
                last.then_inc(answered, 1)

            turn_sums(0)
            with pe.Fori(0, B - 1) as b:
                answer(b, True)
            answer(B - 1, False)

        @block.scalar
        def _(act):
            act.wait_ge(w_turned, 1)
            nc.scalar.copy(eT[:, :, :], p_y[:, 2, 0:2 * D].rearrange("p (a d) -> p a d", a=2)).then_inc(w_ready, 1)
            act.wait_ge(set_up, 4)
            nc.scalar.copy(aT[:, 0:SEQ], aT_all[0:D, 0, :]).then_inc(aT_ready, 1)

            def features_down(b, more):
                if more:
                    act.wait_ge(a_turned, b + 1)
                    nc.scalar.copy(aT[:, 0:SEQ], aT_all[0:D, b + 1, :]).then_inc(aT_ready, 1)
                for a in range(3):
                    act.wait_ge(la_turned, 3 * b + a + 1)
                    act.wait_ge(cored, 2 * NC * b)
                    nc.scalar.copy(laT[0:D, 3 * a * P:3 * a * P + 3 * P], p_la[0:D, 0, 0:3 * P]).then_inc(laT_ready, 1)

            with act.Fori(0, B - 1) as b:
                features_down(b, True)
            features_down(B - 1, False)

        @block.vector
        def _(dve):
            dve.wait_ge(w_turned, 1)
            nc.vector.tensor_copy(dyT[0:D, :, :], p_y[0:D, 0:2, 0:P]).then_inc(w_ready, 1)

            def first_norm(b):
                dve.wait_ge(a_turned, b + 1)
                layernorm_stats(nc, dve, b, a_of, st, mv, ln[0])

            def first_apply(b):
                dve.wait_ge(la_turned, 3 * b)
                layernorm_apply(nc, dve, b, a_of, lambda t: la[:, t, :], mv, ln[0], normed)

            def gate(b):
                for k in range(2 * NC):
                    f, a = divmod(k, NC)
                    cols = slice(a * CH, a * CH + CH)
                    dve.wait_ge(cored, 2 * NC * b + k + 1)
                    dve.wait_ge(answered, b)
                    nc.vector.scalar_tensor_tensor(yT[:, f, cols], p_y[:, k % 3, 0:CH], 0.0, x_all[:, b, f, cols],
                                                   ALU.max, ALU.mult).then_inc(gated, 1)

            def second_stats(b):
                dve.wait_ge(answered, b + 1)
                layernorm_stats(nc, dve, b, v_of, st2, mv2, ln[1])

            def second_apply(b):
                layernorm_apply(nc, dve, b, v_of, lambda t: vs[:, t, :], mv2, ln[1], normed2)
                dve.wait_ge(normed2, NT * b + NT)
                nc.vector.tensor_tensor(hid[:, b, :, :], hid[:, b, :, :], vs[:, :, :], ALU.add).then_inc(added, 1)
                dve.wait_ge(added, b + 1)

            first_norm(0)
            first_apply(0)
            with dve.Fori(0, B - 1) as b:
                gate(b)
                first_norm(b + 1)
                second_stats(b)
                first_apply(b + 1)
                second_apply(b)
            gate(B - 1)
            second_stats(B - 1)
            second_apply(B - 1)


def memory_stage(g):
    nc = g.nc
    with ExitStack() as c:
        sb = lambda n, s, d=F32: c.enter_context(nc.sbuf_tensor(n, s, d))
        x_all = sb("m_x_all", [P, B, 2, SEQ])
        with ExitStack() as c2:
            vn_all = c2.enter_context(nc.sbuf_tensor("m_vn_all", [P, B, NT, D], F32))
            with ExitStack() as c3:
                level = c3.enter_context(nc.sbuf_tensor("m_level", [B, SEQ], F32))
                rate = c3.enter_context(nc.sbuf_tensor("m_rate", [B, SEQ], F32))
                drive_block(g, x_all, vn_all, level)
                level_block(g, level, rate)
                state_block(g, x_all, rate)
            aT_all = c2.enter_context(nc.sbuf_tensor("m_aT_all", [D, B, SEQ], F32))
            recall_block(g, x_all, vn_all, aT_all)
            answer_block(g, x_all, aT_all)


def experts0_stage(g):
    nc, arg = g.nc, g.arg
    with ExitStack() as c:
        sb = lambda n, s, d=F32: c.enter_context(nc.sbuf_tensor(n, s, d))
        xn_all = sb("d_xn_all", [P, B, NT, D])
        with ExitStack() as c2:
            x12_all, x13_all = (c2.enter_context(nc.sbuf_tensor(n, [P, B, SEQ], BF16)) for n in ("d_x12_all", "d_x13_all"))
            cT_all = c2.enter_context(nc.sbuf_tensor("d_cT_all", [GK, B, SEQ], BF16))
            gate_block(g, "d_", 16, arg["L0_ffn_gate_w"], arg["L0_ffn_gate_b"], xn_all, x12_all, x13_all, cT_all)
            experts_block(g, "e_", 16, 128, arg["L0_ffn_w1"], arg["L0_ffn_b1"], arg["L0_ffn_w2"], arg["L0_ffn_b2"],
                          False, x12_all, x13_all, cT_all, xn_all, False)
        affine_block(g, "f_", xn_all, arg["L0_ffn_gamma"], arg["L0_ffn_beta"])


def experts1_stage(g):
    nc, arg = g.nc, g.arg
    with ExitStack() as c:
        x12_all, x13_all = (c.enter_context(nc.sbuf_tensor(n, [P, B, SEQ], BF16)) for n in ("n_x12_all", "n_x13_all"))
        cT_all = c.enter_context(nc.sbuf_tensor("n_cT_all", [GK, B, SEQ], BF16))
        gate_block(g, "n_", 8, arg["L1_ffn_Wg"].rearrange("e d -> d e"), arg["L1_ffn_bg"], None, x12_all, x13_all, cT_all)
        experts_block(g, "o_", 8, 256, arg["L1_ffn_W1"], arg["L1_ffn_b1"], arg["L1_ffn_W2"], arg["L1_ffn_b2"],
                      True, x12_all, x13_all, cT_all, g.hid, True)


def build(nc, arg, const, out, stages):
    with ExitStack() as ctx:
        g = Program(nc, ctx, arg, const, out)
        for stage in stages:
            stage(g)
            if stage in (attend_stage, experts0_stage):
                g.free_sems()
        g.sem_ctx.close()


STAGES = [tokens_stage, project_stage, attend_stage, join_stage, experts0_stage, memory_stage, experts1_stage]
_INS = ["x", "txt", "L0_tok_W", "L0_attn_w_qkv", "L0_attn_b_qkv", "L0_attn_w_out", "L0_attn_b_out",
        "L0_ffn_gate_w", "L0_ffn_gate_b", "L0_ffn_w1", "L0_ffn_b1", "L0_ffn_w2", "L0_ffn_b2", "L0_ffn_gamma",
        "L0_ffn_beta", "L1_attn_E", "L1_attn_Dx", "L1_attn_Dy", "L1_ffn_Wg", "L1_ffn_bg", "L1_ffn_W1",
        "L1_ffn_b1", "L1_ffn_W2", "L1_ffn_b2"]


def kernel(**inputs):
    import concourse.bacc as _bacc
    from concourse.bass_utils import run_bass_kernel_spmd as _run

    nc = _bacc.Bacc("TRN2", target_bir_lowering=False, num_devices=1)
    arrays, arg, const = {}, {}, {}
    for name in _INS:
        a = np.ascontiguousarray(inputs[name])
        arrays[f"in_{name}"] = a
        arg[name] = nc.dram_tensor(f"in_{name}", a.shape, mybir.dt.from_np(a.dtype), kind="ExternalInput").ap()
    for name, a in shape_constants().items():
        arrays[f"const_{name}"] = a
        const[name] = nc.dram_tensor(f"const_{name}", a.shape, mybir.dt.from_np(a.dtype), kind="ExternalInput").ap()
    out = nc.dram_tensor("out", (B, SEQ, D), F32, kind="ExternalOutput").ap()
    build(nc, arg, const, out, STAGES)
    r = _run(nc, [arrays], core_ids=[0])
    return np.asarray(r.results[0]["out"])
```
